# Optimizing a Trainium2 kernel written in Bass

```python
import numpy as np
import jax
import jax.numpy as jnp

def _softmax(x, axis=-1):
    return jax.nn.softmax(x, axis=axis)

def _gelu(x):
    return jax.nn.gelu(x, approximate=True)

def _silu(x):
    return jax.nn.silu(x)

def _sigmoid(x):
    return jax.nn.sigmoid(x)

def _layernorm(x, axis=-1, eps=1e-05):
    m = jnp.mean(x, axis=axis, keepdims=True)
    v = jnp.var(x, axis=axis, keepdims=True)
    return (x - m) / jnp.sqrt(v + eps)

def _scatter_add(tgt, idx, src, axis=0):
    return tgt.at[idx].add(src)

def _segment_sum(src, seg, n):
    return jax.ops.segment_sum(src, seg, n)
kernel_name = 'mk_vit_tower_d2_tok_img768_r4_7344de'

def setup_inputs(seed: int=0):
    np.random.seed(seed)
    _w = jnp.asarray

    def _rec_inputs():
        import jax
        import jax.numpy as jnp
        _rk = jax.random.key(seed)
        x = 7.57192e-06 + 1.00007 * jax.random.normal(jax.random.fold_in(_rk, 1), (4, 96, 96, 3), jnp.float32)
        return x
    x = _rec_inputs()

    def _L0_tok_setup():
        import jax, jax.numpy as jnp
        import numpy as np
        PATCH_SIZES = (8, 16, 32)
        PROJ_DIM = 192
        C = 3

        def _extract_patches(images, p):
            B, H, W, Cc = images.shape
            nh, nw = (H // p, W // p)
            x = images.reshape(B, nh, p, nw, p, Cc)
            x = x.transpose(0, 1, 3, 2, 4, 5)
            return x.reshape(B, nh * nw, p * p * Cc)
        key = jax.random.key(seed)
        ks = jax.random.split(key, 1 + 2 * len(PATCH_SIZES))
        images = jax.random.normal(ks[0], (64, 224, 224, C), dtype=jnp.float32)
        inp = {'images': images}
        for i, p in enumerate(PATCH_SIZES):
            k_in = p * p * C
            scale = 1.0 / np.sqrt(k_in)
            inp[f'W{i}'] = jax.random.uniform(ks[1 + 2 * i], (k_in, PROJ_DIM), dtype=jnp.float32, minval=-scale, maxval=scale)
            inp[f'b{i}'] = jnp.zeros((PROJ_DIM,), dtype=jnp.float32)
        return inp
    _L0_tok_all = _L0_tok_setup()
    _L0_tok_in = {k: v for k, v in _L0_tok_all.items() if k in ('W0', 'b0', 'W1', 'b1', 'W2', 'b2')}
    del _L0_tok_all

    def _L0_attn_setup():
        import jax, jax.numpy as jnp
        import numpy as np
        EPS_NORM = 1e-12

        def _normalize(re, im, axis=-1):
            n = jnp.sqrt(jnp.sum(re * re + im * im, axis=axis, keepdims=True))
            n = jnp.maximum(n, EPS_NORM)
            return (re / n, im / n)
        B, N, D = (4, 512, 192)
        H, d, S = (8, 32, 64)
        Sr, dr = (32, 32)
        K = 3
        key = jax.random.key(seed)
        ks = jax.random.split(key, 40)
        g = lambda i, shape, s=1.0: jax.random.normal(ks[i], shape, dtype=jnp.float32) * s
        scale = 1.0 / d ** 0.5
        inp = {'h': g(0, (B, N, D)), 'W_real': g(1, (H, D, d), 0.02), 'W_imag': g(2, (H, D, d), 0.02), 'pw1': g(3, (H, 16, D), D ** (-0.5)), 'pb1': jnp.zeros((H, 16), jnp.float32), 'pw2': g(4, (H, 16), 0.25), 'pb2': jnp.zeros((H,), jnp.float32), 'm_real': g(5, (H, S, d), scale), 'm_imag': g(6, (H, S, d), scale), 'values': g(7, (H, S, D), 0.02), 'gate_w': g(8, (H, H * D), (H * D) ** (-0.5)), 'gate_b': jnp.zeros((H,), jnp.float32), 'out_w': g(9, (D, D), D ** (-0.5)), 'out_b': jnp.zeros((D,), jnp.float32), 'beta': jnp.float32(0.3), 'P_real': g(10, (Sr, dr), scale), 'P_imag': g(11, (Sr, dr), scale), 'C_real': g(12, (Sr, dr), scale), 'C_imag': g(13, (Sr, dr), scale), 'enc_r_w': g(14, (dr, D), D ** (-0.5)), 'enc_i_w': g(15, (dr, D), D ** (-0.5)), 'r_out_w': g(16, (D, 2 * Sr), 0.05), 'r_out_b': jnp.zeros((D,), jnp.float32), 'ew1': g(17, (K, D, D), D ** (-0.5)), 'eb1': jnp.zeros((K, D), jnp.float32), 'eg': jnp.ones((K, D), jnp.float32), 'ebt': jnp.zeros((K, D), jnp.float32), 'ew2': g(18, (K, D, D), D ** (-0.5)), 'eb2': jnp.zeros((K, D), jnp.float32), 'rw1': g(19, (16, D), D ** (-0.5)), 'rb1': jnp.zeros((16,), jnp.float32), 'rw2': g(20, (K, 16), 0.25), 'rb2': jnp.zeros((K,), jnp.float32)}
        return inp
    _L0_attn_all = _L0_attn_setup()
    _L0_attn_in = {k: v for k, v in _L0_attn_all.items() if k in ('W_real', 'W_imag', 'pw1', 'pb1', 'pw2', 'pb2', 'm_real', 'm_imag', 'values', 'gate_w', 'gate_b', 'out_w', 'out_b', 'beta', 'P_real', 'P_imag', 'C_real', 'C_imag', 'enc_r_w', 'enc_i_w', 'r_out_w', 'r_out_b', 'ew1', 'eb1', 'eg', 'ebt', 'ew2', 'eb2', 'rw1', 'rb1', 'rw2', 'rb2')}
    del _L0_attn_all

    def _L0_ffn_setup():
        import jax, jax.numpy as jnp
        import numpy as np
        H, I, E, K = (192, 384, 7, 2)
        B, S = (8, 512)

        def _mlp(x, wg, wu, wd):
            return jax.nn.silu(x @ wg) * (x @ wu) @ wd
        key = jax.random.key(seed)
        ks = jax.random.split(key, 12)
        s = 0.02
        return {'x': jax.random.normal(ks[0], (B, S, H), dtype=jnp.float32), 'router_w': jax.random.normal(ks[1], (H, E), dtype=jnp.float32) * s, 'routing_bias': jax.random.normal(ks[2], (E,), dtype=jnp.float32), 'sw_gate': jax.random.normal(ks[3], (H, I), dtype=jnp.float32) * s, 'sw_up': jax.random.normal(ks[4], (H, I), dtype=jnp.float32) * s, 'sw_down': jax.random.normal(ks[5], (I, H), dtype=jnp.float32) * s, 'rw_gate': jax.random.normal(ks[6], (E, H, I), dtype=jnp.float32) * s, 'rw_up': jax.random.normal(ks[7], (E, H, I), dtype=jnp.float32) * s, 'rw_down': jax.random.normal(ks[8], (E, I, H), dtype=jnp.float32) * s}
    _L0_ffn_all = _L0_ffn_setup()
    _L0_ffn_in = {k: v for k, v in _L0_ffn_all.items() if k in ('router_w', 'routing_bias', 'sw_gate', 'sw_up', 'sw_down', 'rw_gate', 'rw_up', 'rw_down')}
    del _L0_ffn_all

    def _L1_attn_setup():
        import jax, jax.numpy as jnp
        import numpy as np
        import math
        H = 12
        LOGIT_SCALE_MAX = math.log(1.0 / 0.01)

        def _normalize(t, eps=1e-12):
            n = jnp.linalg.norm(t, axis=-1, keepdims=True)
            return t / jnp.maximum(n, eps)
        key = jax.random.key(seed)
        ks = jax.random.split(key, 4)
        L, N, C = (256, 8, 192)
        scale = (C // H) ** (-0.5)
        return {'x': jax.random.normal(ks[0], (L, N, C), jnp.float32), 'in_proj_weight': jax.random.normal(ks[1], (3 * C, C), jnp.float32) * scale, 'in_proj_bias': jnp.zeros((3 * C,), jnp.float32), 'logit_scale': jnp.full((H, 1, 1), jnp.log(10.0), jnp.float32), 'head_scale': jnp.ones((H, 1, 1), jnp.float32), 'out_w': jax.random.normal(ks[2], (C, C), jnp.float32) * scale, 'out_b': jnp.zeros((C,), jnp.float32)}
    _L1_attn_all = _L1_attn_setup()
    _L1_attn_in = {k: v for k, v in _L1_attn_all.items() if k in ('in_proj_weight', 'in_proj_bias', 'logit_scale', 'head_scale', 'out_w', 'out_b')}
    del _L1_attn_all

    def _L1_ffn_setup():
        import jax, jax.numpy as jnp
        import numpy as np
        import math
        N_HEAD = 12
        N_EXP = 8
        TOP_K = 2
        EVAL_CAPACITY = 1.0
        MIN_CAPACITY = 4
        EPS = 1e-05

        def layer_norm(x, w):
            mu = jnp.mean(x, axis=-1, keepdims=True)
            var = jnp.var(x, axis=-1, keepdims=True)
            return (x - mu) / jnp.sqrt(var + EPS) * w

        def attention(x, c_attn_w, c_proj_w):
            B, T, C = x.shape
            H, D = (N_HEAD, C // N_HEAD)
            qkv = x @ c_attn_w.T
            q, k, v = jnp.split(qkv, 3, axis=-1)
            q = q.reshape(B, T, H, D).transpose(0, 2, 1, 3)
            k = k.reshape(B, T, H, D).transpose(0, 2, 1, 3)
            v = v.reshape(B, T, H, D).transpose(0, 2, 1, 3)
            scores = jnp.einsum('bhqd,bhkd->bhqk', q, k) * (1.0 / math.sqrt(D))
            causal = jnp.tril(jnp.ones((T, T), dtype=bool))
            scores = jnp.where(causal, scores, -jnp.inf)
            att = jax.nn.softmax(scores, axis=-1)
            y = jnp.einsum('bhqk,bhkd->bhqd', att, v)
            y = y.transpose(0, 2, 1, 3).reshape(B, T, C)
            return y @ c_proj_w.T

        def get_capacity(num_tokens):
            cap = int(math.floor(TOP_K * EVAL_CAPACITY * num_tokens / N_EXP))
            cap += cap % 2
            return max(cap, MIN_CAPACITY)

        def moe(x_flat, w_g, c_fc, c_proj_e):
            n_tok, C = x_flat.shape
            logits = x_flat @ w_g.T
            top_vals, top_idx = jax.lax.top_k(logits, TOP_K)
            rows = jnp.arange(n_tok)[:, None]
            masked = jnp.full_like(logits, -jnp.inf).at[rows, top_idx].set(top_vals)
            probs = jax.nn.softmax(masked, axis=-1)
            cap = get_capacity(n_tok)
            flat_e = top_idx.reshape(-1)
            onehot = jax.nn.one_hot(flat_e, N_EXP, dtype=jnp.int32)
            pos = jnp.cumsum(onehot, axis=0) - onehot
            slot = jnp.take_along_axis(pos, flat_e[:, None], axis=1)[:, 0]
            valid = slot < cap
            tok = jnp.repeat(jnp.arange(n_tok), TOP_K)
            slot_c = jnp.where(valid, slot, cap)
            sec = jnp.zeros((n_tok, N_EXP, cap + 1), dtype=x_flat.dtype)
            sec = sec.at[tok, flat_e, slot_c].set(1.0)[:, :, :cap]
            w_tok = probs[tok, flat_e]
            cb = jnp.zeros((n_tok, N_EXP, cap + 1), dtype=x_flat.dtype)
            cb = cb.at[tok, flat_e, slot_c].set(w_tok)[:, :, :cap]
            dispatched = jnp.einsum('tec,td->ecd', sec, x_flat)
            h = jax.nn.gelu(jnp.einsum('ecd,edh->ech', dispatched, c_fc), approximate=False)
            out = jnp.einsum('ech,ehd->ecd', h, c_proj_e)
            return jnp.einsum('tec,ecd->td', cb, out)
        key = jax.random.key(seed)
        ks = jax.random.split(key, 7)
        B, T, C = (2, 512, 192)
        std = 0.02
        return {'x': jax.random.normal(ks[0], (B, T, C), dtype=jnp.float32), 'ln1_w': jnp.ones((C,), dtype=jnp.float32), 'ln2_w': jnp.ones((C,), dtype=jnp.float32), 'c_attn_w': jax.random.normal(ks[1], (3 * C, C), dtype=jnp.float32) * std, 'c_proj_w': jax.random.normal(ks[2], (C, C), dtype=jnp.float32) * std, 'w_g': jax.random.normal(ks[3], (N_EXP, C), dtype=jnp.float32) * std, 'c_fc': jax.random.normal(ks[4], (N_EXP, C, 4 * C), dtype=jnp.float32) * std, 'c_proj_e': jax.random.normal(ks[5], (N_EXP, 4 * C, C), dtype=jnp.float32) * std}
    _L1_ffn_all = _L1_ffn_setup()
    _L1_ffn_in = {k: v for k, v in _L1_ffn_all.items() if k in ('ln1_w', 'ln2_w', 'c_attn_w', 'c_proj_w', 'w_g', 'c_fc', 'c_proj_e')}
    del _L1_ffn_all
    return {'x': x, 'L0_tok_W0': _L0_tok_in['W0'], 'L0_tok_b0': _L0_tok_in['b0'], 'L0_tok_W1': _L0_tok_in['W1'], 'L0_tok_b1': _L0_tok_in['b1'], 'L0_tok_W2': _L0_tok_in['W2'], 'L0_tok_b2': _L0_tok_in['b2'], 'L0_attn_W_real': _L0_attn_in['W_real'], 'L0_attn_W_imag': _L0_attn_in['W_imag'], 'L0_attn_pw1': _L0_attn_in['pw1'], 'L0_attn_pb1': _L0_attn_in['pb1'], 'L0_attn_pw2': _L0_attn_in['pw2'], 'L0_attn_pb2': _L0_attn_in['pb2'], 'L0_attn_m_real': _L0_attn_in['m_real'], 'L0_attn_m_imag': _L0_attn_in['m_imag'], 'L0_attn_values': _L0_attn_in['values'], 'L0_attn_gate_w': _L0_attn_in['gate_w'], 'L0_attn_gate_b': _L0_attn_in['gate_b'], 'L0_attn_out_w': _L0_attn_in['out_w'], 'L0_attn_out_b': _L0_attn_in['out_b'], 'L0_attn_beta': _L0_attn_in['beta'], 'L0_attn_P_real': _L0_attn_in['P_real'], 'L0_attn_P_imag': _L0_attn_in['P_imag'], 'L0_attn_C_real': _L0_attn_in['C_real'], 'L0_attn_C_imag': _L0_attn_in['C_imag'], 'L0_attn_enc_r_w': _L0_attn_in['enc_r_w'], 'L0_attn_enc_i_w': _L0_attn_in['enc_i_w'], 'L0_attn_r_out_w': _L0_attn_in['r_out_w'], 'L0_attn_r_out_b': _L0_attn_in['r_out_b'], 'L0_attn_ew1': _L0_attn_in['ew1'], 'L0_attn_eb1': _L0_attn_in['eb1'], 'L0_attn_eg': _L0_attn_in['eg'], 'L0_attn_ebt': _L0_attn_in['ebt'], 'L0_attn_ew2': _L0_attn_in['ew2'], 'L0_attn_eb2': _L0_attn_in['eb2'], 'L0_attn_rw1': _L0_attn_in['rw1'], 'L0_attn_rb1': _L0_attn_in['rb1'], 'L0_attn_rw2': _L0_attn_in['rw2'], 'L0_attn_rb2': _L0_attn_in['rb2'], 'L0_ffn_router_w': _L0_ffn_in['router_w'], 'L0_ffn_routing_bias': _L0_ffn_in['routing_bias'], 'L0_ffn_sw_gate': _L0_ffn_in['sw_gate'], 'L0_ffn_sw_up': _L0_ffn_in['sw_up'], 'L0_ffn_sw_down': _L0_ffn_in['sw_down'], 'L0_ffn_rw_gate': _L0_ffn_in['rw_gate'], 'L0_ffn_rw_up': _L0_ffn_in['rw_up'], 'L0_ffn_rw_down': _L0_ffn_in['rw_down'], 'L1_attn_in_proj_weight': _L1_attn_in['in_proj_weight'], 'L1_attn_in_proj_bias': _L1_attn_in['in_proj_bias'], 'L1_attn_logit_scale': _L1_attn_in['logit_scale'], 'L1_attn_head_scale': _L1_attn_in['head_scale'], 'L1_attn_out_w': _L1_attn_in['out_w'], 'L1_attn_out_b': _L1_attn_in['out_b'], 'L1_ffn_ln1_w': _L1_ffn_in['ln1_w'], 'L1_ffn_ln2_w': _L1_ffn_in['ln2_w'], 'L1_ffn_c_attn_w': _L1_ffn_in['c_attn_w'], 'L1_ffn_c_proj_w': _L1_ffn_in['c_proj_w'], 'L1_ffn_w_g': _L1_ffn_in['w_g'], 'L1_ffn_c_fc': _L1_ffn_in['c_fc'], 'L1_ffn_c_proj_e': _L1_ffn_in['c_proj_e']}

def reference(x, L0_tok_W0, L0_tok_b0, L0_tok_W1, L0_tok_b1, L0_tok_W2, L0_tok_b2, L0_attn_W_real, L0_attn_W_imag, L0_attn_pw1, L0_attn_pb1, L0_attn_pw2, L0_attn_pb2, L0_attn_m_real, L0_attn_m_imag, L0_attn_values, L0_attn_gate_w, L0_attn_gate_b, L0_attn_out_w, L0_attn_out_b, L0_attn_beta, L0_attn_P_real, L0_attn_P_imag, L0_attn_C_real, L0_attn_C_imag, L0_attn_enc_r_w, L0_attn_enc_i_w, L0_attn_r_out_w, L0_attn_r_out_b, L0_attn_ew1, L0_attn_eb1, L0_attn_eg, L0_attn_ebt, L0_attn_ew2, L0_attn_eb2, L0_attn_rw1, L0_attn_rb1, L0_attn_rw2, L0_attn_rb2, L0_ffn_router_w, L0_ffn_routing_bias, L0_ffn_sw_gate, L0_ffn_sw_up, L0_ffn_sw_down, L0_ffn_rw_gate, L0_ffn_rw_up, L0_ffn_rw_down, L1_attn_in_proj_weight, L1_attn_in_proj_bias, L1_attn_logit_scale, L1_attn_head_scale, L1_attn_out_w, L1_attn_out_b, L1_ffn_ln1_w, L1_ffn_ln2_w, L1_ffn_c_attn_w, L1_ffn_c_proj_w, L1_ffn_w_g, L1_ffn_c_fc, L1_ffn_c_proj_e):
    import jax
    import jax.numpy as jnp

    def _L0_tok_ref(images, W0, b0, W1, b1, W2, b2):
        import jax, jax.numpy as jnp
        import numpy as np
        PATCH_SIZES = (8, 16, 32)
        PROJ_DIM = 192
        C = 3

        def _extract_patches(images, p):
            B, H, W, Cc = images.shape
            nh, nw = (H // p, W // p)
            x = images.reshape(B, nh, p, nw, p, Cc)
            x = x.transpose(0, 1, 3, 2, 4, 5)
            return x.reshape(B, nh * nw, p * p * Cc)
        Ws = (W0, W1, W2)
        bs = (b0, b1, b2)
        outs = []
        for p, W, b in zip(PATCH_SIZES, Ws, bs):
            patches = _extract_patches(images, p)
            outs.append(jnp.einsum('bnk,kd->bnd', patches, W) + b)
        return jnp.concatenate(outs, axis=1)

    def _L0_attn_ref(h, W_real, W_imag, pw1, pb1, pw2, pb2, m_real, m_imag, values, gate_w, gate_b, out_w, out_b, beta, P_real, P_imag, C_real, C_imag, enc_r_w, enc_i_w, r_out_w, r_out_b, ew1, eb1, eg, ebt, ew2, eb2, rw1, rb1, rw2, rb2):
        import jax, jax.numpy as jnp
        import numpy as np
        EPS_NORM = 1e-12

        def _normalize(re, im, axis=-1):
            n = jnp.sqrt(jnp.sum(re * re + im * im, axis=axis, keepdims=True))
            n = jnp.maximum(n, EPS_NORM)
            return (re / n, im / n)
        B, N, D = h.shape
        H, _, d = W_real.shape
        pr = jnp.einsum('bnD,hDd->bhnd', h, W_real)
        pi = jnp.einsum('bnD,hDd->bhnd', h, W_imag)
        pr, pi = _normalize(pr, pi)
        z = jax.nn.silu(jnp.einsum('bnD,hkD->bhnk', h, pw1) + pb1[None, :, None, :])
        p = jax.nn.sigmoid(jnp.einsum('bhnk,hk->bhn', z, pw2) + pb2[None, :, None]) * 0.95
        mr, mi = _normalize(m_real, m_imag)
        ov_re = jnp.einsum('bhnd,hsd->bhns', pr, mr) + jnp.einsum('bhnd,hsd->bhns', pi, mi)
        ov_im = jnp.einsum('bhnd,hsd->bhns', pi, mr) - jnp.einsum('bhnd,hsd->bhns', pr, mi)
        raw = (1.0 - p)[..., None] * (ov_re * ov_re + ov_im * ov_im) + p[..., None] / d
        attn = raw / (raw.sum(axis=-1, keepdims=True) + 1e-08)
        out_h = jnp.einsum('bhns,hsD->bhnD', attn, values)
        concat = jnp.transpose(out_h, (0, 2, 1, 3)).reshape(B, N, H * D)
        gates = jax.nn.softmax(concat @ gate_w.T + gate_b, axis=-1)
        combined = jnp.einsum('bhnD,bnh->bnD', out_h, gates)
        attn_out = combined @ out_w.T + out_b
        p_tok = p.mean(axis=1)
        h1 = h + attn_out
        coupling = jax.nn.softmax(jnp.einsum('bnD,bmD->bnm', h1, h1) * D ** (-0.5), axis=-1)
        neigh = jnp.einsum('bnm,bm->bn', coupling, 1.0 - p_tok)
        p_new = jnp.clip(p_tok * (1.0 - jax.nn.sigmoid(beta) * neigh), 0.0, 0.95)
        qr, qi = _normalize(h1 @ enc_r_w.T, h1 @ enc_i_w.T)
        Pr, Pi = _normalize(P_real, P_imag)
        Cr, Ci = _normalize(C_real, C_imag)
        a_re = qr @ Pr.T + qi @ Pi.T
        a_im = qr @ Pi.T - qi @ Pr.T
        b_re = qr @ Cr.T + qi @ Ci.T
        b_im = qr @ Ci.T - qi @ Cr.T
        g_re = (Pr * Cr + Pi * Ci).sum(-1)
        g_im = (Pr * Ci - Pi * Cr).sum(-1)
        t_re = a_re * g_re - a_im * g_im
        t_im = a_re * g_im + a_im * g_re
        R_re = t_re * b_re + t_im * b_im
        R_im = t_im * b_re - t_re * b_im
        feats = jnp.concatenate([R_re, R_im], axis=-1)
        reason = feats @ r_out_w.T + r_out_b
        h2 = h1 + (1.0 - p_new)[..., None] * reason
        x = jnp.einsum('bnD,kED->bnkE', h2, ew1) + eb1
        mu = x.mean(axis=-1, keepdims=True)
        var = ((x - mu) ** 2).mean(axis=-1, keepdims=True)
        x = (x - mu) / jnp.sqrt(var + 1e-05) * eg + ebt
        x = jax.nn.gelu(x, approximate=False)
        y = jnp.einsum('bnkE,kDE->bnkD', x, ew2) + eb2
        rg = jax.nn.softmax(jax.nn.gelu(h2 @ rw1.T + rb1, approximate=False) @ rw2.T + rb2, axis=-1)
        route = jnp.einsum('bnkD,bnk->bnD', y, rg)
        return h2 + route

    def _L0_ffn_ref(x, router_w, routing_bias, sw_gate, sw_up, sw_down, rw_gate, rw_up, rw_down):
        import jax, jax.numpy as jnp
        import numpy as np
        H, I, E, K = (192, 384, 7, 2)
        B, S = (8, 512)

        def _mlp(x, wg, wu, wd):
            return jax.nn.silu(x @ wg) * (x @ wu) @ wd
        b, s, h = x.shape
        xf = x.reshape(-1, h)
        T = xf.shape[0]
        shared = _mlp(xf, sw_gate, sw_up, sw_down)
        logits = xf @ router_w * routing_bias
        probs = jax.nn.sigmoid(logits)
        scores, idx = jax.lax.top_k(probs, K)
        scores = scores / jnp.sum(scores, axis=-1, keepdims=True)
        cw = jnp.zeros((T, E), dtype=xf.dtype)
        cw = cw.at[jnp.arange(T)[:, None], idx].add(scores)
        out = shared
        for e in range(E):
            out = out + cw[:, e:e + 1] * _mlp(xf, rw_gate[e], rw_up[e], rw_down[e])
        return out.reshape(b, s, h)

    def _L1_attn_ref(x, in_proj_weight, in_proj_bias, logit_scale, head_scale, out_w, out_b):
        import jax, jax.numpy as jnp
        import numpy as np
        import math
        H = 12
        LOGIT_SCALE_MAX = math.log(1.0 / 0.01)

        def _normalize(t, eps=1e-12):
            n = jnp.linalg.norm(t, axis=-1, keepdims=True)
            return t / jnp.maximum(n, eps)
        L, N, C = x.shape
        D = C // H
        qkv = x @ in_proj_weight.T + in_proj_bias
        q, k, v = jnp.split(qkv, 3, axis=-1)

        def to_heads(t):
            return t.reshape(L, N, H, D).transpose(1, 2, 0, 3)
        q, k, v = (to_heads(q), to_heads(k), to_heads(v))
        attn = jnp.einsum('nhld,nhmd->nhlm', _normalize(q), _normalize(k))
        ls = jnp.exp(jnp.minimum(logit_scale, LOGIT_SCALE_MAX))
        attn = attn * ls[None]
        attn = jax.nn.softmax(attn, axis=-1)
        o = jnp.einsum('nhlm,nhmd->nhld', attn, v)
        o = o * head_scale[None]
        o = o.transpose(2, 0, 1, 3).reshape(L, N, C)
        return o @ out_w.T + out_b

    def _L1_ffn_ref(x, ln1_w, ln2_w, c_attn_w, c_proj_w, w_g, c_fc, c_proj_e):
        import jax, jax.numpy as jnp
        import numpy as np
        import math
        N_HEAD = 12
        N_EXP = 8
        TOP_K = 2
        EVAL_CAPACITY = 1.0
        MIN_CAPACITY = 4
        EPS = 1e-05

        def layer_norm(x, w):
            mu = jnp.mean(x, axis=-1, keepdims=True)
            var = jnp.var(x, axis=-1, keepdims=True)
            return (x - mu) / jnp.sqrt(var + EPS) * w

        def attention(x, c_attn_w, c_proj_w):
            B, T, C = x.shape
            H, D = (N_HEAD, C // N_HEAD)
            qkv = x @ c_attn_w.T
            q, k, v = jnp.split(qkv, 3, axis=-1)
            q = q.reshape(B, T, H, D).transpose(0, 2, 1, 3)
            k = k.reshape(B, T, H, D).transpose(0, 2, 1, 3)
            v = v.reshape(B, T, H, D).transpose(0, 2, 1, 3)
            scores = jnp.einsum('bhqd,bhkd->bhqk', q, k) * (1.0 / math.sqrt(D))
            causal = jnp.tril(jnp.ones((T, T), dtype=bool))
            scores = jnp.where(causal, scores, -jnp.inf)
            att = jax.nn.softmax(scores, axis=-1)
            y = jnp.einsum('bhqk,bhkd->bhqd', att, v)
            y = y.transpose(0, 2, 1, 3).reshape(B, T, C)
            return y @ c_proj_w.T

        def get_capacity(num_tokens):
            cap = int(math.floor(TOP_K * EVAL_CAPACITY * num_tokens / N_EXP))
            cap += cap % 2
            return max(cap, MIN_CAPACITY)

        def moe(x_flat, w_g, c_fc, c_proj_e):
            n_tok, C = x_flat.shape
            logits = x_flat @ w_g.T
            top_vals, top_idx = jax.lax.top_k(logits, TOP_K)
            rows = jnp.arange(n_tok)[:, None]
            masked = jnp.full_like(logits, -jnp.inf).at[rows, top_idx].set(top_vals)
            probs = jax.nn.softmax(masked, axis=-1)
            cap = get_capacity(n_tok)
            flat_e = top_idx.reshape(-1)
            onehot = jax.nn.one_hot(flat_e, N_EXP, dtype=jnp.int32)
            pos = jnp.cumsum(onehot, axis=0) - onehot
            slot = jnp.take_along_axis(pos, flat_e[:, None], axis=1)[:, 0]
            valid = slot < cap
            tok = jnp.repeat(jnp.arange(n_tok), TOP_K)
            slot_c = jnp.where(valid, slot, cap)
            sec = jnp.zeros((n_tok, N_EXP, cap + 1), dtype=x_flat.dtype)
            sec = sec.at[tok, flat_e, slot_c].set(1.0)[:, :, :cap]
            w_tok = probs[tok, flat_e]
            cb = jnp.zeros((n_tok, N_EXP, cap + 1), dtype=x_flat.dtype)
            cb = cb.at[tok, flat_e, slot_c].set(w_tok)[:, :, :cap]
            dispatched = jnp.einsum('tec,td->ecd', sec, x_flat)
            h = jax.nn.gelu(jnp.einsum('ecd,edh->ech', dispatched, c_fc), approximate=False)
            out = jnp.einsum('ech,ehd->ecd', h, c_proj_e)
            return jnp.einsum('tec,ecd->td', cb, out)
        x = x + attention(layer_norm(x, ln1_w), c_attn_w, c_proj_w)
        B, T, C = x.shape
        x_ln = layer_norm(x, ln2_w)
        moe_out = moe(x_ln.reshape(B * T, C), w_g, c_fc, c_proj_e)
        return x + moe_out.reshape(B, T, C)
    h = _L0_tok_ref(x, L0_tok_W0, L0_tok_b0, L0_tok_W1, L0_tok_b1, L0_tok_W2, L0_tok_b2)
    h = h + _L0_attn_ref(_layernorm(h, axis=-1), L0_attn_W_real, L0_attn_W_imag, L0_attn_pw1, L0_attn_pb1, L0_attn_pw2, L0_attn_pb2, L0_attn_m_real, L0_attn_m_imag, L0_attn_values, L0_attn_gate_w, L0_attn_gate_b, L0_attn_out_w, L0_attn_out_b, L0_attn_beta, L0_attn_P_real, L0_attn_P_imag, L0_attn_C_real, L0_attn_C_imag, L0_attn_enc_r_w, L0_attn_enc_i_w, L0_attn_r_out_w, L0_attn_r_out_b, L0_attn_ew1, L0_attn_eb1, L0_attn_eg, L0_attn_ebt, L0_attn_ew2, L0_attn_eb2, L0_attn_rw1, L0_attn_rb1, L0_attn_rw2, L0_attn_rb2)
    h = h + _L0_ffn_ref(_layernorm(h, axis=-1), L0_ffn_router_w, L0_ffn_routing_bias, L0_ffn_sw_gate, L0_ffn_sw_up, L0_ffn_sw_down, L0_ffn_rw_gate, L0_ffn_rw_up, L0_ffn_rw_down)
    h = h + _L1_attn_ref(_layernorm(h, axis=-1), L1_attn_in_proj_weight, L1_attn_in_proj_bias, L1_attn_logit_scale, L1_attn_head_scale, L1_attn_out_w, L1_attn_out_b)
    h = h + _L1_ffn_ref(_layernorm(h, axis=-1), L1_ffn_ln1_w, L1_ffn_ln2_w, L1_ffn_c_attn_w, L1_ffn_c_proj_w, L1_ffn_w_g, L1_ffn_c_fc, L1_ffn_c_proj_e)
    return h

_drawn_inputs = setup_inputs


def setup_inputs(seed=0):
    import zlib

    import numpy as np

    out = dict(_drawn_inputs(seed))
    spreads = {'L0_tok_b0': (0.0, 0.1),
     'L0_tok_b1': (0.0, 0.1),
     'L0_tok_b2': (0.0, 0.1),
     'L0_attn_pb1': (0.0, 0.8),
     'L0_attn_pb2': (0.0, 0.8),
     'L0_attn_gate_b': (0.0, 0.8),
     'L0_attn_out_b': (0.0, 0.1),
     'L0_attn_r_out_b': (0.0, 0.1),
     'L0_attn_eb1': (0.0, 0.1),
     'L0_attn_eg': (1.0, 0.2),
     'L0_attn_ebt': (0.0, 0.1),
     'L0_attn_eb2': (0.0, 0.1),
     'L0_attn_rb1': (0.0, 0.444),
     'L0_attn_rb2': (0.0, 0.359),
     'L1_attn_in_proj_bias': (0.0, 0.1),
     'L1_attn_logit_scale': (2.3025851249694824, 0.2),
     'L1_attn_head_scale': (1.0, 0.2),
     'L1_attn_out_b': (0.0, 0.8),
     'L1_ffn_ln1_w': (1.0, 0.6),
     'L1_ffn_ln2_w': (1.0, 0.6)}
    factors = {'L0_attn_W_real': 8.0,
     'L0_attn_W_imag': 8.0,
     'L0_attn_pw1': 8.0,
     'L0_attn_pw2': 8.0,
     'L0_attn_m_real': 8.0,
     'L0_attn_m_imag': 8.0,
     'L0_attn_values': 8.0,
     'L0_attn_gate_w': 8.0,
     'L0_attn_out_w': 8.0,
     'L0_attn_P_real': 8.0,
     'L0_attn_P_imag': 8.0,
     'L0_attn_C_real': 8.0,
     'L0_attn_C_imag': 8.0,
     'L0_attn_enc_r_w': 8.0,
     'L0_attn_enc_i_w': 8.0,
     'L0_attn_r_out_w': 8.0,
     'L0_ffn_router_w': 6.302,
     'L0_ffn_routing_bias': 5.759,
     'L0_ffn_sw_gate': 3.564,
     'L0_ffn_sw_up': 3.498,
     'L0_ffn_sw_down': 3.551,
     'L0_ffn_rw_gate': 4.9,
     'L0_ffn_rw_up': 4.885,
     'L0_ffn_rw_down': 4.983,
     'L1_ffn_c_attn_w': 8.0,
     'L1_ffn_c_proj_w': 8.0,
     'L1_ffn_w_g': 8.0,
     'L1_ffn_c_fc': 8.0,
     'L1_ffn_c_proj_e': 8.0}
    for name, (base, spread) in spreads.items():
        noise = np.random.default_rng([zlib.crc32(name.encode()), seed]).standard_normal(out[name].shape)
        drawn = base * np.exp(spread * noise) if base else spread * noise
        out[name] = jnp.asarray(drawn.astype(out[name].dtype))
    for name, factor in factors.items():
        out[name] = (out[name] * factor).astype(out[name].dtype)
    return out
```

```python
from contextlib import ExitStack

import concourse.bass as bass
from concourse import mybir

F32 = mybir.dt.float32
BF16 = mybir.dt.bfloat16
ACT = mybir.ActivationFunctionType
ALU = mybir.AluOpType
X = mybir.AxisListType.X

B, IMG, C, D = 4, 96, 3, 192
SIDES = (8, 16, 32)
PATCHES = [(IMG // s) ** 2 for s in SIDES]
N = sum(PATCHES)
T = B * N
HALF = T // 2
TT = 126
NT = T // TT
DH = D // 2
S0H, S0D, S0S = 8, 32, 64
K0 = 3
FE, FI = 8, 384
AH, AD = 12, 16
ME, MI = 8, 768
CAP = 190
CT = CAP // 2
QT = 95
BANKS = 8
BANK = 512
EPS = 1e-5
NEG = -1.0e30


class Ring:

    def __init__(self, bank_full, emptied):
        self.bank_full, self.emptied = bank_full, emptied
        self.n = 0
        self.count = {k: 0 for k in emptied}
        self.at = {}
        self.order = []
        self.loops, self.bodies, self.before = {}, {}, {}

    def add(self, fills, times=1):
        first, base = self.n, dict(self.count)
        for key, eng in fills:
            self.count[eng] += 1
            self.at[key] = [self.n, eng, self.count[eng], len(fills) if times > 1 else 0, 0]
            self.order.append(key)
            self.n += 1
        if times > 1:
            assert len(fills) % BANKS == 0
            for z, (key, eng) in enumerate(fills):
                self.loops[key], self.bodies[key], self.before[key] = z, [f[0] for f in fills], base
                self.at[key][4] = self.count[eng] - base[eng]
            for eng in self.count:
                self.count[eng] += (times - 1) * (self.count[eng] - base[eng])
            self.n = first + times * len(fills)
            self.order += [fills[j][0] for j in range(len(fills))] * (times - 1)

    def bank(self, key):
        return self.at[key][0] % BANKS

    def full(self, key, i=0):
        pos, _, _, stride, _ = self.at[key]
        return self.bank_full, i * stride + (pos + 1) if stride else pos + 1

    def done(self, key, i=0, back=0):
        _, eng, nth, length, stride = self.at[key]
        nth -= back * stride
        assert nth > 0
        return self.emptied[eng], i * stride + nth if length else nth

    def free(self, key, i=0):
        pos, _, _, length, _ = self.at[key]
        if pos < BANKS:
            return None
        if length:
            offset = self.loops[key]
            body = self.bodies[key]
            if offset >= BANKS:
                return self.done(body[offset - BANKS], i)
            return self.done(body[offset - BANKS], i, back=1)
        before = self.order[pos - BANKS]
        own, inside = self.at[before][0], self.at[before][3]
        return self.done(before, (pos - BANKS - own) // inside if inside else 0)

    def all_done(self, key):
        return [(self.emptied[e], n) for e, n in self.before[key].items() if n]


def vit_tower(nc, a, out):
    with ExitStack() as ctx:
        def sb(name, shape, dt=F32):
            return ctx.enter_context(nc.sbuf_tensor(name, shape, dt))

        def sem(name):
            return ctx.enter_context(nc.semaphore(name))

        psum = [ctx.enter_context(nc.psum_tensor(f"bank{i}", [128, BANK], F32)) for i in range(BANKS)]
        bank_full, emptied_v, emptied_s = sem("bank_full"), sem("emptied_v"), sem("emptied_s")
        ring = Ring(bank_full, {"v": emptied_v, "s": emptied_s})
        v_step = sem("v_step")

        ALL_LOADS = {}

        def loaded(name):
            if name not in ALL_LOADS:
                ALL_LOADS[name] = sem("ld_" + name)
            return ALL_LOADS[name], 16 * LOADS[name]

        ident = sb("ident", [128, 128])
        identb = sb("identb", [128, 128], BF16)
        bones = sb("bones", [128, 128])
        sgn = sb("sgn", [128, 1])
        big4 = sb("big4", [128, 6 * T])
        p8 = big4[0:DH, 0:1152].rearrange("p (k n) -> p k n", k=2)
        w8 = big4[0:DH, 1152:1536].rearrange("p (k n) -> p k n", k=2)
        p16 = big4[:, 1536:2400].rearrange("p (k n) -> p k n", k=6)
        w16 = big4[:, 2400:3552].rearrange("p (k n) -> p k n", k=6)
        gT = big4[0:DH + 1, :].rearrange("p (c t) -> p c t", c=6)
        arena = sb("arena", [128, 2, 2, 1536])
        arena_flat = arena[:, :, :, :].rearrange("p a b n -> p (a b n)")
        w32 = arena_flat[:, 0:24 * D].rearrange("p (k n) -> p k n", k=24)
        p32 = arena_flat[:, 24 * D:24 * D + 24 * 36].rearrange("p (k n) -> p k n", k=24)
        tokb = sb("tokb", [DH, 2, 3])
        h = sb("h", [TT, NT, D])
        xn = sb("xn", [TT, NT, D])
        xT = sb("xT", [DH + 1, 2, T])
        bn = sb("bn", [TT, 18, 6]); mv = sb("mv", [TT, 18, 2]); rstd = sb("rstd", [TT, 18])
        flnw = sb("flnw", [DH, 2, 2])
        rwt = sb("rwt", [DH, 2, 7]); rbias = sb("rbias", [TT, 7]); tri8 = sb("tri8", [TT, 64])
        pv = sb("pv", [TT, NT, 8]); sel = sb("sel", [TT, NT, 8]); cw = sb("cw", [TT, NT, 10])
        wqkv = sb("wqkv", [DH + 1, 2, 3 * D]); ow1 = sb("ow1", [DH + 1, 2, D])
        lsc = sb("lsc", [QT, AH]); hsc = sb("hsc", [QT, AH])
        ssum = sb("ssum", [QT, 4, 24]); lg = sb("lg", [QT, 4, 4, AH]); lmx = sb("lmx", [QT, 4, AH])
        wq2 = sb("wq2", [DH, 2, 768]); wv2 = sb("wv2", [DH, 2, D]); cpw = sb("cpw", [DH, 2, D])
        xb = sb("xb", [DH, 2, N]); v17 = sb("v17", [QT, 2, AH, 17]); ysb = sb("ysb", [QT, 2, D])
        mx0 = sb("mx0", [QT, 4, 3]); mx1 = sb("mx1", [QT, 4, 3]); yrc = sb("yrc", [QT, 2, AH])
        maskA = sb("maskA", [QT, 474], BF16); maskB = sb("maskB", [QT, 378], BF16)
        wg = sb("wg", [DH, 2, ME]); tri = sb("tri", [TT, TT]); tones = sb("tones", [TT, TT])
        iota = sb("iota", [TT, CAP]); key = sb("key", [TT, NT, 10])
        wp = sb("wp", [DH, 2, 512]); pw1 = sb("pw1", [DH, 2, 128]); pb1 = sb("pb1", [128, 1])
        pw2 = sb("pw2", [128, 8]); pb2 = sb("pb2", [TT, 8]); hones = sb("hones", [128, 2])
        mT = sb("mT", [128, 2, 4, 64]); msq = sb("msq", [128, 4 * 64 + 64]); mi = sb("mi", [128, 320])
        pc = sb("pc", [64, 2, 2, 32]); gg = sb("gg", [64, 2, 32]); gsb = sb("gsb", [64, 64])
        enU = sb("enU", [64, 2, 128]); utmp = sb("utmp", [64, 2, 32])
        valT = sb("valT", [DH, 2, 512]); owT = sb("owT", [DH, 2, D]); gwT = sb("gwT", [DH, 2, 4, 16])
        vp = sb("vp", [128, 4, D]); gm = sb("gm", [128, 4, 8])
        gateb = sb("gateb", [TT, 8]); outb = sb("outb", [TT, D])
        beta = sb("beta", [TT, 1])
        big1 = sb("big1", [128, 4 * T])
        prT = big1[:, :].rearrange("p (j t) -> p j t", j=4)
        big2 = sb("big2", [128, 4 * T])
        sqT = big2[:, :].rearrange("p (j t) -> p j t", j=4)
        zT = sb("zT", [128, T])
        pn = sb("pn", [TT, NT, 16]); pp = sb("pp", [TT, NT, 8]); pa = sb("pa", [TT, NT, 8]); rr = sb("rr", [TT, NT, 8])
        ptok = sb("ptok", [TT, NT]); vtok = sb("vtok", [TT, NT]); vB = sb("vB", [TT, T])
        ovs = sb("ovs", [TT, 2, 8, 128])
        big3 = sb("big3", [128, NT * 576])
        att = big3[0:TT, 0:NT * 512].rearrange("p (t n) -> p t n", t=NT)
        x1 = big3[0:TT, :].rearrange("p (t n) -> p t n", t=NT)
        gts = sb("gts", [TT, NT, 8]); red = sb("red", [TT, NT]); gsum = sb("gsum", [TT, NT])
        h1 = sb("h1", [TT, NT, D]); h2 = sb("h2", [TT, NT, D])
        h1T = sb("h1T", [DH + 1, 2, T])
        encT = sb("encT", [DH, 2, 64]); qT0 = sb("qT0", [64, T]); qsq = sb("qsq", [64, T]); uu = sb("uu", [128, T])
        roW = sb("roW", [128, D]); rob = sb("rob", [TT, D]); ones = sb("ones", [128, 1]); sg4 = sb("sg4", [128, 1])
        imgL = sb("imgL", [2, TT]); imgR = sb("imgR", [2, HALF])
        nmax = sb("nmax", [TT, NT]); esum = sb("esum", [TT, NT]); ex = sb("ex", [TT, 2, HALF]); nei = sb("nei", [TT, NT])
        sc1 = sb("sc1", [TT, NT]); sc2 = sb("sc2", [TT, NT]); nq = sb("nq", [TT, NT])
        rw1 = sb("rw1", [DH + 1, 2, 16]); r1T = sb("r1T", [16, T]); rw2 = sb("rw2", [16, 3]); rb2 = sb("rb2", [TT, 3])
        rg = sb("rg", [TT, NT, 3])
        ew1 = sb("ew1", [DH + 1, 2, 576]); egb = sb("egb", [DH, 6, 2]); ew2 = sb("ew2", [DH + 1, 6, D])

        h2T = h1T
        aT = [b[:, 0:3 * T].rearrange("p (m t) -> p m t", m=3) for b in (big1, big2)]
        sg = big3[:, 0:6 * HALF].rearrange("p (z t) -> p z t", z=6)
        qkv = [b[0:QT, 0:4 * 3 * D].rearrange("p (l n) -> p l n", l=4) for b in (big1, big2)]
        prod = big3[0:QT, 0:3072]
        P1 = big1[0:QT, 0:12 * N].rearrange("p (g m n) -> p g m n", g=4, m=3)
        P0 = big2[0:QT, 0:12 * QT].rearrange("p (g m n) -> p g m n", g=4, m=3)
        qk = big2[:, 12 * QT:12 * QT + 6 * N].rearrange("p (z n) -> p z n", z=6)
        PT = big3[0:QT, 0:36 * QT].rearrange("p (z n) -> p z n", z=36)
        ohT = big1[0:CT, 0:4 * T].rearrange("p (s c t) -> p s c t", s=2, c=2)
        heT = big2[:, 0:12 * CAP].rearrange("p (s m c) -> p s m c", s=2, m=6)
        b3b = big3[0:TT, :].bitcast(BF16)
        xs = b3b[:, 0:3 * NT * D].rearrange("p (z t d) -> p z t d", z=3, t=NT)
        oh = b3b[:, 3 * NT * D:3 * NT * D + 2 * NT * CAP].rearrange("p (s t c) -> p s t c", s=2, t=NT)
        o1 = big4[0:QT, 0:8 * D].rearrange("p (j l n) -> p j l n", j=2, l=4)
        sqk = ovs[0:QT, :, :, :].rearrange("p a b n -> p (a b n)")[:, 0:8 * D].rearrange("p (l n) -> p l n", l=4)
        xe = big4[0:DH, 1536:1536 + 4 * CAP].rearrange("p (s k c) -> p s k c", s=2, k=2)
        eo = big4[0:CT, 2304:2304 + 4 * D].rearrange("p (s c d) -> p s c d", s=2, c=2)
        cmp = big4[0:TT, 3072:3072 + 128 * NT].rearrange("p (z t n) -> p z t n", z=2, t=NT)
        vrep = ex[:, :, :].rearrange("p a b -> p (a b)").rearrange("p (t n) -> p t n", t=NT)
        SQ = float(D) ** -0.5
        iters = FE // 2

        LOADS = dict(route=3, qkv=4, l1=5, caus=5, moe=5, mask=2, const=5, tok8=3, tok16=2, tok32=2, m=3, val=3, wp=4, small=6, b0=7, enc=3, ew1=2, ew2=3)

        LN = lambda name: [((name, g), "s") for g in range(NT // 2)]
        ring.add([(("emb", u, m), "s") for u in range(2) for m in range(2)])
        ring.add([("norms", "s"), ("g", "v")])
        ring.add([(("vp", c), "v") for c in range(4)])
        ring.add([(("h0", t), "v") for t in range(NT)])
        ring.add(LN("ln0"))
        ring.add([(("z", u), "s") for u in range(2)])
        ring.add([(("pr", j, u), "v") for j in range(4) for u in range(2)])
        ring.add([("pn", "v")])
        ring.add([(("ov", t, q), "s") for t in range(NT) for q in range(2)])
        ring.add([(("vb", u), "s") for u in range(2)])
        ring.add([(("aT", t), "s") for t in range(NT)])
        ring.add([("gl", "v")])
        ring.add([(("agT", t), "s") for t in range(NT)])
        ring.add([(("h1", t), "v") for t in range(NT)])
        ring.add(LN("h1T"))
        ring.add([(("enc", u), "s") for u in range(2)])
        ring.add([("nq", "v")])
        ring.add([((n, u), e) for u in range(2) for n, e in (("u1", "s"), ("u2", "v"))])
        ring.add([(("S", t), "s") for t in range(NT)])
        ring.add([(("rs", t), "v") for t in range(NT)])
        ring.add(LN("h2T"))
        ring.add([(("r1", u), "s") for u in range(2)])
        ring.add([("rl", "v")])
        ring.add([(("e1", t, q), "s") for t in range(NT) for q in range(2)])
        ring.add([(("e1T", u, c), "s") for u in range(2) for c in range(6)])
        ring.add([(("y", t, q), "v") for t in range(NT) for q in range(2)])

        DN = [(0, 1), (2, 3), (4,), (5,)]
        CB = [(0, 1), (2,), (3,), (4,), (5,)]
        ring.add(LN("ln1"))
        ring.add([("rt", "v")])
        ring.add([((n, s, u, m), e) for s in range(2) for u in range(2) for m in range(3) for n, e in (("g", "s"), ("u", "v"))]
                 + [(("dn", s, z), "v") for s in range(2) for z in range(4)], times=FE // 2)
        ring.add(LN("ln2"))
        ring.add([((n, j, l), e) for j in range(2) for l in range(4) for n, e in (("qk", "s"), ("vv", "s"))])
        ring.add([(("oT", j, l), "s") for j in range(2) for l in range(4)])
        ring.add([(("op", t), "v") for t in range(NT)])
        ring.add(LN("ln3"))
        ring.add([(("q2", z), "s") for z in range(3)] + [("v2", "v")]
                 + [((n, g), "v") for g in range(4) for n in ("SA", "SB")]
                 + [(("PT", z), "s") for z in range(8)] + [(("yy", j), "v") for j in range(2)]
                 + [(("yT", j), "s") for j in range(2)], times=B)
        ring.add([(("cp", t), "v") for t in range(NT)])
        ring.add(LN("ln4"))
        ring.add([("mr", "v"), ("cs", "v")])
        ring.add([(("d", s), "v") for s in range(2)] + [(("T", s, c), "s") for s in range(2) for c in range(2)]
                 + [(("fc", s, z), "s") for s in range(2) for z in range(3)] + [(("pj", s), "v") for s in range(2)]
                 + [(("cb", s, z), "v") for s in range(2) for z in range(5)], times=ME // 2)

        f_up = [sem(f"f_up{s}") for s in range(2)]; f_down = [sem(f"f_down{s}") for s in range(2)]
        m_fc = [sem(f"m_fc{s}") for s in range(2)]; m_pj = [sem(f"m_pj{s}") for s in range(2)]
        rsig_in = sem("rsig_in"); rsig = sem("rsig"); sqk_r = sem("sqk_r"); ssum_r = sem("ssum_r"); snorm = sem("snorm")
        lexp_in = sem("lexp_in"); lexp = sem("lexp"); lsexp_in = sem("lsexp_in"); lsexp = sem("lsexp"); o_ready = sem("o_ready")
        xb_r = sem("xb_r"); exp_r = sem("exp_r"); v_set = sem("v_set"); mlg = sem("mlg"); mexp = sem("mexp")
        sel_r = sem("sel_r"); xs_r = sem("xs_r"); oh_r = sem("oh_r"); h_done = sem("h_done"); v2z = sem("v2z")
        xn_ready = sem("xn_ready")
        var_ready = sem("var_ready")
        std_ready = sem("std_ready")
        prep = sem("prep")
        prep_s = sem("prep_s")
        sq_ready = sem("sq_ready")
        plog = sem("plog"); psig = sem("psig"); vrow = sem("vrow"); att_w = sem("att_w"); att_g = sem("att_g")
        gexp = sem("gexp"); ovr = sem("ovr"); nm = sem("nm"); e_used = sem("e_used")
        xob = sem("xob"); h1r = sem("h1r"); ones_set = sem("ones_set"); hh = sem("hh"); hb = sem("hb")
        rlog = sem("rlog"); rexp = sem("rexp"); e1n = sem("e1n"); bsig = sem("bsig"); stored = sem("stored")
        gact = sem("gact")

        block = ctx.enter_context(nc.Block())

        @block.sync
        def _(sp):
            def load(name, *pairs):
                s, n = loaded(name)
                assert len(pairs) * 16 == n, name
                for dst, src in pairs:
                    sp.dma_start(dst, src).then_inc(s, 16)

            load("tok8", (p8, a["p8"]), (w8, a["w8"]), (tokb[:, :, :], a["tokb"]))
            load("const", (ident[:, :], a["ident"]), (bones[:, :], a["bones"]), (sgn[:, :], a["sgn"]),
                 (hones[:, :], a["hones"]), (sg4[:, :], a["sg4"]))
            load("m", (mT[:, 0, :, :], a["m_re"]), (mT[:, 1, :, :], a["m_im"]), (pc[:, :, :, :], a["pc"]))
            load("tok16", (p16, a["p16"]), (w16, a["w16"]))
            load("tok32", (p32, a["p32"]), (w32, a["w32"]))
            load("val", (valT[:, :, :], a["valT"]), (owT[:, :, :], a["owT"]), (gwT[:, :, :, :], a["gwT"]))
            load("wp", (wp[:, :, :], a["wp"]), (pw1[:, :, :], a["pw1"]), (pb1[:, :], a["pb1"]), (pw2[:, :], a["pw2"]))
            load("b0", (pb2[:, :], a["pb2"].partition_broadcast(TT)), (gateb[:, :], a["gateb"].partition_broadcast(TT)),
                 (outb[:, :], a["outb"].partition_broadcast(TT)), (beta[:, :], a["beta"].partition_broadcast(TT)),
                 (rob[:, :], a["rob"].partition_broadcast(TT)), (rb2[:, :], a["rb2"].partition_broadcast(TT)),
                 (egb[:, :, :], a["egb"]))
            load("enc", (encT[:, :, :], a["encT"]), (roW[:, :], a["roW"]), (imgL[:, :], a["imgL"]))
            load("small", (imgR[:, :], a["imgR"]), (rw1[0:DH, :, :], a["rw1"]), (rw1[DH:DH + 1, 0, :], a["rb1"]), (rw2[:, :], a["rw2"]),
                 (identb[:, :], a["identb"]), (ones[:, :], a["ones"]))
            load("ew1", (ew1[0:DH, :, :], a["ew1"]), (ew1[DH:DH + 1, 0, :], a["eb1"]))
            load("ew2", (ew2[0:DH, :, :], a["ew2"]), (ew2[DH:DH + 1, 0:6:2, :], a["eb2"]), (ew2[DH:DH + 1, 1:6:2, :], a["eb2"]))
            load("route", (rwt[:, :, :], a["rwt"]), (rbias[:, :], a["rbias"].partition_broadcast(TT)),
                 (tri8[:, :], a["tri8"].partition_broadcast(TT)))

            def f_load(s, layer, e):
                src = a[("fgu", "fdn")[layer]][bass.ds(e, 1), :, :].rearrange("o p n -> p (o n)")
                dst = arena[0:DH, s, 0, :] if layer == 0 else arena[:, s, 1, 0:3 * D]
                sp.dma_start(dst, src).then_inc((f_up, f_down)[layer][s], 16)

            def m_load(s, layer, e):
                src = a[("mfc", "mpj")[layer]][bass.ds(e, 1), :, :].rearrange("o p n -> p (o n)")
                dst = arena[0:DH, s, 0, :] if layer == 0 else arena[:, s, 1, 0:6 * D]
                sp.dma_start(dst, src).then_inc((m_fc, m_pj)[layer][s], 16)

            sp.wait_ge(*ring.full(("emb", 1, 1)))
            for layer in range(2):
                for s in range(2):
                    f_load(s, layer, s)
            load("qkv", (wqkv[0:DH, :, :], a["wqkv"]), (wqkv[DH:DH + 1, 0, :], a["bqkv"]),
                 (ow1[0:DH, :, :], a["ow1"]), (ow1[DH:DH + 1, 0, :], a["ob1"]))
            load("l1", (lsc[:, :], a["lsc"].partition_broadcast(QT)), (hsc[:, :], a["hsc"].partition_broadcast(QT)),
                 (flnw[:, :, :], a["flnw"]), (wq2[:, :, :], a["wq2"]), (wv2[:, :, :], a["wv2"]))
            load("mask", (maskA[:, :], a["maskA"]), (maskB[:, :], a["maskB"]))
            load("moe", (cpw[:, :, :], a["cpw"]), (wg[:, :, :], a["wg"]), (tri[:, :], a["tri"]), (tones[:, :], a["tones"]),
                 (iota[:, :], a["iota"].partition_broadcast(TT)))
            with sp.Fori(0, FE // 2 - 1) as i:
                for layer in range(2):
                    for s in range(2):
                        sp.wait_ge(*ring.full((("u", s, 1, 2), ("dn", s, 3))[layer], i))
                        f_load(s, layer, 2 * i + 2 + s)
            for layer in range(2):
                for s in range(2):
                    sp.wait_ge(*ring.full((("u", s, 1, 2), ("dn", s, 3))[layer], FE // 2 - 1))
                    m_load(s, layer, s)
            with sp.Fori(0, ME // 2 - 1) as i:
                for layer in range(2):
                    for s in range(2):
                        sp.wait_ge(*ring.full((("fc", s, 2), ("pj", s))[layer], i))
                        m_load(s, layer, 2 * i + 2 + s)
            sp.wait_ge(hh, 2)
            sp.dma_start(out.rearrange("b n d -> (b n) d").rearrange("(t p) d -> p t d", p=TT), h[:, :, :]).then_inc(stored, 16)
            sp.wait_ge(stored, 16)

        @block.tensor
        def _(te):
            def take(key, i=0):
                w = ring.free(key, i)
                if w:
                    te.wait_ge(*w)
                return psum[ring.bank(key)]

            def acc(o, pairs, first=True, last=True):
                for k, (l, r) in enumerate(pairs):
                    mm = te.matmul(o, l, r, start=first and k == 0, stop=last and k == len(pairs) - 1)
                return mm

            def tr_pairs(name, src, xn_base):
                for g in range(NT // 2):
                    ps = take((name, g))
                    for q in range(2):
                        t = 2 * g + q
                        te.wait_ge(xn_ready, xn_base + t + 1)
                        for k in range(2):
                            c0 = k * 252 + q * TT
                            mm = te.transpose(ps[0:DH, c0:c0 + TT], src[:, t, k * DH:(k + 1) * DH], ident[0:TT, 0:TT])
                    mm.then_inc(bank_full, 1)

            te.wait_ge(*loaded("tok8"))
            eb = {(u, m): take(("emb", u, m)) for u in range(2) for m in range(2)}

            def emb(pt, w, kt, off, n):
                for u in range(2):
                    for m in range(2):
                        o = eb[u, m][0:DH, 0:HALF].rearrange("p (i n) -> p i n", i=2)[:, :, off:off + n]
                        mm = acc(o, [(w[:, k, m * DH:(m + 1) * DH],
                                      pt[:, k, 2 * u * n:2 * (u + 1) * n].rearrange("p (i n) -> p i n", i=2)) for k in range(kt)])
                        if kt == 24:
                            mm.then_inc(bank_full, 1)
            emb(p8, w8, 2, 0, 144)
            te.wait_ge(*loaded("tok16"))
            emb(p16, w16, 6, 144, 36)
            te.wait_ge(*loaded("tok32"))
            emb(p32, w32, 24, 180, 9)

            ps = take("norms")
            te.wait_ge(*loaded("const"))
            te.wait_ge(prep, 2)
            te.matmul(ps[:, 0:256], bones[:, :], msq[:, 0:256], start=True, stop=True)
            te.matmul(ps[0:64, 256:320], bones[0:64, 0:64], msq[0:64, 256:320], start=True, stop=True).then_inc(bank_full, 1)
            ps = take("g")
            te.wait_ge(prep, 4)
            te.matmul(ps[0:64, 0:64], bones[0:64, 0:64], gg[:, :, :], start=True, stop=True).then_inc(bank_full, 1)
            te.wait_ge(*loaded("val"))
            for c in range(4):
                ps = take(("vp", c))
                acc(ps[:, 0:D], [(valT[:, k, c * 128:(c + 1) * 128], owT[:, k, :]) for k in range(2)])
                acc(ps[:, D:D + 16], [(valT[:, k, c * 128:(c + 1) * 128], gwT[:, k, c, :]) for k in range(2)]).then_inc(bank_full, 1)

            for t in range(NT):
                ps = take(("h0", t))
                te.wait_ge(*ring.done(("emb", t // 3, 1)))
                for k in range(2):
                    mm = te.transpose(ps[0:TT, k * DH:(k + 1) * DH], xT[0:DH, k, t * TT:(t + 1) * TT], ident[0:DH, 0:DH])
                mm.then_inc(bank_full, 1)

            tr_pairs("ln0", xn, 0)
            te.wait_ge(*loaded("wp"))
            te.wait_ge(*ring.done(("ln0", 2)))
            for u in range(2):
                cs = slice(u * HALF, (u + 1) * HALF)
                acc(take(("z", u))[:, 0:HALF], [(pw1[:, k, :], xT[0:DH, k, cs]) for k in range(2)]).then_inc(bank_full, 1)
            for j in range(4):
                for u in range(2):
                    cs = slice(u * HALF, (u + 1) * HALF)
                    acc(take(("pr", j, u))[:, 0:HALF],
                        [(wp[:, k, j * 128:(j + 1) * 128], xT[0:DH, k, cs]) for k in range(2)]).then_inc(bank_full, 1)
            ps = take("pn")
            te.wait_ge(*ring.done(("z", 1)))
            te.wait_ge(sq_ready, 8)
            for t in range(NT):
                cs = slice(t * TT, (t + 1) * TT)
                for j in range(4):
                    te.matmul(ps[0:TT, t * 16 + 2 * j:t * 16 + 2 * j + 2], sqT[:, j, cs], hones[:, :], start=True, stop=True)
                mm = te.matmul(ps[0:TT, t * 16 + 8:t * 16 + 16], zT[:, cs], pw2[:, :], start=True, stop=True)
            mm.then_inc(bank_full, 1)
            te.wait_ge(*ring.done(("pr", 3, 1)))
            te.wait_ge(prep, 6)
            for t in range(NT):
                pq = [take(("ov", t, q)) for q in range(2)]
                for z in range(4):
                    for q in range(2):
                        r = slice(64 * q, 64 * q + 64)
                        mm = te.matmul(pq[q][0:TT, z * 128:(z + 1) * 128].rearrange("p (f s) -> p f s", f=2),
                                       prT[r, z, t * TT:(t + 1) * TT], mT[r, :, z, :], start=True, stop=True)
                        if z == 3:
                            mm.then_inc(bank_full, 1)
            for u in range(2):
                ps = take(("vb", u))
                if u == 0:
                    te.wait_ge(vrow, 1)
                for t in range(3):
                    mm = te.matmul(ps[0:TT, t * TT:(t + 1) * TT], vrep[:, 3 * u + t, :], ident[0:TT, 0:TT], start=True, stop=True)
                mm.then_inc(bank_full, 1)
            for t in range(NT):
                ps = take(("aT", t))
                te.wait_ge(att_w, t + 1)
                for j in range(4):
                    mm = te.transpose(ps[:, j * TT:(j + 1) * TT], att[:, t, j * 128:(j + 1) * 128], ident[0:TT, 0:TT])
                mm.then_inc(bank_full, 1)
            ps = take("gl")
            te.wait_ge(*ring.done(("vp", 3)))
            for t in range(NT):
                te.wait_ge(*ring.done(("aT", t)))
                mm = acc(ps[0:TT, t * 8:(t + 1) * 8], [(sqT[:, j, t * TT:(t + 1) * TT], gm[:, j, :]) for j in range(4)])
            mm.then_inc(bank_full, 1)
            for t in range(NT):
                ps = take(("agT", t))
                te.wait_ge(att_g, t + 1)
                for j in range(4):
                    mm = te.transpose(ps[:, j * TT:(j + 1) * TT], att[:, t, j * 128:(j + 1) * 128], ident[0:TT, 0:TT])
                mm.then_inc(bank_full, 1)
            for t in range(NT):
                ps = take(("h1", t))
                te.wait_ge(*ring.done(("agT", t)))
                acc(ps[0:TT, 0:D], [(prT[:, j, t * TT:(t + 1) * TT], vp[:, j, :]) for j in range(4)]).then_inc(bank_full, 1)
            for g in range(NT // 2):
                ps = take(("h1T", g))
                for q in range(2):
                    t = 2 * g + q
                    te.wait_ge(*ring.done(("h1", t)))
                    for k in range(2):
                        c0 = k * 252 + q * TT
                        mm = te.transpose(ps[0:DH, c0:c0 + TT], h1[:, t, k * DH:(k + 1) * DH], ident[0:TT, 0:TT])
                mm.then_inc(bank_full, 1)
            te.wait_ge(*ring.done(("h1T", 2)))
            te.wait_ge(*loaded("enc"))
            for u in range(2):
                cs = slice(u * HALF, (u + 1) * HALF)
                acc(take(("enc", u))[0:64, 0:HALF], [(encT[:, k, :], h1T[0:DH, k, cs]) for k in range(2)]).then_inc(bank_full, 1)
            ps = take("nq")
            te.wait_ge(sq_ready, 10)
            te.wait_ge(*loaded("small"))
            for t in range(NT):
                mm = te.matmul(ps[0:TT, t:t + 1], qsq[:, t * TT:(t + 1) * TT], ones[0:64, :], start=True, stop=True)
            mm.then_inc(bank_full, 1)
            te.wait_ge(prep, 10)
            te.wait_ge(*ring.done(("enc", 1)))
            for u in range(2):
                cs = slice(u * HALF, (u + 1) * HALF)
                for z in range(2):
                    te.matmul(take((("u1", "u2")[z], u))[:, 0:HALF], enU[:, z, :], qT0[:, cs], start=True, stop=True).then_inc(bank_full, 1)
            for t in range(NT):
                ps = take(("S", t))
                c0 = (t // 3) * HALF + (0 if t % 3 < 2 else N)
                n = HALF if t % 3 == 1 else N
                pairs = [(h1T[0:DH, k, t * TT:(t + 1) * TT], h1T[0:DH, k, c0:c0 + n]) for k in range(2)]
                if t % 3 == 1:
                    pairs.append((imgL[:, :], imgR[:, :]))
                acc(ps[0:TT, 0:n], pairs).then_inc(bank_full, 1)
            te.wait_ge(*ring.done(("u2", 1)))
            te.wait_ge(prep, 11)
            for t in range(NT):
                ps = take(("rs", t))
                te.matmul(ps[0:TT, 0:D], uu[:, t * TT:(t + 1) * TT], roW[:, :], start=True, stop=True).then_inc(bank_full, 1)
            for g in range(NT // 2):
                ps = take(("h2T", g))
                for q in range(2):
                    t = 2 * g + q
                    te.wait_ge(*ring.done(("rs", t)))
                    for k in range(2):
                        c0 = k * 252 + q * TT
                        mm = te.transpose(ps[0:DH, c0:c0 + TT], h2[:, t, k * DH:(k + 1) * DH], ident[0:TT, 0:TT])
                mm.then_inc(bank_full, 1)
            te.wait_ge(*ring.done(("h2T", 2)))
            te.wait_ge(ones_set, 3)

            def kr(k):
                return DH + 1 if k % 2 == 0 else DH
            for u in range(2):
                cs = slice(u * HALF, (u + 1) * HALF)
                acc(take(("r1", u))[0:16, 0:HALF], [(rw1[0:kr(k), k, :], h2T[0:kr(k), k, cs]) for k in range(2)]).then_inc(bank_full, 1)
            ps = take("rl")
            te.wait_ge(*ring.done(("r1", 1)))
            for t in range(NT):
                mm = te.matmul(ps[0:TT, t * 3:t * 3 + 3], r1T[:, t * TT:(t + 1) * TT], rw2[:, :], start=True, stop=True)
            mm.then_inc(bank_full, 1)
            te.wait_ge(*loaded("ew1"))
            for t in range(NT):
                for q in range(2):
                    n0, n1 = (0, 384) if q == 0 else (384, 576)
                    acc(take(("e1", t, q))[0:TT, 0:n1 - n0],
                        [(h2T[0:kr(k), k, t * TT:(t + 1) * TT], ew1[0:kr(k), k, n0:n1]) for k in range(2)]).then_inc(bank_full, 1)
            for u in range(2):
                te.wait_ge(e1n, 9 * (u + 1))
                for c in range(6):
                    ps = take(("e1T", u, c))
                    for t in range(3):
                        mm = te.transpose(ps[0:DH, t * TT:(t + 1) * TT], x1[:, 3 * u + t, c * DH:(c + 1) * DH], ident[0:TT, 0:TT])
                    mm.then_inc(bank_full, 1)
            te.wait_ge(*loaded("ew2"))
            for t in range(NT):
                te.wait_ge(*ring.done(("e1T", t // 3, 5)))
                for q in range(2):
                    ps = take(("y", t, q))
                    for z in range(2 - q):
                        e = 2 * q + z
                        mm = acc(ps[0:TT, z * D:(z + 1) * D],
                                 [(gT[0:kr(c), c, t * TT:(t + 1) * TT], ew2[0:kr(c), c, :]) for c in (2 * e, 2 * e + 1)])
                    mm.then_inc(bank_full, 1)
            tr_pairs("ln1", xn, NT)
            te.wait_ge(*loaded("route"))
            te.wait_ge(*ring.done(("ln1", 2)))
            ps = take("rt")
            for t in range(NT):
                mm = acc(ps[0:TT, t * 7:t * 7 + 7], [(xT[0:DH, k, t * TT:(t + 1) * TT], rwt[:, k, :]) for k in range(2)])
            mm.then_inc(bank_full, 1)
            for w in ring.all_done(("g", 0, 0, 0)):
                te.wait_ge(*w)
            with te.Fori(0, FE // 2) as i:
                for s in range(2):
                    te.wait_ge(f_up[s], 16 * i + 16)
                    up = arena[0:DH, s, 0, :].rearrange("p (k g n) -> p k g n", k=2, g=2)
                    for u in range(2):
                        cs = slice(u * HALF, (u + 1) * HALF)
                        for m in range(3):
                            for z, nm_ in enumerate("gu"):
                                acc(take((nm_, s, u, m), i)[:, 0:HALF],
                                    [(up[:, k, z, m * 128:(m + 1) * 128], xT[0:DH, k, cs]) for k in range(2)]).then_inc(bank_full, 1)
                for s in range(2):
                    te.wait_ge(f_down[s], 16 * i + 16)
                    dn = arena[:, s, 1, 0:3 * D].rearrange("p (m n) -> p m n", m=3)
                    for z, tiles in enumerate(DN):
                        ps = take(("dn", s, z), i)
                        te.wait_ge(*ring.done(("u", s, min(z, 1), 2), i))
                        for q, t in enumerate(tiles):
                            mm = acc(ps[0:TT, q * D:(q + 1) * D], [(aT[s][:, m, t * TT:(t + 1) * TT], dn[:, m, :]) for m in range(3)])
                        mm.then_inc(bank_full, 1)
            tr_pairs("ln2", xn, 2 * NT)
            te.wait_ge(*loaded("qkv"))
            te.wait_ge(*ring.done(("ln2", 2)))
            for j in range(2):
                for l in range(4):
                    c0 = l * N + j * (N - QT)
                    for z, (n0, n1) in enumerate(((0, 2 * D), (2 * D, 3 * D))):
                        acc(take((("qk", "vv")[z], j, l))[0:QT, 0:n1 - n0],
                            [(xT[0:kr(k), k, c0:c0 + QT], wqkv[0:kr(k), k, n0:n1]) for k in range(2)]).then_inc(bank_full, 1)
            for j in range(2):
                te.wait_ge(o_ready, j + 1)
                for l in range(4):
                    ps = take(("oT", j, l))
                    for k in range(2):
                        mm = te.transpose(ps[0:DH, k * QT:(k + 1) * QT], o1[:, j, l, k * DH:(k + 1) * DH], ident[0:QT, 0:QT])
                    mm.then_inc(bank_full, 1)
            te.wait_ge(*ring.done(("oT", 1, 3)))
            for t in range(NT):
                acc(take(("op", t))[0:TT, 0:D], [(h1T[0:kr(k), k, t * TT:(t + 1) * TT], ow1[0:kr(k), k, :]) for k in range(2)]).then_inc(bank_full, 1)
            tr_pairs("ln3", xn, 3 * NT)
            te.wait_ge(*loaded("l1"))
            te.wait_ge(*loaded("mask"))
            te.wait_ge(*loaded("small"))
            for w in ring.all_done(("q2", 0)):
                te.wait_ge(*w)
            with te.Fori(0, B) as b:
                te.wait_ge(xb_r, b + 1)
                for z in range(3):
                    ps = take(("q2", z), b)
                    for q in range(2):
                        m = 2 * z + q
                        mm = acc(ps[:, q * N:(q + 1) * N], [(wq2[:, k, m * 128:(m + 1) * 128], xb[:, k, :]) for k in range(2)])
                    mm.then_inc(bank_full, 1)
                ps = take("v2", b)
                for j in range(2):
                    mm = acc(ps[0:QT, j * D:(j + 1) * D],
                             [(xb[:, k, j * (N - QT):j * (N - QT) + QT], wv2[:, k, :]) for k in range(2)])
                mm.then_inc(bank_full, 1)
                te.wait_ge(*ring.done(("q2", 2), b))
                for g in range(4):
                    r = slice(32 * g, 32 * g + AD)
                    pA, pB = take(("SA", g), b), take(("SB", g), b)
                    te.matmul(pA[0:QT, 0:474], identb[0:QT, 0:QT], maskA[:, :], start=True, stop=False, skip_group_check=True)
                    for m in range(3):
                        te.matmul(pA[0:QT, m * QT:(m + 1) * QT], qk[r, m, 0:QT], qk[r, 3 + m, 0:QT], start=False, stop=True, skip_group_check=True)
                    te.matmul(pA[0:QT, 285:474], qk[r, 2, N - QT:N], qk[r, 5, :], start=False, stop=True, skip_group_check=True).then_inc(bank_full, 1)
                    te.matmul(pB[0:QT, 0:378], identb[0:QT, 0:QT], maskB[:, :], start=True, stop=False, skip_group_check=True)
                    for m in range(2):
                        mm = te.matmul(pB[0:QT, m * N:(m + 1) * N], qk[r, m, N - QT:N], qk[r, 3 + m, :], start=False, stop=True, skip_group_check=True)
                    mm.then_inc(bank_full, 1)
                for z in range(8):
                    ps = take(("PT", z), b)
                    for y in range(5 * z, min(5 * z + 5, 36)):
                        hd, c = y // 3, y % 3
                        if y % 9 == 0:
                            te.wait_ge(exp_r, 4 * b + y // 9 + 1)
                        g, m = hd // 3, hd % 3
                        src = (P0[:, g, m, :], P1[:, g, m, 0:QT], P1[:, g, m, N - QT:N])[c]
                        mm = te.transpose(ps[0:QT, (y - 5 * z) * QT:(y - 5 * z + 1) * QT], src, ident[0:QT, 0:QT])
                    mm.then_inc(bank_full, 1)
                te.wait_ge(v2z, b + 1)
                te.wait_ge(*ring.done(("PT", 7), b))
                for j in range(2):
                    ps = take(("yy", j), b)
                    for g in range(4):
                        for m in range(3):
                            hd, y = 4 * m + g, 3 * (3 * g + m)
                            pairs = [(PT[:, y, :], v17[:, 0, hd, :])] if j == 0 else \
                                [(PT[:, y + 1, :], v17[:, 0, hd, :]), (PT[:, y + 2, :], v17[:, 1, hd, :])]
                            mm = acc(ps[0:QT, hd * 17:(hd + 1) * 17], pairs)
                    mm.then_inc(bank_full, 1)
                for j in range(2):
                    ps = take(("yT", j), b)
                    te.wait_ge(*ring.done(("yy", j), b))
                    for k in range(2):
                        mm = te.transpose(ps[0:DH, k * QT:(k + 1) * QT], ysb[:, j, k * DH:(k + 1) * DH], ident[0:QT, 0:QT])
                    mm.then_inc(bank_full, 1)
            te.wait_ge(*ring.done(("yT", 1), B - 1))
            te.wait_ge(*loaded("moe"))
            for t in range(NT):
                acc(take(("cp", t))[0:TT, 0:D], [(h1T[0:DH, k, t * TT:(t + 1) * TT], cpw[:, k, :]) for k in range(2)]).then_inc(bank_full, 1)
            tr_pairs("ln4", xn, 4 * NT)
            te.wait_ge(*ring.done(("ln4", 2)))
            ps = take("mr")
            for t in range(NT):
                mm = acc(ps[0:TT, t * 8:t * 8 + 8], [(xT[0:DH, k, t * TT:(t + 1) * TT], wg[:, k, :]) for k in range(2)])
            mm.then_inc(bank_full, 1)
            ps = take("cs")
            te.wait_ge(sel_r, 1)
            for t in range(NT):
                mm = acc(ps[0:TT, t * 8:t * 8 + 8], [(tones[:, :], sel[:, q, :]) for q in range(t)] + [(tri[:, :], sel[:, t, :])])
            mm.then_inc(bank_full, 1)
            te.wait_ge(xs_r, 1)
            for w in ring.all_done(("d", 0)):
                te.wait_ge(*w)
            with te.Fori(0, ME // 2) as i:
                for s in range(2):
                    ps = take(("d", s), i)
                    te.wait_ge(oh_r, 2 * i + s + 1)
                    for k in range(2):
                        mm = acc(ps[0:DH, k * CAP:(k + 1) * CAP],
                                 [(xs[:, z, t, k * DH:(k + 1) * DH], oh[:, s, t, :]) for t in range(NT) for z in range(3)])
                    mm.then_inc(bank_full, 1)
                for s in range(2):
                    for c in range(2):
                        ps = take(("T", s, c), i)[:, :].bitcast(BF16)
                        for t in range(NT):
                            mm = te.transpose(ps[0:CT, t * TT:(t + 1) * TT], oh[:, s, t, c * CT:(c + 1) * CT], identb[0:TT, 0:TT])
                        mm.then_inc(bank_full, 1)
                for s in range(2):
                    te.wait_ge(m_fc[s], 16 * i + 16)
                    te.wait_ge(*ring.done(("d", s), i))
                    fc = arena[0:DH, s, 0, :].rearrange("p (k n) -> p k n", k=2)
                    for z in range(3):
                        ps = take(("fc", s, z), i)
                        for q in range(2):
                            m = 2 * z + q
                            mm = acc(ps[:, q * CAP:(q + 1) * CAP], [(fc[:, k, m * 128:(m + 1) * 128], xe[:, s, k, :]) for k in range(2)])
                        mm.then_inc(bank_full, 1)
                for s in range(2):
                    te.wait_ge(m_pj[s], 16 * i + 16)
                    pj = arena[:, s, 1, 0:6 * D].rearrange("p (m n) -> p m n", m=6)
                    ps = take(("pj", s), i)
                    te.wait_ge(*ring.done(("fc", s, 2), i))
                    for c in range(2):
                        mm = acc(ps[0:CT, c * D:(c + 1) * D], [(heT[:, s, m, c * CT:(c + 1) * CT], pj[:, m, :]) for m in range(6)])
                    mm.then_inc(bank_full, 1)
                for s in range(2):
                    te.wait_ge(*ring.done(("T", s, 1), i))
                    te.wait_ge(*ring.done(("pj", s), i))
                    for z, tiles in enumerate(CB):
                        ps = take(("cb", s, z), i)
                        for q, t in enumerate(tiles):
                            mm = acc(ps[0:TT, q * D:(q + 1) * D], [(ohT[:, s, c, t * TT:(t + 1) * TT], eo[:, s, c, :]) for c in range(2)])
                        mm.then_inc(bank_full, 1)

        @block.scalar
        def _(ac):
            step = [0]

            def full(key, i=0):
                ac.wait_ge(*ring.full(key, i))
                return psum[ring.bank(key)]

            def evac_pairs(name, dst):
                for g in range(NT // 2):
                    ps = full((name, g))
                    ac.activation(dst[0:DH, :, g * 252:(g + 1) * 252], ps[0:DH, 0:504].rearrange("p (k t) -> p k t", k=2),
                                  ACT.Copy).then_inc(emptied_s, 1)

            ac.wait_ge(*loaded("tok8"))
            for u in range(2):
                for m in range(2):
                    ps = full(("emb", u, m))
                    src = ps[0:DH, 0:HALF].rearrange("p (i n) -> p i n", i=2)
                    dst = xT[0:DH, m, u * HALF:(u + 1) * HALF].rearrange("p (i n) -> p i n", i=2)
                    off = 0
                    for k, n in enumerate(PATCHES):
                        it = ac.activation(dst[:, :, off:off + n], src[:, :, off:off + n], ACT.Identity, bias=tokb[:, m, k:k + 1])
                        off += n
                    it.then_inc(emptied_s, 1)
            ps = full("norms")
            ac.activation(mi[:, 0:256], ps[:, 0:256], ACT.Sqrt)
            ac.activation(mi[0:64, 256:320], ps[0:64, 256:320], ACT.Sqrt).then_inc(emptied_s, 1)

            ac.wait_ge(var_ready, 1)
            ac.activation(rstd[:, 0:NT], rstd[:, 0:NT], ACT.Sqrt).then_inc(std_ready, 1)
            evac_pairs("ln0", xT)
            ac.wait_ge(*loaded("wp"))
            for u in range(2):
                ps = full(("z", u))
                ac.activation(zT[:, u * HALF:(u + 1) * HALF], ps[:, 0:HALF], ACT.Silu, bias=pb1[:, 0:1]).then_inc(emptied_s, 1)
            for j in range(4):
                for u in range(2):
                    ac.wait_ge(*ring.done(("pr", j, u)))
                    cs = slice(u * HALF, (u + 1) * HALF)
                    ac.activation(sqT[:, j, cs], prT[:, j, cs], ACT.Square).then_inc(sq_ready, 1)
            ac.wait_ge(plog, 1)
            ac.activation(pp[:, :, :], pn[:, :, 8:16], ACT.Sigmoid).then_inc(psig, 1)
            ac.wait_ge(*loaded("b0"))
            ac.activation(beta[:, :], beta[:, :], ACT.Sigmoid).then_inc(bsig, 1)
            for t in range(NT):
                for q in range(2):
                    ps = full(("ov", t, q))
                    if t >= 2 and q == 0:
                        ac.wait_ge(ovr, t - 1)
                    ac.activation(ovs[:, t % 2, q:8:2, :], ps[0:TT, :].rearrange("p (a n) -> p a n", a=4),
                                  ACT.Square).then_inc(emptied_s, 1)
            for u in range(2):
                ps = full(("vb", u))
                ac.activation(vB[:, u * HALF:(u + 1) * HALF], ps[0:TT, 0:HALF], ACT.Copy).then_inc(emptied_s, 1)
            for t in range(NT):
                ps = full(("aT", t))
                ac.activation(sqT[:, :, t * TT:(t + 1) * TT], ps[:, 0:504].rearrange("p (j t) -> p j t", j=4), ACT.Copy).then_inc(emptied_s, 1)
            ac.wait_ge(plog, 2)
            ac.activation(gts[:, :, :], gts[:, :, :], ACT.Exp).then_inc(gexp, 1)
            for t in range(NT):
                ps = full(("agT", t))
                ac.activation(prT[:, :, t * TT:(t + 1) * TT], ps[:, 0:504].rearrange("p (j t) -> p j t", j=4), ACT.Copy).then_inc(emptied_s, 1)
            evac_pairs("h1T", h1T)
            for u in range(2):
                cs = slice(u * HALF, (u + 1) * HALF)
                ps = full(("enc", u))
                ac.activation(qsq[:, cs], ps[0:64, 0:HALF], ACT.Square).then_inc(sq_ready, 1)
                ac.activation(qT0[:, cs], ps[0:64, 0:HALF], ACT.Copy).then_inc(emptied_s, 1)
            for u in range(2):
                ps = full(("u1", u))
                ac.activation(uu[:, u * HALF:(u + 1) * HALF], ps[:, 0:HALF], ACT.Copy).then_inc(emptied_s, 1)
            for t in range(NT):
                ps = full(("S", t))
                n = HALF if t % 3 == 1 else N
                ac.wait_ge(nm, t + 1)
                if t >= 2:
                    ac.wait_ge(e_used, t - 1)
                ac.activation(ex[:, t % 2, 0:n], ps[0:TT, 0:n], ACT.Exp, bias=nmax[:, t:t + 1], scale=SQ,
                              accum_out=esum[:, t:t + 1]).then_inc(emptied_s, 1)
            evac_pairs("h2T", h2T)
            for u in range(2):
                cs = slice(u * HALF, (u + 1) * HALF)
                ps = full(("r1", u))
                ac.activation(r1T[:, cs], ps[0:16, 0:HALF], ACT.Gelu).then_inc(emptied_s, 1)
            for t in range(NT):
                for q in range(2):
                    n0, n1 = (0, 384) if q == 0 else (384, 576)
                    ps = full(("e1", t, q))
                    ac.activation(x1[:, t, n0:n1], ps[0:TT, 0:n1 - n0], ACT.Copy).then_inc(emptied_s, 1)
            ac.wait_ge(rlog, 1)
            ac.activation(rg[:, :, :], rg[:, :, :], ACT.Exp).then_inc(rexp, 1)
            ac.wait_ge(var_ready, 2)
            ac.activation(rstd[:, :], rstd[:, :], ACT.Sqrt).then_inc(std_ready, 1)
            for u in range(2):
                for c in range(6):
                    ps = full(("e1T", u, c))
                    ac.activation(gT[0:DH, c, u * HALF:(u + 1) * HALF], ps[0:DH, 0:HALF], ACT.Gelu,
                                  scale=egb[:, c, 0:1], bias=egb[:, c, 1:2]).then_inc(emptied_s, 1)
            ac.wait_ge(var_ready, 3)
            ac.activation(rstd[:, 0:NT], rstd[:, 0:NT], ACT.Sqrt).then_inc(std_ready, 1)
            evac_pairs("ln1", xT)
            ac.wait_ge(rsig_in, 1)
            ac.activation(pv[:, :, 0:7], pv[:, :, 0:7], ACT.Sigmoid).then_inc(rsig, 1)
            with ac.Fori(0, FE // 2) as i:
                for s in range(2):
                    for u in range(2):
                        for m in range(3):
                            ps = full(("g", s, u, m), i)
                            ac.wait_ge(*ring.done(("u", 1 - s, u, m), i, back=1 - s))
                            ac.activation(sg[:, 3 * u + m, :], ps[:, 0:HALF], ACT.Silu).then_inc(emptied_s, 1)
            ac.wait_ge(var_ready, 4)
            ac.activation(rstd[:, 0:NT], rstd[:, 0:NT], ACT.Sqrt).then_inc(std_ready, 1)
            evac_pairs("ln2", xT)
            for j in range(2):
                for l in range(4):
                    ps = full(("qk", j, l))
                    ac.activation(qkv[j][:, l, 0:2 * D], ps[0:QT, 0:2 * D], ACT.Copy)
                    if j == 1:
                        ac.wait_ge(ssum_r, 1)
                    ac.activation(sqk[:, l, :], ps[0:QT, 0:2 * D], ACT.Square).then_inc(emptied_s, 1)
                    ps = full(("vv", j, l))
                    ac.activation(qkv[j][:, l, 2 * D:3 * D], ps[0:QT, 0:D], ACT.Copy).then_inc(emptied_s, 1)
                ac.wait_ge(ssum_r, j + 1)
                ac.activation(ssum[:, :, :], ssum[:, :, :], ACT.Sqrt).then_inc(snorm, 1)
                if j == 0:
                    ac.wait_ge(lsexp_in, 1)
                    ac.activation(lsc[:, :], lsc[:, :], ACT.Exp).then_inc(lsexp, 1)
                ac.wait_ge(lexp_in, j + 1)
                ac.activation(lg[:, :, :, :], lg[:, :, :, :], ACT.Exp).then_inc(lexp, 1)
            for j in range(2):
                for l in range(4):
                    ps = full(("oT", j, l))
                    c0 = l * N + j * QT
                    ac.activation(h1T[0:DH, :, c0:c0 + QT - j], ps[0:DH, 0:2 * QT].rearrange("p (k t) -> p k t", k=2)[:, :, j:QT],
                                  ACT.Copy).then_inc(emptied_s, 1)

            def evac_scaled(name, w):
                for g in range(NT // 2):
                    ps = full((name, g))
                    for k in range(2):
                        it = ac.activation(xT[0:DH, k, g * 252:(g + 1) * 252], ps[0:DH, k * 252:(k + 1) * 252],
                                           ACT.Copy, scale=flnw[:, w, k:k + 1])
                    it.then_inc(emptied_s, 1)
            for n in (5, 6):
                ac.wait_ge(var_ready, n)
                ac.activation(rstd[:, 0:NT], rstd[:, 0:NT], ACT.Sqrt).then_inc(std_ready, 1)
            ac.wait_ge(*loaded("l1"))
            evac_scaled("ln3", 0)
            ac.wait_ge(*ring.done(("ln3", 2)))
            with ac.Fori(0, B) as b:
                ac.activation(xb[:, :, :], xT[0:DH, :, bass.ds(b * N, N)], ACT.Copy).then_inc(xb_r, 1)
                for z in range(3):
                    ps = full(("q2", z), b)
                    ac.activation(qk[:, 2 * z:2 * z + 2, :], ps[:, 0:2 * N].rearrange("p (q n) -> p q n", q=2), ACT.Copy).then_inc(emptied_s, 1)
                for g in range(4):
                    ac.wait_ge(*ring.done(("SB", g), b))
                    ac.activation(P0[:, g, :, :], P0[:, g, :, :], ACT.Exp, scale=float(AD) ** -0.5)
                    ac.activation(P1[:, g, :, :], P1[:, g, :, :], ACT.Exp, scale=float(AD) ** -0.5).then_inc(exp_r, 1)
                for z in range(8):
                    n = min(5, 36 - 5 * z)
                    ps = full(("PT", z), b)
                    ac.activation(PT[:, 5 * z:5 * z + n, :], ps[0:QT, 0:n * QT].rearrange("p (z n) -> p z n", z=n), ACT.Copy).then_inc(emptied_s, 1)
                for j in range(2):
                    ps = full(("yT", j), b)
                    ac.activation(h1T[0:DH, :, bass.ds(b * N + j * QT, QT - j)], ps[0:DH, 0:2 * QT].rearrange("p (k t) -> p k t", k=2)[:, :, j:QT],
                                  ACT.Copy).then_inc(emptied_s, 1)
            ac.wait_ge(var_ready, 7)
            ac.activation(rstd[:, 0:NT], rstd[:, 0:NT], ACT.Sqrt).then_inc(std_ready, 1)
            evac_scaled("ln4", 1)
            ac.wait_ge(mlg, 1)
            ac.activation(pv[:, :, :], pv[:, :, :], ACT.Exp).then_inc(mexp, 1)
            with ac.Fori(0, ME // 2) as i:
                for s in range(2):
                    for c in range(2):
                        ps = full(("T", s, c), i)
                        ac.activation(ohT[:, s, c, :], ps[:, :].bitcast(BF16)[0:CT, 0:T], ACT.Copy).then_inc(emptied_s, 1)
                for s in range(2):
                    for z in range(3):
                        ps = full(("fc", s, z), i)
                        ac.activation(heT[:, s, 2 * z:2 * z + 2, :], ps[:, 0:2 * CAP].rearrange("p (q c) -> p q c", q=2),
                                      ACT.Gelu).then_inc(emptied_s, 1)

        @block.vector
        def _(ve):
            n_step = [0]

            def st(inst):
                inst.then_inc(v_step, 1)
                n_step[0] += 1

            def own():
                ve.wait_ge(v_step, n_step[0])

            def full(key, i=0):
                ve.wait_ge(*ring.full(key, i))
                return psum[ring.bank(key)]

            def bc(ap, shape):
                return ap.unsqueeze(len(ap.shape)).to_broadcast(shape)

            def layernorm(var_n, src=h, dst=xn):
                for t in range(NT):
                    st(ve.bn_stats(bn[:, t, :], src[:, t, :]))
                own()
                for t in range(NT):
                    st(ve.bn_aggr(mv[:, t, :], bn[:, t, :]))
                own()
                ve.tensor_scalar(rstd[:, 0:NT], mv[:, 0:NT, 1], EPS, None, ALU.add).then_inc(var_ready, 1)
                ve.wait_ge(std_ready, var_n)
                st(ve.reciprocal(rstd[:, 0:NT], rstd[:, 0:NT]))
                own()
                for t in range(NT):
                    it = ve.tensor_scalar(dst[:, t, :], src[:, t, :], mv[:, t, 0:1], rstd[:, t:t + 1], ALU.subtract, ALU.mult)
                    if dst is xn:
                        it.then_inc(xn_ready, 1)
                    else:
                        st(it)
                own()

            ve.memset(xT[DH:DH + 1, :, :], 1.0).then_inc(ones_set, 1)
            ve.memset(h1T[DH:DH + 1, :, :], 1.0).then_inc(ones_set, 1)
            ve.wait_ge(*loaded("m"))
            ve.wait_ge(*loaded("const"))
            ve.tensor_tensor(msq[:, 0:256], mT[:, 0, :, :], mT[:, 0, :, :], ALU.mult).then_inc(prep, 1)
            ve.tensor_tensor(msq[0:64, 256:320], pc[:, 0, :, :], pc[:, 0, :, :], ALU.mult).then_inc(prep, 1)
            st(ve.tensor_scalar(mT[:, 1, :, :], mT[:, 1, :, :], sgn[:, 0:1], None, ALU.mult))
            st(ve.tensor_scalar(pc[:, 1, :, :], pc[:, 1, :, :], sgn[0:64, 0:1], None, ALU.mult))
            ve.wait_ge(*ring.done("norms"))
            own()
            st(ve.tensor_scalar(mi[:, 0:256], mi[:, 0:256], 1e-12, None, ALU.max))
            st(ve.tensor_scalar(mi[0:64, 256:320], mi[0:64, 256:320], 1e-12, None, ALU.max))
            own()
            st(ve.reciprocal(mi[:, 0:256], mi[:, 0:256]))
            st(ve.reciprocal(mi[0:64, 256:320], mi[0:64, 256:320]))
            own()
            for f in range(2):
                st(ve.tensor_tensor(pc[:, f, :, :], pc[:, f, :, :], mi[0:64, 256:320].rearrange("p (a r) -> p a r", a=2), ALU.mult))
            own()
            for f in range(2):
                ve.tensor_tensor(gg[:, f, :], pc[:, 0, 0, :], pc[:, f, 1, :], ALU.mult).then_inc(prep, 1)
            for f in range(2):
                ve.tensor_tensor(mT[:, f, :, :], mT[:, f, :, :], mi[:, 0:256].rearrange("p (a s) -> p a s", a=4), ALU.mult).then_inc(prep, 1)
            ps = full("g")
            ve.tensor_copy(gsb[:, :], ps[0:64, 0:64]).then_inc(emptied_v, 1)
            ve.wait_ge(*ring.done("g"))
            gre, gim = gsb[:, 0:32], gsb[:, 32:64]
            st(ve.tensor_tensor(utmp[:, 0, :], pc[:, 1, 0, :], gim, ALU.mult))
            st(ve.tensor_tensor(utmp[:, 1, :], pc[:, 1, 0, :], gre, ALU.mult))
            st(ve.tensor_tensor(enU[:, 0, 0:32], pc[:, 0, 0, :], gre, ALU.mult))
            st(ve.tensor_tensor(enU[:, 0, 32:64], pc[:, 0, 0, :], gim, ALU.mult))
            own()
            st(ve.tensor_tensor(enU[:, 0, 0:32], enU[:, 0, 0:32], utmp[:, 0, :], ALU.subtract))
            st(ve.tensor_tensor(enU[:, 0, 32:64], enU[:, 0, 32:64], utmp[:, 1, :], ALU.add))
            own()
            ve.tensor_copy(enU[:, 0, 64:96], enU[:, 0, 32:64]).then_inc(prep, 1)
            ve.tensor_copy(enU[:, 0, 96:128], enU[:, 0, 0:32]).then_inc(prep, 1)
            for q in range(2):
                ve.tensor_copy(enU[:, 1, 64 * q:64 * q + 64].rearrange("p (f r) -> p f r", f=2), pc[:, :, 1, :]).then_inc(prep, 1)
            for c in range(4):
                ps = full(("vp", c))
                ve.tensor_copy(gm[0:64, c, :], ps[0:64, D:D + 8])
                ve.tensor_copy(gm[64:128, c, :], ps[64:128, D + 8:D + 16])
                ve.tensor_copy(vp[:, c, :], ps[:, 0:D]).then_inc(emptied_v, 1)
            for t in range(NT):
                ps = full(("h0", t))
                ve.tensor_copy(h[:, t, :], ps[0:TT, 0:D]).then_inc(emptied_v, 1)
            ve.wait_ge(*ring.done(("h0", NT - 1)))
            ve.memset(gT[DH:DH + 1, :, :], 1.0).then_inc(ones_set, 1)
            layernorm(1)
            for j in range(4):
                for u in range(2):
                    ps = full(("pr", j, u))
                    ve.tensor_copy(prT[:, j, u * HALF:(u + 1) * HALF], ps[:, 0:HALF]).then_inc(emptied_v, 1)
            ve.wait_ge(*loaded("b0"))
            ps = full("pn")
            ve.tensor_copy(pn[:, :, :], ps[0:TT, 0:96].rearrange("p (t n) -> p t n", t=NT)).then_inc(emptied_v, 1)
            ve.wait_ge(*ring.done("pn"))
            ve.tensor_tensor(pn[:, :, 8:16], pn[:, :, 8:16], pb2[:, :].unsqueeze(1).to_broadcast([TT, NT, 8]), ALU.add).then_inc(plog, 1)
            st(ve.tensor_scalar(pn[:, :, 0:8], pn[:, :, 0:8], 1e-24, None, ALU.max))
            own()
            st(ve.reciprocal(pn[:, :, 0:8], pn[:, :, 0:8]))
            ve.wait_ge(psig, 1)
            st(ve.tensor_scalar(pp[:, :, :], pp[:, :, :], 0.95, None, ALU.mult))
            own()
            st(ve.tensor_scalar(pa[:, :, :], pp[:, :, :], -1.0, 1.0, ALU.mult, ALU.add))
            st(ve.tensor_reduce(ptok[:, :], pp[:, :, :], X, ALU.add))
            own()
            st(ve.tensor_tensor(pa[:, :, :], pa[:, :, :], pn[:, :, 0:8], ALU.mult))
            st(ve.tensor_scalar(ptok[:, :], ptok[:, :], 1.0 / S0H, None, ALU.mult))
            own()
            st(ve.tensor_scalar(vtok[:, :], ptok[:, :], -1.0, 1.0, ALU.mult, ALU.add))
            own()
            ve.tensor_copy(vrep[:, :, :], bc(vtok[:, :], [TT, NT, TT])).then_inc(vrow, 1)
            for t in range(NT):
                av = att[:, t, :].rearrange("p (a s) -> p a s", a=8)
                ve.wait_ge(*ring.done(("ov", t, 1)))
                ve.tensor_tensor(av, ovs[:, t % 2, :, 0:64], ovs[:, t % 2, :, 64:128], ALU.add).then_inc(ovr, 1)
                ve.wait_ge(ovr, t + 1)
                st(ve.tensor_reduce(rr[:, t, :], av, X, ALU.add))
                own()
                st(ve.tensor_tensor(rr[:, t, :], rr[:, t, :], pa[:, t, :], ALU.mult))
                own()
                st(ve.scalar_tensor_tensor(rr[:, t, :], pp[:, t, :], float(S0S) / S0D, rr[:, t, :], ALU.mult, ALU.add))
                own()
                st(ve.tensor_scalar(rr[:, t, :], rr[:, t, :], 1e-8, None, ALU.add))
                own()
                st(ve.reciprocal(rr[:, t, :], rr[:, t, :]))
                own()
                st(ve.tensor_tensor(pn[:, t, 0:8], pa[:, t, :], rr[:, t, :], ALU.mult))
                st(ve.scalar_tensor_tensor(pn[:, t, 8:16], pp[:, t, :], 1.0 / S0D, rr[:, t, :], ALU.mult, ALU.mult))
                own()
                st(ve.tensor_tensor(av, av, bc(pn[:, t, 0:8], [TT, 8, 64]), ALU.mult))
                own()
                ve.tensor_tensor(av, av, bc(pn[:, t, 8:16], [TT, 8, 64]), ALU.add).then_inc(att_w, 1)
            ps = full("gl")
            ve.tensor_tensor(gts[:, :, :], ps[0:TT, 0:48].rearrange("p (t n) -> p t n", t=NT),
                             gateb[:, :].unsqueeze(1).to_broadcast([TT, NT, 8]), ALU.add).then_inc(emptied_v, 1)
            ve.wait_ge(*ring.done("gl"))
            st(ve.tensor_reduce(red[:, :], gts[:, :, :], X, ALU.max))
            own()
            ve.tensor_tensor(gts[:, :, :], gts[:, :, :], bc(red[:, :], [TT, NT, 8]), ALU.subtract).then_inc(plog, 1)
            ve.wait_ge(gexp, 1)
            st(ve.tensor_reduce(gsum[:, :], gts[:, :, :], X, ALU.add))
            own()
            st(ve.reciprocal(gsum[:, :], gsum[:, :]))
            own()
            st(ve.tensor_tensor(gts[:, :, :], gts[:, :, :], bc(gsum[:, :], [TT, NT, 8]), ALU.mult))
            own()
            for t in range(NT):
                av = att[:, t, :].rearrange("p (a s) -> p a s", a=8)
                ve.tensor_tensor(av, av, bc(gts[:, t, :], [TT, 8, 64]), ALU.mult).then_inc(att_g, 1)
            for t in range(NT):
                ps = full(("h1", t))
                ve.wait_ge(xob, t + 1)
                ve.tensor_tensor(h1[:, t, :], ps[0:TT, 0:D], xn[:, t, :], ALU.add).then_inc(emptied_v, 1)
            ps = full("nq")
            ve.tensor_scalar(nq[:, :], ps[0:TT, 0:NT], 1e-24, None, ALU.max).then_inc(emptied_v, 1)
            ve.wait_ge(*ring.done("nq"))
            st(ve.reciprocal(nq[:, :], nq[:, :]))
            for u in range(2):
                ps = full(("u2", u))
                ve.wait_ge(*ring.done(("u1", u)))
                cs = slice(u * HALF, (u + 1) * HALF)
                ve.tensor_tensor(uu[:, cs], uu[:, cs], ps[:, 0:HALF], ALU.mult).then_inc(emptied_v, 1)
            ve.wait_ge(*loaded("enc"))
            ve.tensor_scalar(roW[:, :], roW[:, :], sg4[:, 0:1], None, ALU.mult).then_inc(prep, 1)

            def coupled(t):
                n = HALF if t % 3 == 1 else N
                c0 = (t // 3) * HALF + (0 if t % 3 < 2 else N)
                ve.wait_ge(*ring.done(("S", t)))
                ve.tensor_tensor_reduce(ex[:, t % 2, 0:n], ex[:, t % 2, 0:n], vB[:, c0:c0 + n], 1.0, 0.0,
                                        ALU.mult, ALU.add, nei[:, t:t + 1]).then_inc(e_used, 1)
            ve.wait_ge(*ring.done(("vb", 1)))
            for t in range(NT):
                n = HALF if t % 3 == 1 else N
                c0 = (t // 3) * HALF + (0 if t % 3 < 2 else N)
                ps = full(("S", t))
                st(ve.tensor_reduce(red[:, t:t + 1], ps[0:TT, 0:n], X, ALU.max))
                own()
                ve.tensor_scalar(nmax[:, t:t + 1], red[:, t:t + 1], -SQ, None, ALU.mult).then_inc(nm, 1)
                if t >= 1:
                    coupled(t - 1)
            coupled(NT - 1)
            ve.wait_ge(e_used, NT)
            st(ve.reciprocal(esum[:, :], esum[:, :]))
            own()
            st(ve.tensor_tensor(nei[:, :], nei[:, :], esum[:, :], ALU.mult))
            own()
            ve.wait_ge(bsig, 1)
            st(ve.tensor_scalar(nei[:, :], nei[:, :], beta[:, 0:1], None, ALU.mult))
            own()
            st(ve.tensor_scalar(nei[:, :], nei[:, :], -1.0, 1.0, ALU.mult, ALU.add))
            own()
            st(ve.tensor_tensor(sc2[:, :], ptok[:, :], nei[:, :], ALU.mult))
            own()
            st(ve.tensor_scalar(sc2[:, :], sc2[:, :], 0.0, 0.95, ALU.max, ALU.min))
            own()
            st(ve.tensor_scalar(sc2[:, :], sc2[:, :], -1.0, 1.0, ALU.mult, ALU.add))
            own()
            st(ve.tensor_tensor(sc1[:, :], sc2[:, :], nq[:, :], ALU.mult))
            for t in range(NT):
                st(ve.scalar_tensor_tensor(h2[:, t, :], rob[:, :], sc2[:, t:t + 1], h1[:, t, :], ALU.mult, ALU.add))
            own()
            for t in range(NT):
                ps = full(("rs", t))
                ve.scalar_tensor_tensor(h2[:, t, :], ps[0:TT, 0:D], sc1[:, t:t + 1], h2[:, t, :], ALU.mult, ALU.add).then_inc(emptied_v, 1)
            ps = full("rl")
            ve.tensor_tensor(rg[:, :, :], ps[0:TT, 0:18].rearrange("p (t n) -> p t n", t=NT),
                             rb2[:, :].unsqueeze(1).to_broadcast([TT, NT, 3]), ALU.add).then_inc(emptied_v, 1)
            ve.wait_ge(*ring.done("rl"))
            st(ve.tensor_reduce(red[:, :], rg[:, :, :], X, ALU.max))
            own()
            ve.tensor_tensor(rg[:, :, :], rg[:, :, :], bc(red[:, :], [TT, NT, 3]), ALU.subtract).then_inc(rlog, 1)
            for t in range(NT):
                ve.wait_ge(*ring.done(("e1", t, 1)))
                for e in range(3):
                    st(ve.bn_stats(bn[:, 3 * t + e, :], x1[:, t, e * D:(e + 1) * D]))
                own()
                for e in range(3):
                    st(ve.bn_aggr(mv[:, 3 * t + e, :], bn[:, 3 * t + e, :]))
            own()
            ve.tensor_scalar(rstd[:, :], mv[:, :, 1], EPS, None, ALU.add).then_inc(var_ready, 1)
            ve.wait_ge(rexp, 1)
            st(ve.tensor_reduce(gsum[:, :], rg[:, :, :], X, ALU.add))
            own()
            st(ve.reciprocal(gsum[:, :], gsum[:, :]))
            own()
            st(ve.tensor_tensor(rg[:, :, :], rg[:, :, :], bc(gsum[:, :], [TT, NT, 3]), ALU.mult))
            ve.wait_ge(std_ready, 2)
            st(ve.reciprocal(rstd[:, :], rstd[:, :]))
            own()
            for t in range(NT):
                for e in range(3):
                    z = 3 * t + e
                    ve.tensor_scalar(x1[:, t, e * D:(e + 1) * D], x1[:, t, e * D:(e + 1) * D], mv[:, z, 0:1], rstd[:, z:z + 1],
                                     ALU.subtract, ALU.mult).then_inc(e1n, 1)
            for t in range(NT):
                ve.wait_ge(hb, t + 1)
                for e in range(3):
                    ps = full(("y", t, e // 2))
                    own()
                    it = ve.scalar_tensor_tensor(h[:, t, :], ps[0:TT, (e % 2) * D:(e % 2 + 1) * D], rg[:, t, e:e + 1], h[:, t, :],
                                                 ALU.mult, ALU.add)
                    if e == 0:
                        st(it)
                    else:
                        it.then_inc(emptied_v, 1)
                        ve.wait_ge(*ring.done(("y", t, e // 2)))
            def top_two(v):
                lo = v.unsqueeze(3).to_broadcast([TT, NT, 8, 8])
                hi = v.unsqueeze(2).to_broadcast([TT, NT, 8, 8])
                g_, e_ = (cmp[:, z, :, :].rearrange("p t (a b) -> p t a b", a=8) for z in range(2))
                st(ve.tensor_tensor(g_, hi, lo, ALU.is_gt))
                st(ve.tensor_tensor(e_, hi, lo, ALU.is_equal))
                own()
                st(ve.tensor_tensor(cmp[:, 1, :, :], cmp[:, 1, :, :], tri8[:, :].unsqueeze(1).to_broadcast([TT, NT, 64]), ALU.mult))
                own()
                st(ve.tensor_tensor(cmp[:, 0, :, :], cmp[:, 0, :, :], cmp[:, 1, :, :], ALU.add))
                own()
                st(ve.tensor_reduce(sel[:, :, :], g_, X, ALU.add))
                own()

            layernorm(3)
            st(ve.memset(pv[:, :, 7:8], -1.0))
            st(ve.memset(cw[:, :, 7:8], 1.0))
            ve.wait_ge(*loaded("route"))
            ps = full("rt")
            ve.tensor_tensor(pv[:, :, 0:7], ps[0:TT, 0:42].rearrange("p (t n) -> p t n", t=NT),
                             rbias[:, :].unsqueeze(1).to_broadcast([TT, NT, 7]), ALU.mult).then_inc(emptied_v, 1)
            ve.wait_ge(*ring.done("rt"))
            ve.memset(red[:, :], 0.0).then_inc(rsig_in, 1)
            ve.wait_ge(rsig, 1)
            own()
            top_two(pv[:, :, :])
            st(ve.tensor_scalar(sel[:, :, :], sel[:, :, :], 1.5, None, ALU.is_lt))
            own()
            st(ve.tensor_tensor(sel[:, :, 0:7], sel[:, :, 0:7], pv[:, :, 0:7], ALU.mult))
            own()
            st(ve.tensor_reduce(gsum[:, :], sel[:, :, 0:7], X, ALU.add))
            own()
            st(ve.reciprocal(gsum[:, :], gsum[:, :]))
            own()
            st(ve.tensor_tensor(cw[:, :, 0:7], sel[:, :, 0:7], bc(gsum[:, :], [TT, NT, 7]), ALU.mult))
            own()
            with ve.Fori(0, FE // 2) as i:
                for s in range(2):
                    for u in range(2):
                        for m in range(3):
                            ps = full(("u", s, u, m), i)
                            ve.wait_ge(*ring.done(("g", s, u, m), i))
                            ve.tensor_tensor(aT[s][:, m, u * HALF:(u + 1) * HALF], ps[:, 0:HALF], sg[:, 3 * u + m, :],
                                             ALU.mult).then_inc(emptied_v, 1)
                for s in range(2):
                    ve.wait_ge(*ring.done(("dn", 1 - s, 3), i, back=1 - s))
                    for z, tiles in enumerate(DN):
                        ps = full(("dn", s, z), i)
                        for q, t in enumerate(tiles):
                            it = ve.scalar_tensor_tensor(h[:, t, :], ps[0:TT, q * D:(q + 1) * D], cw[:, t, bass.ds(2 * i + s, 1)],
                                                         h[:, t, :], ALU.mult, ALU.add)
                        it.then_inc(emptied_v, 1)
            ve.wait_ge(*ring.done(("dn", 1, 3), FE // 2 - 1))
            layernorm(4)
            ve.wait_ge(*loaded("l1"))
            ve.tensor_scalar(lsc[:, :], lsc[:, :], 4.605170185988092, None, ALU.min).then_inc(lsexp_in, 1)
            for j in range(2):
                Q = qkv[j]
                ve.wait_ge(*ring.done(("vv", j, 3)))
                ve.tensor_reduce(ssum[:, :, :], sqk[:, :, :].rearrange("p l (a d) -> p l a d", d=AD), X, ALU.add).then_inc(ssum_r, 1)
                own()
                for l in range(4):
                    st(ve.tensor_tensor(prod[:, l * 768:(l + 1) * 768].rearrange("p (m n) -> p m n", m=4),
                                        Q[:, l:l + 1, 0:D].to_broadcast([QT, 4, D]), Q[:, :, D:2 * D], ALU.mult))
                own()
                st(ve.tensor_reduce(lg[:, :, :, :].rearrange("p l m h -> p (l m h)"), prod.rearrange("p (a d) -> p a d", d=AD), X, ALU.add))
                ve.wait_ge(snorm, j + 1)
                st(ve.tensor_scalar(ssum[:, :, :], ssum[:, :, :], 1e-12, None, ALU.max))
                own()
                st(ve.reciprocal(ssum[:, :, :], ssum[:, :, :]))
                own()
                ve.wait_ge(lsexp, 1)
                st(ve.tensor_tensor(ssum[:, :, 0:AH], ssum[:, :, 0:AH], lsc[:, :].unsqueeze(1).to_broadcast([QT, 4, AH]), ALU.mult))
                own()
                st(ve.tensor_tensor(lg[:, :, :, :], lg[:, :, :, :], ssum[:, :, 0:AH].unsqueeze(2).to_broadcast([QT, 4, 4, AH]), ALU.mult))
                own()
                st(ve.tensor_tensor(lg[:, :, :, :], lg[:, :, :, :], ssum[:, :, AH:24].unsqueeze(1).to_broadcast([QT, 4, 4, AH]), ALU.mult))
                own()
                st(ve.tensor_reduce(lmx[:, :, :], lg[:, :, :, :].rearrange("p l m h -> p l h m"), X, ALU.max))
                own()
                ve.tensor_tensor(lg[:, :, :, :], lg[:, :, :, :], lmx[:, :, :].unsqueeze(2).to_broadcast([QT, 4, 4, AH]), ALU.subtract).then_inc(lexp_in, 1)
                ve.wait_ge(lexp, j + 1)
                st(ve.tensor_reduce(lmx[:, :, :], lg[:, :, :, :].rearrange("p l m h -> p l h m"), X, ALU.add))
                own()
                st(ve.reciprocal(lmx[:, :, :], lmx[:, :, :]))
                own()
                st(ve.tensor_tensor(lmx[:, :, :], lmx[:, :, :], hsc[:, :].unsqueeze(1).to_broadcast([QT, 4, AH]), ALU.mult))
                own()
                st(ve.tensor_tensor(lg[:, :, :, :], lg[:, :, :, :], lmx[:, :, :].unsqueeze(2).to_broadcast([QT, 4, 4, AH]), ALU.mult))
                own()
                for l in range(4):
                    st(ve.tensor_tensor(prod[:, l * 768:(l + 1) * 768].rearrange("p (m h d) -> p m h d", m=4, h=AH),
                                        lg[:, l, :, :].unsqueeze(3).to_broadcast([QT, 4, AH, AD]),
                                        Q[:, :, 2 * D:3 * D].rearrange("p m (h d) -> p m h d", h=AH), ALU.mult))
                own()
                ve.tensor_reduce(o1[:, j, :, :], prod.rearrange("p (l m n) -> p l n m", l=4, m=4), X, ALU.add).then_inc(o_ready, 1)
                ve.wait_ge(o_ready, j + 1)

            def residual(name, to):
                for t in range(NT):
                    ps = full((name, t))
                    ve.tensor_tensor(to[:, t, :], ps[0:TT, 0:D], to[:, t, :], ALU.add).then_inc(emptied_v, 1)
                ve.wait_ge(*ring.done((name, NT - 1)))
            residual("op", h)
            layernorm(5, h, h2)
            layernorm(6, h2, xn)
            st(ve.memset(v17[:, :, :, 16:17], 1.0))
            own()
            with ve.Fori(0, B) as b:
                ps = full("v2", b)
                ve.tensor_copy(v17[:, :, :, 0:AD], ps[0:QT, 0:2 * D].rearrange("p (j h d) -> p j h d", j=2, h=AH)).then_inc(emptied_v, 1)
                ve.wait_ge(*ring.done("v2", b))
                ve.memset(v17[0:1, 1, :, :], 0.0).then_inc(v2z, 1)
                for g in range(4):
                    ps = full(("SA", g), b)
                    s0 = ps[0:QT, 0:285].rearrange("p (m n) -> p m n", m=3)
                    s1 = ps[0:QT, 285:474].rearrange("p (m n) -> p m n", m=1)
                    ve.tensor_reduce(mx0[:, g, :], s0, X, ALU.max)
                    ve.tensor_reduce(mx1[:, g, 2:3], s1, X, ALU.max).then_inc(v_set, 1)
                    ve.wait_ge(v_set, 8 * b + 2 * g + 1)
                    ve.tensor_tensor(P0[:, g, :, :], s0, bc(mx0[:, g, :], [QT, 3, QT]), ALU.subtract)
                    ve.tensor_tensor(P1[:, g, 2:3, :], s1, bc(mx1[:, g, 2:3], [QT, 1, N]), ALU.subtract).then_inc(emptied_v, 1)
                    ps = full(("SB", g), b)
                    s1 = ps[0:QT, 0:378].rearrange("p (m n) -> p m n", m=2)
                    ve.tensor_reduce(mx1[:, g, 0:2], s1, X, ALU.max).then_inc(v_set, 1)
                    ve.wait_ge(v_set, 8 * b + 2 * g + 2)
                    ve.tensor_tensor(P1[:, g, 0:2, :], s1, bc(mx1[:, g, 0:2], [QT, 2, N]), ALU.subtract).then_inc(emptied_v, 1)
                for j in range(2):
                    ps = full(("yy", j), b)
                    yv = ps[0:QT, 0:204].rearrange("p (h n) -> p h n", h=AH)
                    ve.reciprocal(yrc[:, j, :], yv[:, :, AD]).then_inc(h_done, 1)
                    ve.wait_ge(h_done, 2 * b + j + 1)
                    ve.tensor_tensor(ysb[:, j, :].rearrange("p (h d) -> p h d", h=AH), yv[:, :, 0:AD],
                                     bc(yrc[:, j, :], [QT, AH, AD]), ALU.mult).then_inc(emptied_v, 1)
            residual("cp", h2)
            layernorm(7, h2, xn)
            ve.wait_ge(xn_ready, 5 * NT)
            st(ve.tensor_copy(xs[:, 0, :, :], xn[:, :, :]))
            own()
            st(ve.tensor_tensor(h1[:, :, :], xn[:, :, :], xs[:, 0, :, :], ALU.subtract))
            own()
            st(ve.tensor_copy(xs[:, 1, :, :], h1[:, :, :]))
            own()
            st(ve.tensor_tensor(h1[:, :, :], h1[:, :, :], xs[:, 1, :, :], ALU.subtract))
            own()
            ve.tensor_copy(xs[:, 2, :, :], h1[:, :, :]).then_inc(xs_r, 1)
            ps = full("mr")
            ve.tensor_copy(pv[:, :, :], ps[0:TT, 0:48].rearrange("p (t n) -> p t n", t=NT)).then_inc(emptied_v, 1)
            ve.wait_ge(*ring.done("mr"))
            top_two(pv[:, :, :])
            ve.tensor_scalar(sel[:, :, :], sel[:, :, :], 1.5, None, ALU.is_lt).then_inc(sel_r, 1)
            st(ve.tensor_reduce(red[:, :], pv[:, :, :], X, ALU.max))
            own()
            ve.tensor_tensor(pv[:, :, :], pv[:, :, :], bc(red[:, :], [TT, NT, 8]), ALU.subtract).then_inc(mlg, 1)
            ve.wait_ge(mexp, 1)
            ve.wait_ge(sel_r, 1)
            st(ve.tensor_tensor(pv[:, :, :], pv[:, :, :], sel[:, :, :], ALU.mult))
            own()
            st(ve.tensor_reduce(gsum[:, :], pv[:, :, :], X, ALU.add))
            own()
            st(ve.reciprocal(gsum[:, :], gsum[:, :]))
            own()
            st(ve.tensor_tensor(cw[:, :, 0:8], pv[:, :, :], bc(gsum[:, :], [TT, NT, 8]), ALU.mult))
            st(ve.memset(key[:, :, 8:10], 1000.0))
            ps = full("cs")
            ve.scalar_tensor_tensor(key[:, :, 0:8], sel[:, :, :], -1000.0, ps[0:TT, 0:48].rearrange("p (t n) -> p t n", t=NT),
                                    ALU.mult, ALU.add).then_inc(emptied_v, 1)
            ve.wait_ge(*ring.done("cs"))
            st(ve.tensor_scalar(key[:, :, 0:8], key[:, :, 0:8], 1000.0, None, ALU.add))
            own()

            def one_hot(s, e):
                for t in range(NT):
                    it = ve.tensor_scalar(oh[:, s, t, :], iota[:, :], key[:, t, bass.ds(e, 1)], None, ALU.is_equal)
                it.then_inc(oh_r, 1)
            for s in range(2):
                one_hot(s, s)
            ve.wait_ge(hb, 2 * NT)
            with ve.Fori(0, ME // 2) as i:
                for s in range(2):
                    ps = full(("d", s), i)
                    for k in range(2):
                        it = ve.tensor_scalar(xe[:, s, k, :], ps[0:DH, k * CAP:(k + 1) * CAP], flnw[:, 1, k:k + 1], None, ALU.mult)
                    it.then_inc(emptied_v, 1)
                for s in range(2):
                    ve.wait_ge(*ring.full(("T", s, 1), i))
                    one_hot(s, 2 * i + 2 + s)
                for s in range(2):
                    ps = full(("pj", s), i)
                    ve.tensor_copy(eo[:, s, :, :], ps[0:CT, 0:2 * D].rearrange("p (c d) -> p c d", c=2)).then_inc(emptied_v, 1)
                for s in range(2):
                    ve.wait_ge(*ring.done(("cb", 1 - s, 4), i, back=1 - s))
                    for z, tiles in enumerate(CB):
                        ps = full(("cb", s, z), i)
                        for q, t in enumerate(tiles):
                            it = ve.scalar_tensor_tensor(h[:, t, :], ps[0:TT, q * D:(q + 1) * D], cw[:, t, bass.ds(2 * i + s, 1)],
                                                         h[:, t, :], ALU.mult, ALU.add)
                        it.then_inc(emptied_v, 1)
            ve.wait_ge(*ring.done(("cb", 1, 4), ME // 2 - 1))
            ve.memset(red[:, :], 0.0).then_inc(hh, 2)

        @block.gpsimd
        def _(po):
            po.wait_ge(*loaded("b0"))
            po.wait_ge(*ring.full(("ln0", 2)))
            for t in range(NT):
                po.tensor_tensor(xn[:, t, :], xn[:, t, :], outb[:, :], ALU.add).then_inc(xob, 1)
            for t in range(NT):
                po.wait_ge(*ring.done(("rs", t)))
                po.tensor_tensor(h[:, t, :], h[:, t, :], h2[:, t, :], ALU.add).then_inc(hb, 1)
            for t in range(NT):
                po.wait_ge(*ring.done(("cp", t)))
                po.tensor_tensor(h[:, t, :], h[:, t, :], h2[:, t, :], ALU.add).then_inc(hb, 1)


def lay_out(x, n):
    import numpy as np
    a = {}

    def put(name, v):
        v = np.ascontiguousarray(v)
        a[name] = v.astype(np.float32) if v.dtype == np.float64 else v

    def rows(w, p):
        return w.reshape(w.shape[0] // p, p, *w.shape[1:]).swapaxes(0, 1)

    for s, key, w, p in ((8, "8", "W0", DH), (16, "16", "W1", 128), (32, "32", "W2", 128)):
        g = IMG // s
        v = x.reshape(B, g, s, g, s, C).transpose(2, 4, 5, 0, 1, 3).reshape(s * s * C, B * g * g)
        put("p" + key, rows(v, p))
        put("w" + key, rows(n["L0_tok_" + w], p))
    put("tokb", np.stack([n[f"L0_tok_b{i}"].reshape(2, DH) for i in range(3)], -1).transpose(1, 0, 2))
    put("ident", np.eye(128, dtype=np.float32))
    put("identb", np.eye(128, dtype=np.float32).astype(mybir.dt.np(BF16)))
    put("bones", np.kron(np.eye(2), np.ones((64, 64))).astype(np.float32))
    put("hones", np.kron(np.eye(2), np.ones((64, 1))).astype(np.float32))
    put("ones", np.ones((128, 1), np.float32))
    put("sgn", np.tile(np.repeat([1.0, -1.0], 32), 2)[:, None].astype(np.float32))
    put("sg4", np.repeat([1.0, 1.0, 1.0, -1.0], 32)[:, None].astype(np.float32))
    l0 = lambda k: n["L0_attn_" + k]
    mr, mi = (l0(k).reshape(4, 2, 64, 32).transpose(1, 3, 0, 2) for k in ("m_real", "m_imag"))
    put("m_re", np.stack([mr, mi], 1).reshape(128, 4, 64))
    put("m_im", np.stack([mi, mr], 1).reshape(128, 4, 64))
    pr, pi, cr, ci = (l0(k).T for k in ("P_real", "P_imag", "C_real", "C_imag"))
    put("pc", np.stack([np.stack([np.concatenate([pr, pi]), np.concatenate([cr, ci])], 1),
                        np.stack([np.concatenate([pi, pr]), np.concatenate([ci, cr])], 1)], 1))
    w = np.stack([l0("W_real"), l0("W_imag")], 1)
    put("wp", rows(w.transpose(2, 0, 1, 3).reshape(D, 512), DH))
    put("pw1", rows(l0("pw1").transpose(2, 0, 1).reshape(D, 128), DH))
    put("pb1", l0("pb1").reshape(128, 1))
    pw2 = np.zeros((8, 16, 8), np.float32)
    for j in range(8):
        pw2[j, :, j] = l0("pw2")[j]
    put("pw2", pw2.reshape(128, 8))
    put("valT", rows(l0("values").transpose(2, 0, 1).reshape(D, 512), DH))
    put("owT", rows(l0("out_w").T, DH))
    put("gwT", rows(l0("gate_w").reshape(8, 8, D).transpose(2, 1, 0).reshape(D, 64), DH).reshape(DH, 2, 4, 16))
    put("pb2", l0("pb2")); put("gateb", l0("gate_b")); put("outb", l0("out_b")); put("beta", l0("beta").reshape(1))
    put("rob", l0("r_out_b")); put("rb2", l0("rb2"))
    put("encT", rows(np.concatenate([l0("enc_r_w"), l0("enc_i_w")]).T, DH))
    wr, wi = l0("r_out_w").T[:32], l0("r_out_w").T[32:]
    put("roW", np.concatenate([wr, wr, wi, wi]))
    il = np.zeros((2, TT), np.float32); il[0, :N - TT] = 1; il[1, N - TT:] = 1
    ir = np.zeros((2, HALF), np.float32); ir[0, N:] = NEG; ir[1, :N] = NEG
    put("imgL", il); put("imgR", ir)
    put("rw1", rows(l0("rw1").T, DH)); put("rb1", l0("rb1").reshape(1, 16)); put("rw2", l0("rw2").T)
    put("ew1", rows(l0("ew1").transpose(2, 0, 1).reshape(D, 576), DH)); put("eb1", l0("eb1").reshape(1, 576))
    put("egb", np.stack([l0("eg").reshape(6, DH), l0("ebt").reshape(6, DH)], -1).transpose(1, 0, 2))
    put("ew2", rows(l0("ew2").transpose(0, 2, 1).reshape(576, D), DH)); put("eb2", l0("eb2").reshape(1, 3, D))
    f = lambda k: n["L0_ffn_" + k]
    put("rwt", rows(f("router_w"), DH)); put("rbias", f("routing_bias"))
    put("tri8", (np.arange(8)[None, :] < np.arange(8)[:, None]).astype(np.float32).reshape(64))
    gu = np.stack([np.concatenate([f("rw_" + k), f("sw_" + k)[None]]) for k in ("gate", "up")], 2)
    put("fgu", gu.reshape(FE, 2, DH, 2 * FI).swapaxes(1, 2).reshape(FE, DH, 4 * FI))
    dn = np.concatenate([f("rw_down"), f("sw_down")[None]])
    put("fdn", dn.reshape(FE, 3, 128, D).swapaxes(1, 2).reshape(FE, 128, 3 * D))
    l1 = lambda k: n["L1_attn_" + k]
    put("wqkv", rows(l1("in_proj_weight").T, DH)); put("bqkv", l1("in_proj_bias").reshape(1, 3 * D))
    put("ow1", rows(l1("out_w").T, DH)); put("ob1", l1("out_b").reshape(1, D))
    put("lsc", l1("logit_scale").reshape(AH)); put("hsc", l1("head_scale").reshape(AH))
    c = lambda k: n["L1_ffn_" + k]
    put("flnw", np.stack([c("ln1_w").reshape(2, DH), c("ln2_w").reshape(2, DH)], 1).transpose(2, 1, 0))
    w = c("c_attn_w").T
    pad = np.zeros((D, 2, 3, 4, 32), np.float32)
    pad[..., :AD] = w[:, :2 * D].reshape(D, 2, 3, 4, AD)
    put("wq2", rows(pad.reshape(D, 768), DH)); put("wv2", rows(w[:, 2 * D:], DH)); put("cpw", rows(c("c_proj_w").T, DH))
    q0, q1 = np.arange(QT)[:, None], np.arange(N - QT, N)[:, None]
    m0 = np.where(np.arange(QT)[None] <= q0, 0.0, NEG)
    m1 = np.where(np.arange(N)[None] <= q1, 0.0, NEG)
    put("maskA", np.concatenate([m0, m0, m0, m1], 1).astype(mybir.dt.np(BF16)))
    put("maskB", np.concatenate([m1, m1], 1).astype(mybir.dt.np(BF16)))
    put("wg", rows(c("w_g").T, DH))
    put("tri", (np.arange(TT)[:, None] < np.arange(TT)[None]).astype(np.float32)); put("tones", np.ones((TT, TT), np.float32))
    put("iota", np.arange(CAP, dtype=np.float32))
    put("mfc", c("c_fc").reshape(ME, 2, DH, MI).swapaxes(1, 2).reshape(ME, DH, 2 * MI))
    put("mpj", c("c_proj_e").reshape(ME, 6, 128, D).swapaxes(1, 2).reshape(ME, 128, 6 * D))
    return a


def kernel(**inputs):
    import numpy as np
    import concourse.bacc as bacc
    from concourse.bass_utils import run_bass_kernel_spmd as run

    n = {k: np.asarray(v) for k, v in inputs.items()}
    arrays = lay_out(n.pop("x"), n)
    nc = bacc.Bacc("TRN2", target_bir_lowering=False, num_devices=1)
    aps = {k: nc.dram_tensor("in_" + k, v.shape, mybir.dt.from_np(v.dtype), kind="ExternalInput").ap() for k, v in arrays.items()}
    out = nc.dram_tensor("out", (B, N, D), F32, kind="ExternalOutput").ap()
    vit_tower(nc, aps, out)
    r = run(nc, [{"in_" + k: v for k, v in arrays.items()}], core_ids=[0])
    return r.results[0]["out"]
```

```python
from contextlib import ExitStack

import concourse.bass as bass
from concourse import mybir

F32 = mybir.dt.float32
F32R = mybir.dt.float32r
BF16 = mybir.dt.bfloat16
ACT = mybir.ActivationFunctionType
ALU = mybir.AluOpType
X = mybir.AxisListType.X

B, IMG, C, D = 4, 96, 3, 192
SIDES = (8, 16, 32)
PATCHES = [(IMG // s) ** 2 for s in SIDES]
N = sum(PATCHES)
T = B * N
HALF = T // 2
TT = 126
NT = T // TT
DH = D // 2
S0H, S0D, S0S = 8, 32, 64
K0 = 3
FE, FI = 8, 384
AH, AD = 12, 16
ME, MI = 8, 768
CAP = 190
CT = CAP // 2
QT = 95
BANKS = 8
BANK = 512
EPS = 1e-5
NEG = -1.0e30


class Ring:

    def __init__(self, bank_full, emptied):
        self.bank_full, self.emptied = bank_full, emptied
        self.n = 0
        self.count = {k: 0 for k in emptied}
        self.at = {}
        self.order = []
        self.loops, self.bodies, self.before = {}, {}, {}

    def add(self, fills, times=1):
        first, base = self.n, dict(self.count)
        for key, eng in fills:
            self.count[eng] += 1
            self.at[key] = [self.n, eng, self.count[eng], len(fills) if times > 1 else 0, 0]
            self.order.append(key)
            self.n += 1
        if times > 1:
            assert len(fills) % BANKS == 0
            for z, (key, eng) in enumerate(fills):
                self.loops[key], self.bodies[key], self.before[key] = z, [f[0] for f in fills], base
                self.at[key][4] = self.count[eng] - base[eng]
            for eng in self.count:
                self.count[eng] += (times - 1) * (self.count[eng] - base[eng])
            self.n = first + times * len(fills)
            self.order += [fills[j][0] for j in range(len(fills))] * (times - 1)

    def bank(self, key):
        return self.at[key][0] % BANKS

    def full(self, key, i=0, back=0):
        pos, _, _, stride, _ = self.at[key]
        pos -= back * stride
        return self.bank_full, i * stride + (pos + 1) if stride else pos + 1

    def done(self, key, i=0, back=0):
        _, eng, nth, length, stride = self.at[key]
        nth -= back * stride
        assert nth > 0
        return self.emptied[eng], i * stride + nth if length else nth

    def free(self, key, i=0):
        pos, _, _, length, _ = self.at[key]
        if pos < BANKS:
            return None
        if length:
            offset = self.loops[key]
            body = self.bodies[key]
            if offset >= BANKS:
                return self.done(body[offset - BANKS], i)
            return self.done(body[offset - BANKS], i, back=1)
        before = self.order[pos - BANKS]
        own, inside = self.at[before][0], self.at[before][3]
        return self.done(before, (pos - BANKS - own) // inside if inside else 0)

    def all_done(self, key):
        return [(self.emptied[e], n) for e, n in self.before[key].items() if n]


def vit_tower(nc, a, out):
    with ExitStack() as ctx:
        def sb(name, shape, dt=F32):
            return ctx.enter_context(nc.sbuf_tensor(name, shape, dt))

        def sem(name):
            return ctx.enter_context(nc.semaphore(name))

        psum = [ctx.enter_context(nc.psum_tensor(f"bank{i}", [128, BANK], F32)) for i in range(BANKS)]
        bank_full, emptied_v, emptied_s = sem("bank_full"), sem("emptied_v"), sem("emptied_s")
        ring = Ring(bank_full, {"v": emptied_v, "s": emptied_s})
        v_step = sem("v_step")

        ALL_LOADS = {}

        def loaded(name):
            if name not in ALL_LOADS:
                ALL_LOADS[name] = sem("ld_" + name)
            return ALL_LOADS[name], 16 * LOADS[name]

        ident = sb("ident", [128, 128])
        identb = sb("identb", [128, 128], BF16)
        bones = sb("bones", [128, 128])
        sgn = sb("sgn", [128, 1])
        big4 = sb("big4", [128, 6 * T])
        p8 = big4[0:DH, 0:1152].rearrange("p (k n) -> p k n", k=2)
        w8 = big4[0:DH, 1152:1536].rearrange("p (k n) -> p k n", k=2)
        p16 = big4[:, 1536:2400].rearrange("p (k n) -> p k n", k=6)
        w16 = big4[:, 2400:3552].rearrange("p (k n) -> p k n", k=6)
        gT = big4[0:DH + 1, :].rearrange("p (c t) -> p c t", c=6)
        raw1 = sb("raw1", [128, 2 * 1536]); raw2 = sb("raw2", [128, 2, 1152])
        rawf = raw1[:, 0:3 * 768].rearrange("p (c n) -> p c n", c=3)
        xS = sb("xS", [128, 3, T], F32R)
        wA = sb("wA", [128, 3, 768], F32R); wB = sb("wB", [128, 2, 768], F32R)
        tokb = sb("tokb", [DH, 2, 3])
        e32 = sb("e32", [B * 9, D])
        h = sb("h", [TT, NT, D])
        xn = sb("xn", [TT, NT, D])
        xT = sb("xT", [DH + 1, 2, T])
        bn = sb("bn", [TT, 18, 6]); mv = sb("mv", [TT, 18, 2]); rstd = sb("rstd", [TT, 18])
        flnw = sb("flnw", [DH, 2, 2])
        rwt = sb("rwt", [DH, 2, 7]); rbias = sb("rbias", [TT, 7]); tri8 = sb("tri8", [TT, 64])
        pv = sb("pv", [TT, NT, 8]); sel = sb("sel", [TT, NT, 8]); cw = sb("cw", [TT, NT, 10])
        wqq = sb("wqq", [DH + 1, 1536]); ow1 = sb("ow1", [DH + 1, 2, D])
        lsc = sb("lsc", [QT, AH]); hsc = sb("hsc", [QT, AH])
        ssum2 = sb("ssum2", [QT, 2, 4, 24]); lg2 = sb("lg2", [QT, 2, 4, 4, AH]); lmx2 = sb("lmx2", [QT, 2, 4, AH])
        wv2 = sb("wv2", [DH, 2, D]); cpw = sb("cpw", [112, 3, D])
        xb = sb("xb", [DH, 2, 2, N])
        mx = sb("mx", [QT, 2, 4, 6]); psums = sb("psums", [QT, 2, 4, 6])
        maskA = sb("maskA", [QT, 474], BF16); maskB = sb("maskB", [QT, 378], BF16)
        wg = sb("wg", [DH, 2, ME]); tri = sb("tri", [TT, TT], BF16); tones = sb("tones", [TT, TT], BF16)
        selb = sb("selb", [TT, NT, 8], BF16)
        iota = sb("iota", [TT, CAP]); key = sb("key", [TT, NT, 10])
        valT = sb("valT", [DH, 2, 512]); wp = sb("wp", [DH, 2, 512])
        ew1 = sb("ew1", [DH + 1, 2, 576]); ew2 = sb("ew2", [DH + 1, 6, D])
        pw1 = sb("pw1", [DH, 2, 128]); pb1 = sb("pb1", [128, 1])
        pw2 = sb("pw2", [128, 8]); pb2 = sb("pb2", [TT, 8]); hones = sb("hones", [128, 2])
        mT = sb("mT", [128, 2, 4, 64])
        pc = sb("pc", [64, 2, 2, 32]); gg = sb("gg", [64, 2, 32]); gsb = sb("gsb", [64, 64])
        enU = sb("enU", [64, 2, 128]); utmp = sb("utmp", [64, 2, 32])
        owT = sb("owT", [DH, 2, D]); gwT = sb("gwT", [DH, 2, 4, 16])
        vp = sb("vp", [128, 4, D]); gm = sb("gm", [128, 4, 8])
        gateb = sb("gateb", [TT, 8]); outb = sb("outb", [TT, D])
        beta = sb("beta", [TT, 1])
        big1 = sb("big1", [128, 4 * T])
        prT = big1[:, :].rearrange("p (j t) -> p j t", j=4)
        big2 = sb("big2", [128, 4 * T])
        sqT = big2[:, :].rearrange("p (j t) -> p j t", j=4)
        pn = sb("pn", [TT, NT, 16]); pp = sb("pp", [TT, NT, 8]); pa = sb("pa", [TT, NT, 8]); rr = sb("rr", [TT, NT, 8])
        ptok = sb("ptok", [TT, NT]); vtok = sb("vtok", [TT, NT]); vB = sb("vB", [TT, T])
        ovs = sb("ovs", [TT, 2304])
        ov2 = ovs[:, 0:2048].rearrange("p (a b n) -> p a b n", a=2, b=8)
        big3 = sb("big3", [128, NT * 576])
        att = big3[0:TT, 0:NT * 512].rearrange("p (t n) -> p t n", t=NT)
        x1 = big3[0:TT, :].rearrange("p (t n) -> p t n", t=NT)
        gts = sb("gts", [TT, NT, 8]); red = sb("red", [TT, NT]); gsum = sb("gsum", [TT, NT])
        h1 = sb("h1", [TT, NT, D]); h2 = sb("h2", [TT, NT, D])
        h1T = sb("h1T", [DH + 1, 2, T])
        encT = sb("encT", [DH, 2, 64])
        roW = sb("roW", [128, D]); rob = sb("rob", [TT, D]); ones = sb("ones", [128, 1]); sg4 = sb("sg4", [128, 1])
        imgL = sb("imgL", [2, TT]); imgR = sb("imgR", [2, HALF])
        nmax = sb("nmax", [TT, NT]); esum = sb("esum", [TT, NT]); ex = sb("ex", [TT, 2, HALF]); nei = sb("nei", [TT, NT])
        sc1 = sb("sc1", [TT, NT]); sc2 = sb("sc2", [TT, NT]); nq = sb("nq", [TT, NT])
        rw1 = sb("rw1", [DH + 1, 2, 16]); r1T = sb("r1T", [16, T]); rw2 = sb("rw2", [16, 3]); rb2 = sb("rb2", [TT, 3])
        rg = sb("rg", [TT, NT, 3])
        egb = sb("egb", [DH, 6, 2])

        h2T = h1T
        aT = [b[:, 0:3 * T].rearrange("p (m t) -> p m t", m=3) for b in (big1, big2)]
        sg = big3[:, 0:6 * HALF].rearrange("p (z t) -> p z t", z=6)
        qkv = [b[0:QT, 0:4 * 3 * D].rearrange("p (l n) -> p l n", l=4) for b in (big1, big2)]
        prod = [b[0:QT, 0:3072] for b in (big3, big4)]
        P1 = [b[0:QT, 0:12 * N].rearrange("p (g m n) -> p g m n", g=4, m=3) for b in (big1, big2)]
        P0 = [b.rearrange("p a n -> p (a n)")[0:QT, 0:12 * QT].rearrange("p (g m n) -> p g m n", g=4, m=3)
              for b in (ew1[:, :, :], ew2[:, :, :])]
        qk = [ovs[:, s * 1134:(s + 1) * 1134].rearrange("p (z n) -> p z n", z=6) for s in range(2)]
        PT = [b[0:QT, 0:36 * QT].rearrange("p (z n) -> p z n", z=36) for b in (big3, big4)]
        v32 = [b.rearrange("p a n -> p (a n)")[0:QT, 0:768].rearrange("p (j h n) -> p j h n", j=2, h=AH)
               for b in (valT[:, :, :], wp[:, :, :])]
        yT = [big1[0:112, 12 * N:12 * N + T], big2[0:112, 12 * N:12 * N + T], vB[0:112, :]]
        ohT = big1[0:CT, 0:4 * T].rearrange("p (s c t) -> p s c t", s=2, c=2)
        heT = big2[:, 0:12 * CAP].rearrange("p (s m c) -> p s m c", s=2, m=6)
        b3b = big3[0:TT, :].bitcast(BF16)
        xs = b3b[:, 0:3 * NT * D].rearrange("p (z t d) -> p z t d", z=3, t=NT)
        oh = b3b[:, 3 * NT * D:3 * NT * D + 2 * NT * CAP].rearrange("p (s t c) -> p s t c", s=2, t=NT)
        o1 = [b.rearrange("p t n -> p (t n)")[0:QT, 0:4 * D].rearrange("p (l n) -> p l n", l=4) for b in (h1[:, :, :], h2[:, :, :])]
        sqk0 = ovs[0:QT, 0:8 * D].rearrange("p (l n) -> p l n", l=4)
        sqk = [[sqk0[:, l, :] for l in range(4)],
               [b.rearrange("p a n -> p (a n)")[0:QT, z * 2 * D:(z + 1) * 2 * D] for b in (valT[:, :, :], wp[:, :, :]) for z in range(2)]]
        wqkv = wqq[:, 0:6 * D].rearrange("p (k n) -> p k n", k=2)
        wq2 = wqq[0:DH, :].rearrange("p (k n) -> p k n", k=2)
        zT, qT0, qsq, uu = (big4[0:r, z * T:(z + 1) * T] for z, r in enumerate((128, 64, 64, 128)))
        msq, mi = big3[:, 1000:1320], big3[:, 1320:1640]
        p32 = big3[:, 0:24 * 36].rearrange("p (k n) -> p k n", k=24)
        w32 = [b[:, 0:12 * D].rearrange("p (k n) -> p k n", k=12) for b in (big1, big2)]
        cat = big3[0:TT, 0:12 * D * NT // 6].rearrange("p (t n) -> p t n", t=NT)
        xe = big4[0:DH, 1536:1536 + 4 * CAP].rearrange("p (s k c) -> p s k c", s=2, k=2)
        eo = big4[0:CT, 2304:2304 + 4 * D].rearrange("p (s c d) -> p s c d", s=2, c=2)
        cmp = big4[0:TT, 3072:3072 + 128 * NT].rearrange("p (z t n) -> p z t n", z=2, t=NT)
        vrep = ex[:, :, :].rearrange("p a b -> p (a b)").rearrange("p (t n) -> p t n", t=NT)
        SQ = float(D) ** -0.5

        LOADS = dict(route=3, qkv=4, l1=4, wq2=1, caus=5, moe=5, mask=2, const=5, tok8=3, tok16=2, tok32=3, m=3, val=3, wp=4, small=6, b0=7, enc=3, ew1=2, ew2=3)

        LN = lambda name: [((name, g), "s") for g in range(NT // 2)]
        ring.add([(("emb", u, m), "s") for u in range(2) for m in range(2)])
        ring.add([(("e16", m), "s") for m in range(2)])
        ring.add([("norms", "s"), ("g", "v")])
        ring.add([(("vp", c), "v") for c in range(4)])
        ring.add([("e32", "s"), ("e32T", "s")])
        ring.add([(("h0", t), "v") for t in range(NT)])
        ring.add(LN("ln0"))
        ring.add([(("z", u), "s") for u in range(2)])
        ring.add([(("pr", j, u), "v") for j in range(4) for u in range(2)])
        ring.add([("pn", "v")])
        ring.add([(("ov", t, q), "s") for t in range(NT) for q in range(2)])
        ring.add([(("vb", u), "s") for u in range(2)])
        ring.add([(("aT", t), "s") for t in range(NT)])
        ring.add([("gl", "v")])
        ring.add([(("agT", t), "s") for t in range(NT)])
        ring.add([(("h1", t), "v") for t in range(NT)])
        ring.add(LN("h1T"))
        ring.add([(("enc", u), "s") for u in range(2)])
        ring.add([("nq", "v")])
        ring.add([((n, u), e) for u in range(2) for n, e in (("u1", "s"), ("u2", "v"))])
        ring.add([(("S", t), "s") for t in range(NT)])
        ring.add([(("rs", t), "v") for t in range(NT)])
        ring.add(LN("h2T"))
        ring.add([(("r1", u), "s") for u in range(2)])
        ring.add([("rl", "v")])
        ring.add([(("e1", t, q), "s") for t in range(NT) for q in range(2)])
        ring.add([(("e1T", u, c), "s") for u in range(2) for c in range(6)])
        ring.add([(("y", t, q), "v") for t in range(NT) for q in range(2)])

        DN = [(0, 1), (2, 3), (4,), (5,)]
        CB = [(0, 1), (2,), (3,), (4,), (5,)]
        ring.add(LN("ln1"))
        ring.add([("rt", "v")])
        ring.add([(("xs", t), "s") for t in range(NT)])
        ring.add([f for s in range(2) for f in
                  [((n, s, u, m), e) for u in range(2) for m in range(3) for n, e in (("g", "s"), ("u", "v"))]
                  + [(("dn", s, z), "v") for z in range(4)]], times=FE // 2)
        ring.add(LN("ln2"))
        ring.add([((n, j, l), e) for j in range(2) for l in range(4) for n, e in (("qk", "s"), ("vv", "s"))])
        ring.add([(("oT", j, l), "s") for j in range(2) for l in range(4)])
        ring.add([(("op", t), "v") for t in range(NT)])
        ring.add(LN("ln3"))
        ring.add([f for s in range(2) for f in [(("q2", s, z), "s") for z in range(3)] + [(("v2", s, j), "v") for j in range(2)]]
                 + [((n, s, g), "s") for s in range(2) for g in range(4) for n in ("SA", "SB")]
                 + [(("PT", s, z), "vs"[z % 2]) for s in range(2) for z in range(8)]
                 + [(("yu", s, m), "v") for s in range(2) for m in range(3)], times=B // 2)
        ring.add([(("cp", t), "v") for t in range(NT)])
        ring.add(LN("ln4"))
        ring.add([("mr", "v"), ("cs", "v")])
        ring.add([(("d", s), "v") for s in range(2)] + [(("T", s, c), "s") for s in range(2) for c in range(2)]
                 + [(("fc", s, z), "s") for s in range(2) for z in range(3)] + [(("pj", s), "v") for s in range(2)]
                 + [(("cb", s, z), "v") for s in range(2) for z in range(5)], times=ME // 2)

        f_up = sem("f_up"); f_wh = sem("f_wh"); f_split = sem("f_split"); cat_r = sem("cat_r")
        f_down = [sem(f"f_down{s}") for s in range(2)]
        m_fc = [sem(f"m_fc{s}") for s in range(2)]; m_pj = [sem(f"m_pj{s}") for s in range(2)]
        rsig_in = sem("rsig_in"); rsig = sem("rsig"); sqk_r = sem("sqk_r"); ssum_r = sem("ssum_r"); snorm = sem("snorm")
        lexp_in = sem("lexp_in"); lexp = sem("lexp"); lsexp_in = sem("lsexp_in"); lsexp = sem("lsexp"); o_ready = sem("o_ready")
        mx_r = sem("mx_r"); xb_r = sem("xb_r"); exp_r = sem("exp_r"); v_set = sem("v_set"); mlg = sem("mlg"); mexp = sem("mexp")
        sel_r = sem("sel_r"); xs_r = sem("xs_r"); oh_r = sem("oh_r"); v2z = sem("v2z")
        rsum = sem("rsum")
        pq = sem("pq"); pv_in = sem("pv_in"); pv_out = sem("pv_out")
        xn_ready = sem("xn_ready")
        var_ready = sem("var_ready")
        std_ready = sem("std_ready")
        prep = sem("prep")
        sq_ready = sem("sq_ready")
        plog = sem("plog"); psig = sem("psig"); vrow = sem("vrow"); att_w = sem("att_w"); att_g = sem("att_g")
        gexp = sem("gexp"); ovr = sem("ovr"); nm = sem("nm"); e_used = sem("e_used")
        xob = sem("xob"); ones_set = sem("ones_set"); hh = sem("hh"); hb = sem("hb")
        rlog = sem("rlog"); rexp = sem("rexp"); e1n = sem("e1n"); bsig = sem("bsig"); stored = sem("stored")

        block = ctx.enter_context(nc.Block())

        @block.sync
        def _(sp):
            def load(name, *pairs):
                s, n = loaded(name)
                assert len(pairs) * 16 == n, name
                for dst, src in pairs:
                    sp.dma_start(dst, src).then_inc(s, 16)

            load("tok8", (p8, a["p8"]), (w8, a["w8"]), (tokb[:, :, :], a["tokb"]))
            load("const", (ident[:, :], a["ident"]), (bones[:, :], a["bones"]), (sgn[:, :], a["sgn"]),
                 (hones[:, :], a["hones"]), (sg4[:, :], a["sg4"]))
            load("m", (mT[:, 0, :, :], a["m_re"]), (mT[:, 1, :, :], a["m_im"]), (pc[:, :, :, :], a["pc"]))
            load("tok16", (p16, a["p16"]), (w16, a["w16"]))
            load("val", (valT[:, :, :], a["valT"]), (owT[:, :, :], a["owT"]), (gwT[:, :, :, :], a["gwT"]))
            load("tok32", (p32, a["p32"]), (w32[0], a["w32"][:, 0:12, :]), (w32[1], a["w32"][:, 12:24, :]))
            load("wp", (wp[:, :, :], a["wp"]), (pw1[:, :, :], a["pw1"]), (pb1[:, :], a["pb1"]), (pw2[:, :], a["pw2"]))
            load("b0", (pb2[:, :], a["pb2"].partition_broadcast(TT)), (gateb[:, :], a["gateb"].partition_broadcast(TT)),
                 (outb[:, :], a["outb"].partition_broadcast(TT)), (beta[:, :], a["beta"].partition_broadcast(TT)),
                 (rob[:, :], a["rob"].partition_broadcast(TT)), (rb2[:, :], a["rb2"].partition_broadcast(TT)),
                 (egb[:, :, :], a["egb"]))
            load("enc", (encT[:, :, :], a["encT"]), (roW[:, :], a["roW"]), (imgL[:, :], a["imgL"]))
            load("small", (imgR[:, :], a["imgR"]), (rw1[0:DH, :, :], a["rw1"]), (rw1[DH:DH + 1, 0, :], a["rb1"]), (rw2[:, :], a["rw2"]),
                 (identb[:, :], a["identb"]), (ones[:, :], a["ones"]))
            load("ew1", (ew1[0:DH, :, :], a["ew1"]), (ew1[DH:DH + 1, 0, :], a["eb1"]))
            load("ew2", (ew2[0:DH, :, :], a["ew2"]), (ew2[DH:DH + 1, 0:6:2, :], a["eb2"]), (ew2[DH:DH + 1, 1:6:2, :], a["eb2"]))
            load("route", (rwt[:, :, :], a["rwt"]), (rbias[:, :], a["rbias"].partition_broadcast(TT)),
                 (tri8[:, :], a["tri8"].partition_broadcast(TT)))

            def expert(dst, name, e, sem_):
                sp.dma_start(dst, a[name][bass.ds(e, 1), :, :].rearrange("o p n -> p (o n)")).then_inc(sem_, 16)

            def f_down_load(s, e):
                expert(raw2[:, s, 0:3 * D], "fdn", e, f_down[s])

            def m_load(s, layer, e):
                if layer == 0:
                    expert(raw1[0:DH, s * 1536:(s + 1) * 1536], "mfc", e, m_fc[s])
                else:
                    expert(raw2[:, s, :], "mpj", e, m_pj[s])

            expert(raw1[:, 0:3 * 768], "fgu", 0, f_up)
            for s in range(2):
                f_down_load(s, s)
            load("qkv", (wqkv[0:DH, :, :], a["wqkv"]), (wqkv[DH:DH + 1, 0, :], a["bqkv"]),
                 (ow1[0:DH, :, :], a["ow1"]), (ow1[DH:DH + 1, 0, :], a["ob1"]))
            load("l1", (lsc[:, :], a["lsc"].partition_broadcast(QT)), (hsc[:, :], a["hsc"].partition_broadcast(QT)),
                 (flnw[:, :, :], a["flnw"]), (wv2[:, :, :], a["wv2"]))
            load("mask", (maskA[:, :], a["maskA"]), (maskB[:, :], a["maskB"]))
            load("moe", (cpw[:, :, :], a["cpw"]), (wg[:, :, :], a["wg"]), (tri[:, :], a["tri"]), (tones[:, :], a["tones"]),
                 (iota[:, :], a["iota"].partition_broadcast(TT)))
            sp.wait_ge(f_split, 1)
            expert(raw1[:, 0:3 * 768], "fgu", 1, f_up)
            with sp.Fori(0, FE // 2 - 1) as i:
                for s in range(2):
                    sp.wait_ge(f_split, 2 * i + s + 2)
                    expert(raw1[:, 0:3 * 768], "fgu", 2 * i + s + 2, f_up)
                    sp.wait_ge(*ring.full(("dn", s, 3), i))
                    f_down_load(s, 2 * i + s + 2)
            sp.wait_ge(f_split, FE)
            for s in range(2):
                m_load(s, 0, s)
            for s in range(2):
                sp.wait_ge(*ring.full(("dn", s, 3), FE // 2 - 1))
                m_load(s, 1, s)
            sp.wait_ge(*ring.full(("vv", 1, 3)))
            load("wq2", (wq2, a["wq2"]))
            with sp.Fori(0, ME // 2 - 1) as i:
                for layer in range(2):
                    for s in range(2):
                        sp.wait_ge(*ring.full((("fc", s, 2), ("pj", s))[layer], i))
                        m_load(s, layer, 2 * i + 2 + s)
            sp.wait_ge(hh, 2)
            sp.dma_start(out.rearrange("b n d -> (b n) d").rearrange("(t p) d -> p t d", p=TT), h[:, :, :]).then_inc(stored, 16)
            sp.wait_ge(stored, 16)

        @block.tensor
        def _(te):
            def take(key, i=0):
                w = ring.free(key, i)
                if w:
                    te.wait_ge(*w)
                return psum[ring.bank(key)]

            def acc(o, pairs, first=True, last=True):
                for k, (l, r) in enumerate(pairs):
                    mm = te.matmul(o, l, r, start=first and k == 0, stop=last and k == len(pairs) - 1)
                return mm

            def tr_pairs(name, src, xn_base):
                for g in range(NT // 2):
                    ps = take((name, g))
                    for q in range(2):
                        t = 2 * g + q
                        te.wait_ge(xn_ready, xn_base + t + 1)
                        for k in range(2):
                            c0 = k * 252 + q * TT
                            mm = te.transpose(ps[0:DH, c0:c0 + TT], src[:, t, k * DH:(k + 1) * DH], ident[0:TT, 0:TT])
                    mm.then_inc(bank_full, 1)

            te.wait_ge(*loaded("tok8"))
            for u in range(2):
                for m in range(2):
                    acc(take(("emb", u, m))[0:DH, 0:288],
                        [(w8[:, k, m * DH:(m + 1) * DH], p8[:, k, 288 * u:288 * (u + 1)]) for k in range(2)]).then_inc(bank_full, 1)
            te.wait_ge(*loaded("tok16"))
            for m in range(2):
                acc(take(("e16", m))[0:DH, 0:B * 36], [(w16[:, k, m * DH:(m + 1) * DH], p16[:, k, :]) for k in range(6)]).then_inc(bank_full, 1)

            ps = take("norms")
            te.wait_ge(*loaded("const"))
            te.wait_ge(prep, 2)
            te.matmul(ps[:, 0:256], bones[:, :], msq[:, 0:256], start=True, stop=True)
            te.matmul(ps[0:64, 256:320], bones[0:64, 0:64], msq[0:64, 256:320], start=True, stop=True).then_inc(bank_full, 1)
            ps = take("g")
            te.wait_ge(prep, 4)
            te.matmul(ps[0:64, 0:64], bones[0:64, 0:64], gg[:, :, :], start=True, stop=True).then_inc(bank_full, 1)
            te.wait_ge(*loaded("val"))
            for c in range(4):
                ps = take(("vp", c))
                acc(ps[:, 0:D], [(valT[:, k, c * 128:(c + 1) * 128], owT[:, k, :]) for k in range(2)])
                acc(ps[:, D:D + 16], [(valT[:, k, c * 128:(c + 1) * 128], gwT[:, k, c, :]) for k in range(2)]).then_inc(bank_full, 1)

            te.wait_ge(*loaded("tok32"))
            acc(take("e32")[0:B * 9, 0:D], [(p32[:, k, :], w32[k // 12][:, k % 12, :]) for k in range(24)]).then_inc(bank_full, 1)
            ps = take("e32T")
            te.wait_ge(*ring.done("e32"))
            for k in range(2):
                mm = te.transpose(ps[0:DH, k * 36:(k + 1) * 36], e32[:, k * DH:(k + 1) * DH], ident[0:36, 0:36])
            mm.then_inc(bank_full, 1)
            te.wait_ge(*ring.done("e32T"))
            for t in range(NT):
                ps = take(("h0", t))
                for k in range(2):
                    mm = te.transpose(ps[0:TT, k * DH:(k + 1) * DH], xT[0:DH, k, t * TT:(t + 1) * TT], ident[0:DH, 0:DH])
                mm.then_inc(bank_full, 1)

            tr_pairs("ln0", xn, 0)
            te.wait_ge(*loaded("wp"))
            te.wait_ge(*ring.done(("ln0", 2)))
            for u in range(2):
                cs = slice(u * HALF, (u + 1) * HALF)
                acc(take(("z", u))[:, 0:HALF], [(pw1[:, k, :], xT[0:DH, k, cs]) for k in range(2)]).then_inc(bank_full, 1)
            for j in range(4):
                for u in range(2):
                    cs = slice(u * HALF, (u + 1) * HALF)
                    acc(take(("pr", j, u))[:, 0:HALF],
                        [(wp[:, k, j * 128:(j + 1) * 128], xT[0:DH, k, cs]) for k in range(2)]).then_inc(bank_full, 1)
            ps = take("pn")
            te.wait_ge(*ring.done(("z", 1)))
            te.wait_ge(sq_ready, 8)
            for t in range(NT):
                cs = slice(t * TT, (t + 1) * TT)
                for j in range(4):
                    te.matmul(ps[0:TT, t * 16 + 2 * j:t * 16 + 2 * j + 2], sqT[:, j, cs], hones[:, :], start=True, stop=True)
                mm = te.matmul(ps[0:TT, t * 16 + 8:t * 16 + 16], zT[:, cs], pw2[:, :], start=True, stop=True)
            mm.then_inc(bank_full, 1)
            te.wait_ge(*ring.done(("pr", 3, 1)))
            te.wait_ge(prep, 6)
            for t in range(NT):
                pq = [take(("ov", t, q)) for q in range(2)]
                for z in range(4):
                    for q in range(2):
                        r = slice(64 * q, 64 * q + 64)
                        mm = te.matmul(pq[q][0:TT, z * 128:(z + 1) * 128].rearrange("p (f s) -> p f s", f=2),
                                       prT[r, z, t * TT:(t + 1) * TT], mT[r, :, z, :], start=True, stop=True)
                        if z == 3:
                            mm.then_inc(bank_full, 1)
            for u in range(2):
                ps = take(("vb", u))
                if u == 0:
                    te.wait_ge(vrow, 1)
                for t in range(3):
                    mm = te.matmul(ps[0:TT, t * TT:(t + 1) * TT], vrep[:, 3 * u + t, :], ident[0:TT, 0:TT], start=True, stop=True)
                mm.then_inc(bank_full, 1)
            for t in range(NT):
                ps = take(("aT", t))
                te.wait_ge(att_w, t + 1)
                for j in range(4):
                    mm = te.transpose(ps[:, j * TT:(j + 1) * TT], att[:, t, j * 128:(j + 1) * 128], ident[0:TT, 0:TT])
                mm.then_inc(bank_full, 1)
            ps = take("gl")
            te.wait_ge(*ring.done(("vp", 3)))
            for t in range(NT):
                te.wait_ge(*ring.done(("aT", t)))
                mm = acc(ps[0:TT, t * 8:(t + 1) * 8], [(sqT[:, j, t * TT:(t + 1) * TT], gm[:, j, :]) for j in range(4)])
            mm.then_inc(bank_full, 1)
            for t in range(NT):
                ps = take(("agT", t))
                te.wait_ge(att_g, t + 1)
                for j in range(4):
                    mm = te.transpose(ps[:, j * TT:(j + 1) * TT], att[:, t, j * 128:(j + 1) * 128], ident[0:TT, 0:TT])
                mm.then_inc(bank_full, 1)
            for t in range(NT):
                ps = take(("h1", t))
                te.wait_ge(*ring.done(("agT", t)))
                acc(ps[0:TT, 0:D], [(prT[:, j, t * TT:(t + 1) * TT], vp[:, j, :]) for j in range(4)]).then_inc(bank_full, 1)
            for g in range(NT // 2):
                ps = take(("h1T", g))
                for q in range(2):
                    t = 2 * g + q
                    te.wait_ge(*ring.done(("h1", t)))
                    for k in range(2):
                        c0 = k * 252 + q * TT
                        mm = te.transpose(ps[0:DH, c0:c0 + TT], h1[:, t, k * DH:(k + 1) * DH], ident[0:TT, 0:TT])
                mm.then_inc(bank_full, 1)
            te.wait_ge(*ring.done(("h1T", 2)))
            te.wait_ge(*loaded("enc"))
            for u in range(2):
                cs = slice(u * HALF, (u + 1) * HALF)
                acc(take(("enc", u))[0:64, 0:HALF], [(encT[:, k, :], h1T[0:DH, k, cs]) for k in range(2)]).then_inc(bank_full, 1)
            ps = take("nq")
            te.wait_ge(sq_ready, 10)
            te.wait_ge(*loaded("small"))
            for t in range(NT):
                mm = te.matmul(ps[0:TT, t:t + 1], qsq[:, t * TT:(t + 1) * TT], ones[0:64, :], start=True, stop=True)
            mm.then_inc(bank_full, 1)
            te.wait_ge(prep, 10)
            te.wait_ge(*ring.done(("enc", 1)))
            for u in range(2):
                cs = slice(u * HALF, (u + 1) * HALF)
                for z in range(2):
                    te.matmul(take((("u1", "u2")[z], u))[:, 0:HALF], enU[:, z, :], qT0[:, cs], start=True, stop=True).then_inc(bank_full, 1)
            for t in range(NT):
                ps = take(("S", t))
                c0 = (t // 3) * HALF + (0 if t % 3 < 2 else N)
                n = HALF if t % 3 == 1 else N
                pairs = [(h1T[0:DH, k, t * TT:(t + 1) * TT], h1T[0:DH, k, c0:c0 + n]) for k in range(2)]
                if t % 3 == 1:
                    pairs.append((imgL[:, :], imgR[:, :]))
                acc(ps[0:TT, 0:n], pairs).then_inc(bank_full, 1)
            te.wait_ge(*ring.done(("u2", 1)))
            te.wait_ge(prep, 11)
            for t in range(NT):
                ps = take(("rs", t))
                te.matmul(ps[0:TT, 0:D], uu[:, t * TT:(t + 1) * TT], roW[:, :], start=True, stop=True).then_inc(bank_full, 1)
            for g in range(NT // 2):
                ps = take(("h2T", g))
                for q in range(2):
                    t = 2 * g + q
                    te.wait_ge(*ring.done(("rs", t)))
                    for k in range(2):
                        c0 = k * 252 + q * TT
                        mm = te.transpose(ps[0:DH, c0:c0 + TT], h2[:, t, k * DH:(k + 1) * DH], ident[0:TT, 0:TT])
                mm.then_inc(bank_full, 1)
            te.wait_ge(*ring.done(("h2T", 2)))
            te.wait_ge(ones_set, 2)

            def kr(k):
                return DH + 1 if k % 2 == 0 else DH
            for u in range(2):
                cs = slice(u * HALF, (u + 1) * HALF)
                acc(take(("r1", u))[0:16, 0:HALF], [(rw1[0:kr(k), k, :], h2T[0:kr(k), k, cs]) for k in range(2)]).then_inc(bank_full, 1)
            ps = take("rl")
            te.wait_ge(*ring.done(("r1", 1)))
            for t in range(NT):
                mm = te.matmul(ps[0:TT, t * 3:t * 3 + 3], r1T[:, t * TT:(t + 1) * TT], rw2[:, :], start=True, stop=True)
            mm.then_inc(bank_full, 1)
            te.wait_ge(*loaded("ew1"))
            for t in range(NT):
                for q in range(2):
                    n0, n1 = (0, 384) if q == 0 else (384, 576)
                    acc(take(("e1", t, q))[0:TT, 0:n1 - n0],
                        [(h2T[0:kr(k), k, t * TT:(t + 1) * TT], ew1[0:kr(k), k, n0:n1]) for k in range(2)]).then_inc(bank_full, 1)
            for u in range(2):
                te.wait_ge(e1n, 9 * (u + 1))
                for c in range(6):
                    ps = take(("e1T", u, c))
                    for t in range(3):
                        mm = te.transpose(ps[0:DH, t * TT:(t + 1) * TT], x1[:, 3 * u + t, c * DH:(c + 1) * DH], ident[0:TT, 0:TT])
                    mm.then_inc(bank_full, 1)
            te.wait_ge(*loaded("ew2"))
            te.wait_ge(ones_set, 3)
            for t in range(NT):
                te.wait_ge(*ring.done(("e1T", t // 3, 5)))
                for q in range(2):
                    ps = take(("y", t, q))
                    for z in range(2 - q):
                        e = 2 * q + z
                        mm = acc(ps[0:TT, z * D:(z + 1) * D],
                                 [(gT[0:kr(c), c, t * TT:(t + 1) * TT], ew2[0:kr(c), c, :]) for c in (2 * e, 2 * e + 1)])
                    mm.then_inc(bank_full, 1)
            tr_pairs("ln1", xn, NT)
            te.wait_ge(*loaded("route"))
            te.wait_ge(*ring.done(("ln1", 2)))
            ps = take("rt")
            for t in range(NT):
                mm = acc(ps[0:TT, t * 7:t * 7 + 7], [(xT[0:DH, k, t * TT:(t + 1) * TT], rwt[:, k, :]) for k in range(2)])
            mm.then_inc(bank_full, 1)
            te.wait_ge(cat_r, 1)
            for t in range(NT):
                ps = take(("xs", t))
                for c in range(3):
                    mm = te.transpose(ps[:, c * TT:(c + 1) * TT], cat[:, t, c * 128:(c + 1) * 128], ident[0:TT, 0:TT])
                mm.then_inc(bank_full, 1)
            for w in ring.all_done(("g", 0, 0, 0)):
                te.wait_ge(*w)
            with te.Fori(0, FE // 2) as i:
                for s in range(2):
                    te.wait_ge(f_split, 2 * i + s + 1)
                    for u in range(2):
                        cs = slice(u * HALF, (u + 1) * HALF)
                        for m in range(3):
                            for z, nm_ in enumerate("gu"):
                                n = slice(z * FI + m * 128, z * FI + (m + 1) * 128)
                                acc(take((nm_, s, u, m), i)[:, 0:HALF],
                                    [(wA[:, c, n], xS[:, c, cs]) for c in range(3)] + [(wB[:, c, n], xS[:, c, cs]) for c in range(2)]
                                    ).then_inc(bank_full, 1)
                    te.wait_ge(f_down[s], 16 * i + 16)
                    dn = raw2[:, s, 0:3 * D].rearrange("p (m n) -> p m n", m=3)
                    for z, tiles in enumerate(DN):
                        ps = take(("dn", s, z), i)
                        te.wait_ge(*ring.done(("u", s, min(z, 1), 2), i))
                        for q, t in enumerate(tiles):
                            mm = acc(ps[0:TT, q * D:(q + 1) * D], [(aT[s][:, m, t * TT:(t + 1) * TT], dn[:, m, :]) for m in range(3)])
                        mm.then_inc(bank_full, 1)
            tr_pairs("ln2", xn, 2 * NT)
            te.wait_ge(*loaded("qkv"))
            te.wait_ge(*ring.done(("ln2", 2)))
            for j in range(2):
                for l in range(4):
                    c0 = l * N + j * (N - QT)
                    for z, (n0, n1) in enumerate(((0, 2 * D), (2 * D, 3 * D))):
                        acc(take((("qk", "vv")[z], j, l))[0:QT, 0:n1 - n0],
                            [(xT[0:kr(k), k, c0:c0 + QT], wqkv[0:kr(k), k, n0:n1]) for k in range(2)]).then_inc(bank_full, 1)
            for j in range(2):
                te.wait_ge(o_ready, j + 1)
                for l in range(4):
                    ps = take(("oT", j, l))
                    for k in range(2):
                        mm = te.transpose(ps[0:DH, k * QT:(k + 1) * QT], o1[j][:, l, k * DH:(k + 1) * DH], ident[0:QT, 0:QT])
                    mm.then_inc(bank_full, 1)
            te.wait_ge(*ring.done(("oT", 1, 3)))
            for t in range(NT):
                acc(take(("op", t))[0:TT, 0:D], [(h1T[0:kr(k), k, t * TT:(t + 1) * TT], ow1[0:kr(k), k, :]) for k in range(2)]).then_inc(bank_full, 1)
            tr_pairs("ln3", xn, 3 * NT)
            te.wait_ge(*loaded("l1"))
            te.wait_ge(*loaded("wq2"))
            te.wait_ge(*loaded("mask"))
            te.wait_ge(*loaded("small"))
            for w in ring.all_done(("q2", 0, 0)):
                te.wait_ge(*w)
            with te.Fori(0, B // 2) as i:
                for s in range(2):
                    te.wait_ge(xb_r, 2 * i + s + 1)
                    for z in range(3):
                        ps = take(("q2", s, z), i)
                        for q in range(2):
                            m = 2 * z + q
                            mm = acc(ps[:, q * N:(q + 1) * N], [(wq2[:, k, m * 128:(m + 1) * 128], xb[:, s, k, :]) for k in range(2)])
                        mm.then_inc(bank_full, 1)
                    for j in range(2):
                        acc(take(("v2", s, j), i)[0:QT, 0:D],
                            [(xb[:, s, k, j * (N - QT):j * (N - QT) + QT], wv2[:, k, :]) for k in range(2)]).then_inc(bank_full, 1)
                for s in range(2):
                    te.wait_ge(*ring.done(("q2", s, 2), i))
                    for g in range(4):
                        r = slice(32 * g, 32 * g + AD)
                        pA, pB = take(("SA", s, g), i), take(("SB", s, g), i)
                        te.matmul(pA[0:QT, 0:474], identb[0:QT, 0:QT], maskA[:, :], start=True, stop=False, skip_group_check=True)
                        te.matmul(pB[0:QT, 0:378], identb[0:QT, 0:QT], maskB[:, :], start=True, stop=False, skip_group_check=True)
                        for m in range(3):
                            te.matmul(pA[0:QT, m * QT:(m + 1) * QT], qk[s][r, m, 0:QT], qk[s][r, 3 + m, 0:QT], start=False, stop=True, skip_group_check=True)
                        te.matmul(pA[0:QT, 285:474], qk[s][r, 2, N - QT:N], qk[s][r, 5, :], start=False, stop=True, skip_group_check=True).then_inc(bank_full, 1)
                        for m in range(2):
                            mm = te.matmul(pB[0:QT, m * N:(m + 1) * N], qk[s][r, m, N - QT:N], qk[s][r, 3 + m, :], start=False, stop=True, skip_group_check=True)
                        mm.then_inc(bank_full, 1)
                for s in range(2):
                    for z in range(8):
                        ps = take(("PT", s, z), i)
                        for y in range(5 * z, min(5 * z + 5, 36)):
                            hd, c = y // 3, y % 3
                            if y % 9 == 0:
                                te.wait_ge(exp_r, 8 * i + 4 * s + y // 9 + 1)
                            g, m = hd // 3, hd % 3
                            src = (P0[s][:, g, m, :], P1[s][:, g, m, 0:QT], P1[s][:, g, m, N - QT:N])[c]
                            mm = te.transpose(ps[0:QT, (y - 5 * z) * QT:(y - 5 * z + 1) * QT], src, ident[0:QT, 0:QT])
                        mm.then_inc(bank_full, 1)
                for s in range(2):
                    te.wait_ge(v2z, 2 * i + s + 1)
                    te.wait_ge(*ring.done(("PT", s, 6), i))
                    te.wait_ge(*ring.done(("PT", s, 7), i))
                    for m in range(3):
                        ps = take(("yu", s, m), i)
                        for g in range(4):
                            hd, y = 4 * m + g, 3 * (3 * g + m)
                            r = slice(32 * g, 32 * g + 32)
                            te.matmul(ps[r, 0:2 * QT], v32[s][:, 0, hd, :], PT[s][:, y:y + 2, :],
                                      start=True, stop=False, skip_group_check=True)
                            mm = te.matmul(ps[r, QT:2 * QT], v32[s][:, 1, hd, :], PT[s][:, y + 2, :],
                                           start=False, stop=True, skip_group_check=True)
                        mm.then_inc(bank_full, 1)
            te.wait_ge(*loaded("moe"))
            te.wait_ge(*ring.done(("yu", 1, 2), B // 2 - 1))
            for t in range(NT):
                acc(take(("cp", t))[0:TT, 0:D], [(yT[m][:, t * TT:(t + 1) * TT], cpw[:, m, :]) for m in range(3)]).then_inc(bank_full, 1)
            tr_pairs("ln4", xn, 4 * NT)
            te.wait_ge(*ring.done(("ln4", 2)))
            ps = take("mr")
            for t in range(NT):
                mm = acc(ps[0:TT, t * 8:t * 8 + 8], [(xT[0:DH, k, t * TT:(t + 1) * TT], wg[:, k, :]) for k in range(2)])
            mm.then_inc(bank_full, 1)
            ps = take("cs")
            te.wait_ge(sel_r, 1)
            for t in range(NT):
                mm = acc(ps[0:TT, t * 8:t * 8 + 8], [(tones[:, :], selb[:, q, :]) for q in range(t)] + [(tri[:, :], selb[:, t, :])])
            mm.then_inc(bank_full, 1)
            te.wait_ge(xs_r, 1)
            for w in ring.all_done(("d", 0)):
                te.wait_ge(*w)
            with te.Fori(0, ME // 2) as i:
                for s in range(2):
                    ps = take(("d", s), i)
                    te.wait_ge(oh_r, 2 * i + s + 1)
                    for k in range(2):
                        mm = acc(ps[0:DH, k * CAP:(k + 1) * CAP],
                                 [(xs[:, z, t, k * DH:(k + 1) * DH], oh[:, s, t, :]) for t in range(NT) for z in range(3)])
                    mm.then_inc(bank_full, 1)
                for s in range(2):
                    for c in range(2):
                        ps = take(("T", s, c), i)[:, :].bitcast(BF16)
                        for t in range(NT):
                            mm = te.transpose(ps[0:CT, t * TT:(t + 1) * TT], oh[:, s, t, c * CT:(c + 1) * CT], identb[0:TT, 0:TT])
                        mm.then_inc(bank_full, 1)
                for s in range(2):
                    te.wait_ge(m_fc[s], 16 * i + 16)
                    te.wait_ge(*ring.done(("d", s), i))
                    fc = raw1[0:DH, s * 1536:(s + 1) * 1536].rearrange("p (k n) -> p k n", k=2)
                    for z in range(3):
                        ps = take(("fc", s, z), i)
                        for q in range(2):
                            m = 2 * z + q
                            mm = acc(ps[:, q * CAP:(q + 1) * CAP], [(fc[:, k, m * 128:(m + 1) * 128], xe[:, s, k, :]) for k in range(2)])
                        mm.then_inc(bank_full, 1)
                for s in range(2):
                    te.wait_ge(m_pj[s], 16 * i + 16)
                    pj = raw2[:, s, :].rearrange("p (m n) -> p m n", m=6)
                    ps = take(("pj", s), i)
                    te.wait_ge(*ring.done(("fc", s, 2), i))
                    for c in range(2):
                        mm = acc(ps[0:CT, c * D:(c + 1) * D], [(heT[:, s, m, c * CT:(c + 1) * CT], pj[:, m, :]) for m in range(6)])
                    mm.then_inc(bank_full, 1)
                for s in range(2):
                    te.wait_ge(*ring.done(("T", s, 1), i))
                    te.wait_ge(*ring.done(("pj", s), i))
                    for z, tiles in enumerate(CB):
                        ps = take(("cb", s, z), i)
                        for q, t in enumerate(tiles):
                            mm = acc(ps[0:TT, q * D:(q + 1) * D], [(ohT[:, s, c, t * TT:(t + 1) * TT], eo[:, s, c, :]) for c in range(2)])
                        mm.then_inc(bank_full, 1)

        @block.scalar
        def _(ac):
            def full(key, i=0):
                ac.wait_ge(*ring.full(key, i))
                return psum[ring.bank(key)]

            def evac_pairs(name, dst):
                for g in range(NT // 2):
                    ps = full((name, g))
                    ac.activation(dst[0:DH, :, g * 252:(g + 1) * 252], ps[0:DH, 0:504].rearrange("p (k t) -> p k t", k=2),
                                  ACT.Copy).then_inc(emptied_s, 1)

            ac.wait_ge(*loaded("tok8"))
            byimg = [xT[0:DH, m, :].rearrange("p (i n) -> p i n", i=B) for m in range(2)]
            for u in range(2):
                for m in range(2):
                    ps = full(("emb", u, m))
                    ac.activation(byimg[m][:, 2 * u:2 * u + 2, 0:144], ps[0:DH, 0:288].rearrange("p (i n) -> p i n", i=2),
                                  ACT.Identity, bias=tokb[:, m, 0:1]).then_inc(emptied_s, 1)
            for m in range(2):
                ps = full(("e16", m))
                ac.activation(byimg[m][:, :, 144:180], ps[0:DH, 0:144].rearrange("p (i n) -> p i n", i=B),
                              ACT.Identity, bias=tokb[:, m, 1:2]).then_inc(emptied_s, 1)
            ps = full("norms")
            ac.activation(mi[:, 0:256], ps[:, 0:256], ACT.Sqrt)
            ac.activation(mi[0:64, 256:320], ps[0:64, 256:320], ACT.Sqrt).then_inc(emptied_s, 1)

            ps = full("e32")
            ac.activation(e32[:, :], ps[0:36, 0:D], ACT.Copy).then_inc(emptied_s, 1)
            ps = full("e32T")
            for m in range(2):
                it = ac.activation(byimg[m][:, :, 180:189], ps[0:DH, 36 * m:36 * m + 36].rearrange("p (i n) -> p i n", i=B),
                                   ACT.Identity, bias=tokb[:, m, 2:3])
            it.then_inc(emptied_s, 1)
            ac.wait_ge(var_ready, 1)
            ac.activation(rstd[:, 0:NT], rstd[:, 0:NT], ACT.Sqrt).then_inc(std_ready, 1)
            evac_pairs("ln0", xT)
            ac.wait_ge(*loaded("wp"))
            for u in range(2):
                ps = full(("z", u))
                ac.activation(zT[:, u * HALF:(u + 1) * HALF], ps[:, 0:HALF], ACT.Silu, bias=pb1[:, 0:1]).then_inc(emptied_s, 1)
            for j in range(4):
                for u in range(2):
                    ac.wait_ge(*ring.done(("pr", j, u)))
                    cs = slice(u * HALF, (u + 1) * HALF)
                    ac.activation(sqT[:, j, cs], prT[:, j, cs], ACT.Square).then_inc(sq_ready, 1)
            ac.wait_ge(plog, 1)
            ac.activation(pp[:, :, :], pn[:, :, 8:16], ACT.Sigmoid).then_inc(psig, 1)
            ac.wait_ge(*loaded("b0"))
            ac.activation(beta[:, :], beta[:, :], ACT.Sigmoid).then_inc(bsig, 1)
            for t in range(NT):
                for q in range(2):
                    ps = full(("ov", t, q))
                    if t >= 2 and q == 0:
                        ac.wait_ge(ovr, t - 1)
                    ac.activation(ov2[:, t % 2, q:8:2, :], ps[0:TT, :].rearrange("p (a n) -> p a n", a=4),
                                  ACT.Square).then_inc(emptied_s, 1)
            for u in range(2):
                ps = full(("vb", u))
                ac.activation(vB[:, u * HALF:(u + 1) * HALF], ps[0:TT, 0:HALF], ACT.Copy).then_inc(emptied_s, 1)
            for t in range(NT):
                ps = full(("aT", t))
                ac.activation(sqT[:, :, t * TT:(t + 1) * TT], ps[:, 0:504].rearrange("p (j t) -> p j t", j=4), ACT.Copy).then_inc(emptied_s, 1)
            ac.wait_ge(plog, 2)
            ac.activation(gts[:, :, :], gts[:, :, :], ACT.Exp).then_inc(gexp, 1)
            for t in range(NT):
                ps = full(("agT", t))
                ac.activation(prT[:, :, t * TT:(t + 1) * TT], ps[:, 0:504].rearrange("p (j t) -> p j t", j=4), ACT.Copy).then_inc(emptied_s, 1)
            evac_pairs("h1T", h1T)
            for u in range(2):
                cs = slice(u * HALF, (u + 1) * HALF)
                ps = full(("enc", u))
                ac.activation(qsq[:, cs], ps[0:64, 0:HALF], ACT.Square).then_inc(sq_ready, 1)
                ac.activation(qT0[:, cs], ps[0:64, 0:HALF], ACT.Copy).then_inc(emptied_s, 1)
            for u in range(2):
                ps = full(("u1", u))
                ac.activation(uu[:, u * HALF:(u + 1) * HALF], ps[:, 0:HALF], ACT.Copy).then_inc(emptied_s, 1)
            for t in range(NT):
                ps = full(("S", t))
                n = HALF if t % 3 == 1 else N
                ac.wait_ge(nm, t + 1)
                if t >= 2:
                    ac.wait_ge(e_used, t - 1)
                ac.activation(ex[:, t % 2, 0:n], ps[0:TT, 0:n], ACT.Exp, bias=nmax[:, t:t + 1], scale=SQ,
                              accum_out=esum[:, t:t + 1]).then_inc(emptied_s, 1)
            evac_pairs("h2T", h2T)
            for u in range(2):
                cs = slice(u * HALF, (u + 1) * HALF)
                ps = full(("r1", u))
                ac.activation(r1T[:, cs], ps[0:16, 0:HALF], ACT.Gelu).then_inc(emptied_s, 1)
            for t in range(NT):
                for q in range(2):
                    n0, n1 = (0, 384) if q == 0 else (384, 576)
                    ps = full(("e1", t, q))
                    ac.activation(x1[:, t, n0:n1], ps[0:TT, 0:n1 - n0], ACT.Copy).then_inc(emptied_s, 1)
            ac.wait_ge(rlog, 1)
            ac.activation(rg[:, :, :], rg[:, :, :], ACT.Exp).then_inc(rexp, 1)
            ac.wait_ge(var_ready, 2)
            ac.activation(rstd[:, :], rstd[:, :], ACT.Sqrt).then_inc(std_ready, 1)
            for u in range(2):
                for c in range(6):
                    ps = full(("e1T", u, c))
                    ac.activation(gT[0:DH, c, u * HALF:(u + 1) * HALF], ps[0:DH, 0:HALF], ACT.Gelu,
                                  scale=egb[:, c, 0:1], bias=egb[:, c, 1:2]).then_inc(emptied_s, 1)
            ac.wait_ge(var_ready, 3)
            ac.activation(rstd[:, 0:NT], rstd[:, 0:NT], ACT.Sqrt).then_inc(std_ready, 1)
            evac_pairs("ln1", xT)
            ac.wait_ge(rsig_in, 1)
            ac.activation(pv[:, :, 0:7], pv[:, :, 0:7], ACT.Sigmoid).then_inc(rsig, 1)
            for t in range(NT):
                ps = full(("xs", t))
                ac.activation(xS[:, :, t * TT:(t + 1) * TT], ps[:, 0:3 * TT].rearrange("p (c t) -> p c t", c=3), ACT.Copy).then_inc(emptied_s, 1)
            with ac.Fori(0, FE // 2) as i:
                for s in range(2):
                    ac.wait_ge(*ring.full(("u", 1 - s, 1, 2), i, back=1 - s))
                    ac.wait_ge(f_up, 32 * i + 16 * s + 16)
                    for c in range(3):
                        ac.activation(wA[:, c, :], rawf[:, c, :], ACT.Copy).then_inc(f_wh, 1)
                    for u in range(2):
                        for m in range(3):
                            ps = full(("g", s, u, m), i)
                            ac.wait_ge(*ring.done(("u", 1 - s, u, m), i, back=1 - s))
                            ac.activation(sg[:, 3 * u + m, :], ps[:, 0:HALF], ACT.Silu).then_inc(emptied_s, 1)
            ac.wait_ge(var_ready, 4)
            ac.activation(rstd[:, 0:NT], rstd[:, 0:NT], ACT.Sqrt).then_inc(std_ready, 1)
            evac_pairs("ln2", xT)
            for j in range(2):
                for l in range(4):
                    ps = full(("qk", j, l))
                    ac.activation(qkv[j][:, l, 0:2 * D], ps[0:QT, 0:2 * D], ACT.Copy)
                    ac.activation(sqk[j][l], ps[0:QT, 0:2 * D], ACT.Square).then_inc(emptied_s, 1)
                    ps = full(("vv", j, l))
                    ac.activation(qkv[j][:, l, 2 * D:3 * D], ps[0:QT, 0:D], ACT.Copy).then_inc(emptied_s, 1)
            for j in range(2):
                ac.wait_ge(ssum_r, j + 1)
                ac.activation(ssum2[:, j, :, :], ssum2[:, j, :, :], ACT.Sqrt).then_inc(snorm, 1)
            ac.wait_ge(lsexp_in, 1)
            ac.activation(lsc[:, :], lsc[:, :], ACT.Exp).then_inc(lsexp, 1)
            for j in range(2):
                ac.wait_ge(lexp_in, j + 1)
                ac.activation(lg2[:, j, :, :, :], lg2[:, j, :, :, :], ACT.Exp).then_inc(lexp, 1)
            for j in range(2):
                for l in range(4):
                    ps = full(("oT", j, l))
                    c0 = l * N + j * QT
                    ac.activation(h1T[0:DH, :, c0:c0 + QT - j], ps[0:DH, 0:2 * QT].rearrange("p (k t) -> p k t", k=2)[:, :, j:QT],
                                  ACT.Copy).then_inc(emptied_s, 1)

            def evac_scaled(name, w):
                for g in range(NT // 2):
                    ps = full((name, g))
                    for k in range(2):
                        it = ac.activation(xT[0:DH, k, g * 252:(g + 1) * 252], ps[0:DH, k * 252:(k + 1) * 252],
                                           ACT.Copy, scale=flnw[:, w, k:k + 1])
                    it.then_inc(emptied_s, 1)
            for n in (5, 6):
                ac.wait_ge(var_ready, n)
                ac.activation(rstd[:, 0:NT], rstd[:, 0:NT], ACT.Sqrt).then_inc(std_ready, 1)
            ac.wait_ge(*loaded("l1"))
            evac_scaled("ln3", 0)
            ac.wait_ge(*ring.done(("ln3", 2)))
            with ac.Fori(0, B // 2) as i:
                for s in range(2):
                    ac.activation(xb[:, s, :, :], xT[0:DH, :, bass.ds((2 * i + s) * N, N)], ACT.Copy).then_inc(xb_r, 1)
                for s in range(2):
                    for z in range(3):
                        ps = full(("q2", s, z), i)
                        ac.activation(qk[s][0:112, 2 * z:2 * z + 2, :], ps[0:112, 0:2 * N].rearrange("p (q n) -> p q n", q=2), ACT.Copy).then_inc(emptied_s, 1)
                for s in range(2):
                    for g in range(4):
                        ac.wait_ge(v_set, 8 * i + 4 * s + g + 1)
                        pA, pB = psum[ring.bank(("SA", s, g))], psum[ring.bank(("SB", s, g))]

                        def weights(dst, src, z):
                            return ac.activation(dst, src, ACT.Exp, scale=float(AD) ** -0.5, bias=mx[:, s, g, z:z + 1],
                                                 accum_out=psums[:, s, g, z:z + 1])
                        for m in range(3):
                            weights(P0[s][:, g, m, :], pA[0:QT, m * QT:(m + 1) * QT], m)
                        weights(P1[s][:, g, 2, :], pA[0:QT, 285:474], 5).then_inc(emptied_s, 1)
                        weights(P1[s][:, g, 0, :], pB[0:QT, 0:N], 3)
                        weights(P1[s][:, g, 1, :], pB[0:QT, N:2 * N], 4).then_inc(emptied_s, 1)
                for s in range(2):
                    for z in range(1, 8, 2):
                        n = min(5, 36 - 5 * z)
                        ps = full(("PT", s, z), i)
                        ac.activation(PT[s][:, 5 * z:5 * z + n, :], ps[0:QT, 0:n * QT].rearrange("p (z n) -> p z n", z=n), ACT.Copy).then_inc(emptied_s, 1)
            ac.wait_ge(var_ready, 7)
            ac.activation(rstd[:, 0:NT], rstd[:, 0:NT], ACT.Sqrt).then_inc(std_ready, 1)
            evac_scaled("ln4", 1)
            ac.wait_ge(mlg, 1)
            ac.activation(pv[:, :, :], pv[:, :, :], ACT.Exp).then_inc(mexp, 1)
            with ac.Fori(0, ME // 2) as i:
                for s in range(2):
                    for c in range(2):
                        ps = full(("T", s, c), i)
                        ac.activation(ohT[:, s, c, :], ps[:, :].bitcast(BF16)[0:CT, 0:T], ACT.Copy).then_inc(emptied_s, 1)
                for s in range(2):
                    for z in range(3):
                        ps = full(("fc", s, z), i)
                        ac.activation(heT[:, s, 2 * z:2 * z + 2, :], ps[:, 0:2 * CAP].rearrange("p (q c) -> p q c", q=2),
                                      ACT.Gelu).then_inc(emptied_s, 1)

        @block.vector
        def _(ve):
            n_step = [0]

            def st(inst):
                inst.then_inc(v_step, 1)
                n_step[0] += 1

            def own():
                ve.wait_ge(v_step, n_step[0])

            def full(key, i=0):
                ve.wait_ge(*ring.full(key, i))
                return psum[ring.bank(key)]

            def bc(ap, shape):
                return ap.unsqueeze(len(ap.shape)).to_broadcast(shape)

            def layernorm(var_n, src=h, dst=xn):
                for t in range(NT):
                    st(ve.bn_stats(bn[:, t, :], src[:, t, :]))
                own()
                for t in range(NT):
                    st(ve.bn_aggr(mv[:, t, :], bn[:, t, :]))
                own()
                ve.tensor_scalar(rstd[:, 0:NT], mv[:, 0:NT, 1], EPS, None, ALU.add).then_inc(var_ready, 1)
                ve.wait_ge(std_ready, var_n)
                st(ve.reciprocal(rstd[:, 0:NT], rstd[:, 0:NT]))
                own()
                for t in range(NT):
                    it = ve.tensor_scalar(dst[:, t, :], src[:, t, :], mv[:, t, 0:1], rstd[:, t:t + 1], ALU.subtract, ALU.mult)
                    if dst is xn:
                        it.then_inc(xn_ready, 1)
                    else:
                        st(it)
                own()

            ve.memset(xT[DH:DH + 1, :, :], 1.0).then_inc(ones_set, 1)
            ve.memset(h1T[DH:DH + 1, :, :], 1.0).then_inc(ones_set, 1)
            ve.wait_ge(*loaded("m"))
            ve.wait_ge(*loaded("const"))
            ve.tensor_tensor(msq[:, 0:256], mT[:, 0, :, :], mT[:, 0, :, :], ALU.mult).then_inc(prep, 1)
            ve.tensor_tensor(msq[0:64, 256:320], pc[:, 0, :, :], pc[:, 0, :, :], ALU.mult).then_inc(prep, 1)
            st(ve.tensor_scalar(mT[:, 1, :, :], mT[:, 1, :, :], sgn[:, 0:1], None, ALU.mult))
            st(ve.tensor_scalar(pc[:, 1, :, :], pc[:, 1, :, :], sgn[0:64, 0:1], None, ALU.mult))
            ve.wait_ge(*ring.done("norms"))
            own()
            st(ve.tensor_scalar(mi[:, 0:256], mi[:, 0:256], 1e-12, None, ALU.max))
            st(ve.tensor_scalar(mi[0:64, 256:320], mi[0:64, 256:320], 1e-12, None, ALU.max))
            own()
            st(ve.reciprocal(mi[:, 0:256], mi[:, 0:256]))
            st(ve.reciprocal(mi[0:64, 256:320], mi[0:64, 256:320]))
            own()
            for f in range(2):
                st(ve.tensor_tensor(pc[:, f, :, :], pc[:, f, :, :], mi[0:64, 256:320].rearrange("p (a r) -> p a r", a=2), ALU.mult))
            own()
            for f in range(2):
                ve.tensor_tensor(gg[:, f, :], pc[:, 0, 0, :], pc[:, f, 1, :], ALU.mult).then_inc(prep, 1)
            for f in range(2):
                ve.tensor_tensor(mT[:, f, :, :], mT[:, f, :, :], mi[:, 0:256].rearrange("p (a s) -> p a s", a=4), ALU.mult).then_inc(prep, 1)
            ps = full("g")
            ve.tensor_copy(gsb[:, :], ps[0:64, 0:64]).then_inc(emptied_v, 1)
            ve.wait_ge(*ring.done("g"))
            gre, gim = gsb[:, 0:32], gsb[:, 32:64]
            st(ve.tensor_tensor(utmp[:, 0, :], pc[:, 1, 0, :], gim, ALU.mult))
            st(ve.tensor_tensor(utmp[:, 1, :], pc[:, 1, 0, :], gre, ALU.mult))
            st(ve.tensor_tensor(enU[:, 0, 0:32], pc[:, 0, 0, :], gre, ALU.mult))
            st(ve.tensor_tensor(enU[:, 0, 32:64], pc[:, 0, 0, :], gim, ALU.mult))
            own()
            st(ve.tensor_tensor(enU[:, 0, 0:32], enU[:, 0, 0:32], utmp[:, 0, :], ALU.subtract))
            st(ve.tensor_tensor(enU[:, 0, 32:64], enU[:, 0, 32:64], utmp[:, 1, :], ALU.add))
            own()
            ve.tensor_copy(enU[:, 0, 64:96], enU[:, 0, 32:64]).then_inc(prep, 1)
            ve.tensor_copy(enU[:, 0, 96:128], enU[:, 0, 0:32]).then_inc(prep, 1)
            for q in range(2):
                ve.tensor_copy(enU[:, 1, 64 * q:64 * q + 64].rearrange("p (f r) -> p f r", f=2), pc[:, :, 1, :]).then_inc(prep, 1)
            for c in range(4):
                ps = full(("vp", c))
                ve.tensor_copy(gm[0:64, c, :], ps[0:64, D:D + 8])
                ve.tensor_copy(gm[64:128, c, :], ps[64:128, D + 8:D + 16])
                ve.tensor_copy(vp[:, c, :], ps[:, 0:D]).then_inc(emptied_v, 1)
            for t in range(NT):
                ps = full(("h0", t))
                ve.tensor_copy(h[:, t, :], ps[0:TT, 0:D]).then_inc(emptied_v, 1)
            ve.wait_ge(*ring.done(("h0", NT - 1)))
            layernorm(1)
            for j in range(4):
                for u in range(2):
                    ps = full(("pr", j, u))
                    ve.tensor_copy(prT[:, j, u * HALF:(u + 1) * HALF], ps[:, 0:HALF]).then_inc(emptied_v, 1)
            ve.wait_ge(*loaded("b0"))
            ps = full("pn")
            ve.tensor_copy(pn[:, :, :], ps[0:TT, 0:96].rearrange("p (t n) -> p t n", t=NT)).then_inc(emptied_v, 1)
            ve.wait_ge(*ring.done("pn"))
            ve.tensor_tensor(pn[:, :, 8:16], pn[:, :, 8:16], pb2[:, :].unsqueeze(1).to_broadcast([TT, NT, 8]), ALU.add).then_inc(plog, 1)
            st(ve.tensor_scalar(pn[:, :, 0:8], pn[:, :, 0:8], 1e-24, None, ALU.max))
            own()
            st(ve.reciprocal(pn[:, :, 0:8], pn[:, :, 0:8]))
            ve.wait_ge(psig, 1)
            st(ve.tensor_scalar(pp[:, :, :], pp[:, :, :], 0.95, None, ALU.mult))
            own()
            st(ve.tensor_scalar(pa[:, :, :], pp[:, :, :], -1.0, 1.0, ALU.mult, ALU.add))
            st(ve.tensor_reduce(ptok[:, :], pp[:, :, :], X, ALU.add))
            own()
            st(ve.tensor_tensor(pa[:, :, :], pa[:, :, :], pn[:, :, 0:8], ALU.mult))
            st(ve.tensor_scalar(ptok[:, :], ptok[:, :], 1.0 / S0H, None, ALU.mult))
            own()
            st(ve.tensor_scalar(vtok[:, :], ptok[:, :], -1.0, 1.0, ALU.mult, ALU.add))
            own()
            ve.tensor_copy(vrep[:, :, :], bc(vtok[:, :], [TT, NT, TT])).then_inc(vrow, 1)
            for t in range(NT):
                av = att[:, t, :].rearrange("p (a s) -> p a s", a=8)
                ve.wait_ge(*ring.done(("ov", t, 1)))
                ve.tensor_tensor(av, ov2[:, t % 2, :, 0:64], ov2[:, t % 2, :, 64:128], ALU.add).then_inc(ovr, 1)
                ve.wait_ge(ovr, t + 1)
                st(ve.tensor_reduce(rr[:, t, :], av, X, ALU.add))
            own()
            st(ve.tensor_tensor(rr[:, :, :], rr[:, :, :], pa[:, :, :], ALU.mult))
            own()
            st(ve.scalar_tensor_tensor(rr[:, :, :], pp[:, :, :], float(S0S) / S0D, rr[:, :, :], ALU.mult, ALU.add))
            own()
            st(ve.tensor_scalar(rr[:, :, :], rr[:, :, :], 1e-8, None, ALU.add))
            own()
            st(ve.reciprocal(rr[:, :, :], rr[:, :, :]))
            own()
            st(ve.tensor_tensor(pn[:, :, 0:8], pa[:, :, :], rr[:, :, :], ALU.mult))
            st(ve.scalar_tensor_tensor(pn[:, :, 8:16], pp[:, :, :], 1.0 / S0D, rr[:, :, :], ALU.mult, ALU.mult))
            own()
            for t in range(NT):
                av = att[:, t, :].rearrange("p (a s) -> p a s", a=8)
                st(ve.tensor_tensor(av, av, bc(pn[:, t, 0:8], [TT, 8, 64]), ALU.mult))
                own()
                ve.tensor_tensor(av, av, bc(pn[:, t, 8:16], [TT, 8, 64]), ALU.add).then_inc(att_w, 1)
            ps = full("gl")
            ve.tensor_tensor(gts[:, :, :], ps[0:TT, 0:48].rearrange("p (t n) -> p t n", t=NT),
                             gateb[:, :].unsqueeze(1).to_broadcast([TT, NT, 8]), ALU.add).then_inc(emptied_v, 1)
            ve.wait_ge(*ring.done("gl"))
            st(ve.tensor_reduce(red[:, :], gts[:, :, :], X, ALU.max))
            own()
            ve.tensor_tensor(gts[:, :, :], gts[:, :, :], bc(red[:, :], [TT, NT, 8]), ALU.subtract).then_inc(plog, 1)
            ve.wait_ge(gexp, 1)
            st(ve.tensor_reduce(gsum[:, :], gts[:, :, :], X, ALU.add))
            own()
            st(ve.reciprocal(gsum[:, :], gsum[:, :]))
            own()
            st(ve.tensor_tensor(gts[:, :, :], gts[:, :, :], bc(gsum[:, :], [TT, NT, 8]), ALU.mult))
            own()
            for t in range(NT):
                av = att[:, t, :].rearrange("p (a s) -> p a s", a=8)
                ve.tensor_tensor(av, av, bc(gts[:, t, :], [TT, 8, 64]), ALU.mult).then_inc(att_g, 1)
            for t in range(NT):
                ps = full(("h1", t))
                ve.wait_ge(xob, t + 1)
                ve.tensor_tensor(h1[:, t, :], ps[0:TT, 0:D], xn[:, t, :], ALU.add).then_inc(emptied_v, 1)
            ps = full("nq")
            ve.tensor_scalar(nq[:, :], ps[0:TT, 0:NT], 1e-24, None, ALU.max).then_inc(emptied_v, 1)
            ve.wait_ge(*ring.done("nq"))
            st(ve.reciprocal(nq[:, :], nq[:, :]))
            for u in range(2):
                ps = full(("u2", u))
                ve.wait_ge(*ring.done(("u1", u)))
                cs = slice(u * HALF, (u + 1) * HALF)
                ve.tensor_tensor(uu[:, cs], uu[:, cs], ps[:, 0:HALF], ALU.mult).then_inc(emptied_v, 1)
            ve.wait_ge(*loaded("enc"))
            ve.tensor_scalar(roW[:, :], roW[:, :], sg4[:, 0:1], None, ALU.mult).then_inc(prep, 1)

            def coupled(t):
                n = HALF if t % 3 == 1 else N
                c0 = (t // 3) * HALF + (0 if t % 3 < 2 else N)
                ve.wait_ge(*ring.done(("S", t)))
                ve.tensor_tensor_reduce(ex[:, t % 2, 0:n], ex[:, t % 2, 0:n], vB[:, c0:c0 + n], 1.0, 0.0,
                                        ALU.mult, ALU.add, nei[:, t:t + 1]).then_inc(e_used, 1)
            ve.wait_ge(*ring.done(("vb", 1)))
            for t in range(NT):
                n = HALF if t % 3 == 1 else N
                c0 = (t // 3) * HALF + (0 if t % 3 < 2 else N)
                ps = full(("S", t))
                st(ve.tensor_reduce(red[:, t:t + 1], ps[0:TT, 0:n], X, ALU.max))
                own()
                ve.tensor_scalar(nmax[:, t:t + 1], red[:, t:t + 1], -SQ, None, ALU.mult).then_inc(nm, 1)
                if t >= 1:
                    coupled(t - 1)
            coupled(NT - 1)
            ve.wait_ge(e_used, NT)
            st(ve.reciprocal(esum[:, :], esum[:, :]))
            own()
            st(ve.tensor_tensor(nei[:, :], nei[:, :], esum[:, :], ALU.mult))
            own()
            ve.wait_ge(bsig, 1)
            st(ve.tensor_scalar(nei[:, :], nei[:, :], beta[:, 0:1], None, ALU.mult))
            own()
            st(ve.tensor_scalar(nei[:, :], nei[:, :], -1.0, 1.0, ALU.mult, ALU.add))
            own()
            st(ve.tensor_tensor(sc2[:, :], ptok[:, :], nei[:, :], ALU.mult))
            own()
            st(ve.tensor_scalar(sc2[:, :], sc2[:, :], 0.0, 0.95, ALU.max, ALU.min))
            own()
            st(ve.tensor_scalar(sc2[:, :], sc2[:, :], -1.0, 1.0, ALU.mult, ALU.add))
            own()
            st(ve.tensor_tensor(sc1[:, :], sc2[:, :], nq[:, :], ALU.mult))
            for t in range(NT):
                st(ve.scalar_tensor_tensor(h2[:, t, :], rob[:, :], sc2[:, t:t + 1], h1[:, t, :], ALU.mult, ALU.add))
            own()
            for t in range(NT):
                ps = full(("rs", t))
                ve.scalar_tensor_tensor(h2[:, t, :], ps[0:TT, 0:D], sc1[:, t:t + 1], h2[:, t, :], ALU.mult, ALU.add).then_inc(emptied_v, 1)
            ve.memset(gT[DH:DH + 1, :, :], 1.0).then_inc(ones_set, 1)
            ps = full("rl")
            ve.tensor_tensor(rg[:, :, :], ps[0:TT, 0:18].rearrange("p (t n) -> p t n", t=NT),
                             rb2[:, :].unsqueeze(1).to_broadcast([TT, NT, 3]), ALU.add).then_inc(emptied_v, 1)
            ve.wait_ge(*ring.done("rl"))
            st(ve.tensor_reduce(red[:, :], rg[:, :, :], X, ALU.max))
            own()
            ve.tensor_tensor(rg[:, :, :], rg[:, :, :], bc(red[:, :], [TT, NT, 3]), ALU.subtract).then_inc(rlog, 1)
            for t in range(NT):
                ve.wait_ge(*ring.done(("e1", t, 1)))
                for e in range(3):
                    st(ve.bn_stats(bn[:, 3 * t + e, :], x1[:, t, e * D:(e + 1) * D]))
                own()
                for e in range(3):
                    st(ve.bn_aggr(mv[:, 3 * t + e, :], bn[:, 3 * t + e, :]))
            own()
            ve.tensor_scalar(rstd[:, :], mv[:, :, 1], EPS, None, ALU.add).then_inc(var_ready, 1)
            ve.wait_ge(rexp, 1)
            st(ve.tensor_reduce(gsum[:, :], rg[:, :, :], X, ALU.add))
            own()
            st(ve.reciprocal(gsum[:, :], gsum[:, :]))
            own()
            st(ve.tensor_tensor(rg[:, :, :], rg[:, :, :], bc(gsum[:, :], [TT, NT, 3]), ALU.mult))
            ve.wait_ge(std_ready, 2)
            st(ve.reciprocal(rstd[:, :], rstd[:, :]))
            own()
            for t in range(NT):
                for e in range(3):
                    z = 3 * t + e
                    ve.tensor_scalar(x1[:, t, e * D:(e + 1) * D], x1[:, t, e * D:(e + 1) * D], mv[:, z, 0:1], rstd[:, z:z + 1],
                                     ALU.subtract, ALU.mult).then_inc(e1n, 1)
            for t in range(NT):
                ve.wait_ge(hb, t + 1)
                for e in range(3):
                    ps = full(("y", t, e // 2))
                    own()
                    it = ve.scalar_tensor_tensor(h[:, t, :], ps[0:TT, (e % 2) * D:(e % 2 + 1) * D], rg[:, t, e:e + 1], h[:, t, :],
                                                 ALU.mult, ALU.add)
                    if e == 0:
                        st(it)
                    else:
                        it.then_inc(emptied_v, 1)
                        ve.wait_ge(*ring.done(("y", t, e // 2)))
            def top_two(v):
                lo = v.unsqueeze(3).to_broadcast([TT, NT, 8, 8])
                hi = v.unsqueeze(2).to_broadcast([TT, NT, 8, 8])
                g_, e_ = (cmp[:, z, :, :].rearrange("p t (a b) -> p t a b", a=8) for z in range(2))
                st(ve.tensor_tensor(g_, hi, lo, ALU.is_gt))
                st(ve.tensor_tensor(e_, hi, lo, ALU.is_equal))
                own()
                st(ve.tensor_tensor(cmp[:, 1, :, :], cmp[:, 1, :, :], tri8[:, :].unsqueeze(1).to_broadcast([TT, NT, 64]), ALU.mult))
                own()
                st(ve.tensor_tensor(cmp[:, 0, :, :], cmp[:, 0, :, :], cmp[:, 1, :, :], ALU.add))
                own()
                st(ve.tensor_reduce(sel[:, :, :], g_, X, ALU.add))
                own()

            layernorm(3)
            ve.wait_ge(xn_ready, 2 * NT)
            st(ve.tensor_copy(cat[:, :, 0:D].bitcast(F32R), xn[:, :, :]))
            own()
            ve.tensor_tensor(cat[:, :, D:2 * D], xn[:, :, :], cat[:, :, 0:D], ALU.subtract).then_inc(cat_r, 1)
            st(ve.memset(pv[:, :, 7:8], -1.0))
            st(ve.memset(cw[:, :, 7:8], 1.0))
            ve.wait_ge(*loaded("route"))
            ps = full("rt")
            ve.tensor_tensor(pv[:, :, 0:7], ps[0:TT, 0:42].rearrange("p (t n) -> p t n", t=NT),
                             rbias[:, :].unsqueeze(1).to_broadcast([TT, NT, 7]), ALU.mult).then_inc(emptied_v, 1)
            ve.wait_ge(*ring.done("rt"))
            ve.memset(red[:, :], 0.0).then_inc(rsig_in, 1)
            ve.wait_ge(rsig, 1)
            own()
            top_two(pv[:, :, :])
            st(ve.tensor_scalar(sel[:, :, :], sel[:, :, :], 1.5, None, ALU.is_lt))
            own()
            st(ve.tensor_tensor(sel[:, :, 0:7], sel[:, :, 0:7], pv[:, :, 0:7], ALU.mult))
            own()
            st(ve.tensor_reduce(gsum[:, :], sel[:, :, 0:7], X, ALU.add))
            own()
            st(ve.reciprocal(gsum[:, :], gsum[:, :]))
            own()
            st(ve.tensor_tensor(cw[:, :, 0:7], sel[:, :, 0:7], bc(gsum[:, :], [TT, NT, 7]), ALU.mult))
            own()
            with ve.Fori(0, FE // 2) as i:
                for s in range(2):
                    for u in range(2):
                        for m in range(3):
                            ps = full(("u", s, u, m), i)
                            ve.wait_ge(*ring.done(("g", s, u, m), i))
                            ve.tensor_tensor(aT[s][:, m, u * HALF:(u + 1) * HALF], ps[:, 0:HALF], sg[:, 3 * u + m, :],
                                             ALU.mult).then_inc(emptied_v, 1)
                    ve.wait_ge(*ring.done(("dn", 1 - s, 3), i, back=1 - s))
                    for z, tiles in enumerate(DN):
                        ps = full(("dn", s, z), i)
                        for q, t in enumerate(tiles):
                            it = ve.scalar_tensor_tensor(h[:, t, :], ps[0:TT, q * D:(q + 1) * D], cw[:, t, bass.ds(2 * i + s, 1)],
                                                         h[:, t, :], ALU.mult, ALU.add)
                        it.then_inc(emptied_v, 1)
            ve.wait_ge(*ring.done(("dn", 1, 3), FE // 2 - 1))
            layernorm(4)
            ve.wait_ge(*loaded("l1"))
            ve.tensor_scalar(lsc[:, :], lsc[:, :], 4.605170185988092, None, ALU.min).then_inc(lsexp_in, 1)
            for j in range(2):
                ve.wait_ge(*ring.done(("vv", j, 3)))
                if j == 0:
                    ve.tensor_reduce(ssum2[:, 0, :, :], sqk0.rearrange("p l (a d) -> p l a d", d=AD), X, ALU.add).then_inc(ssum_r, 1)
                    for l in range(4):
                        st(ve.tensor_tensor(prod[0][:, l * 768:(l + 1) * 768].rearrange("p (m n) -> p m n", m=4),
                                            qkv[0][:, l:l + 1, 0:D].to_broadcast([QT, 4, D]), qkv[0][:, :, D:2 * D], ALU.mult))
                else:
                    for l in range(4):
                        it = ve.tensor_reduce(ssum2[:, 1, l, :], sqk[1][l].rearrange("p (a d) -> p a d", d=AD), X, ALU.add)
                    it.then_inc(ssum_r, 1)
            for j in range(2):
                lg, ssum, lmx = lg2[:, j, :, :, :], ssum2[:, j, :, :], lmx2[:, j, :, :]
                if j == 1:
                    ve.wait_ge(pq, 1)
                own()
                st(ve.tensor_reduce(lg.rearrange("p l m h -> p (l m h)"), prod[j].rearrange("p (a d) -> p a d", d=AD), X, ALU.add))
                ve.wait_ge(snorm, j + 1)
                st(ve.tensor_scalar(ssum, ssum, 1e-12, None, ALU.max))
                own()
                st(ve.reciprocal(ssum, ssum))
                own()
                ve.wait_ge(lsexp, 1)
                st(ve.tensor_tensor(ssum[:, :, 0:AH], ssum[:, :, 0:AH], lsc[:, :].unsqueeze(1).to_broadcast([QT, 4, AH]), ALU.mult))
                own()
                st(ve.tensor_tensor(lg, lg, ssum[:, :, 0:AH].unsqueeze(2).to_broadcast([QT, 4, 4, AH]), ALU.mult))
                own()
                st(ve.tensor_tensor(lg, lg, ssum[:, :, AH:24].unsqueeze(1).to_broadcast([QT, 4, 4, AH]), ALU.mult))
                own()
                st(ve.tensor_reduce(lmx, lg.rearrange("p l m h -> p l h m"), X, ALU.max))
                own()
                ve.tensor_tensor(lg, lg, lmx.unsqueeze(2).to_broadcast([QT, 4, 4, AH]), ALU.subtract).then_inc(lexp_in, 1)
            for j in (1, 0):
                lg, lmx = lg2[:, j, :, :, :], lmx2[:, j, :, :]
                ve.wait_ge(lexp, 2)
                st(ve.tensor_reduce(lmx, lg.rearrange("p l m h -> p l h m"), X, ALU.add))
                own()
                st(ve.reciprocal(lmx, lmx))
                own()
                st(ve.tensor_tensor(lmx, lmx, hsc[:, :].unsqueeze(1).to_broadcast([QT, 4, AH]), ALU.mult))
                own()
                it = ve.tensor_tensor(lg, lg, lmx.unsqueeze(2).to_broadcast([QT, 4, 4, AH]), ALU.mult)
                if j == 1:
                    it.then_inc(pv_in, 1)
                else:
                    st(it)
            own()
            for l in range(4):
                st(ve.tensor_tensor(prod[0][:, l * 768:(l + 1) * 768].rearrange("p (m h d) -> p m h d", m=4, h=AH),
                                    lg2[:, 0, l, :, :].unsqueeze(3).to_broadcast([QT, 4, AH, AD]),
                                    qkv[0][:, :, 2 * D:3 * D].rearrange("p m (h d) -> p m h d", h=AH), ALU.mult))
            own()
            for j in range(2):
                if j == 1:
                    ve.wait_ge(pv_out, 1)
                ve.tensor_reduce(o1[j], prod[j].rearrange("p (l m n) -> p l n m", l=4, m=4), X, ALU.add).then_inc(o_ready, 1)

            def residual(name, to):
                for t in range(NT):
                    ps = full((name, t))
                    ve.tensor_tensor(to[:, t, :], ps[0:TT, 0:D], to[:, t, :], ALU.add).then_inc(emptied_v, 1)
                ve.wait_ge(*ring.done((name, NT - 1)))
            residual("op", h)
            layernorm(5, h, h2)
            layernorm(6, h2, xn)
            for s in range(2):
                st(ve.memset(v32[s], 0.0))
            own()
            with ve.Fori(0, B // 2) as i:
                for s in range(2):
                    for j in range(2):
                        ps = full(("v2", s, j), i)
                        ve.tensor_copy(v32[s][:, j, :, 0:AD], ps[0:QT, 0:D].rearrange("p (h d) -> p h d", h=AH)).then_inc(emptied_v, 1)
                    ve.wait_ge(*ring.done(("v2", s, 1), i))
                    ve.memset(v32[s][0:1, 1, :, :], 0.0).then_inc(v2z, 1)

                def inverse(s, g):
                    ve.wait_ge(*ring.done(("SB", s, g), i))
                    ve.reciprocal(psums[:, s, g, :], psums[:, s, g, :]).then_inc(rsum, 1)
                for s in range(2):
                    for g in range(4):
                        ps = full(("SA", s, g), i)
                        ve.tensor_reduce(mx[:, s, g, 0:3], ps[0:QT, 0:285].rearrange("p (m n) -> p m n", m=3), X, ALU.max)
                        ve.tensor_reduce(mx[:, s, g, 5:6], ps[0:QT, 285:474], X, ALU.max)
                        ps = full(("SB", s, g), i)
                        ve.tensor_reduce(mx[:, s, g, 3:5], ps[0:QT, 0:378].rearrange("p (m n) -> p m n", m=2), X, ALU.max).then_inc(mx_r, 1)
                        ve.wait_ge(mx_r, 8 * i + 4 * s + g + 1)
                        ve.tensor_scalar(mx[:, s, g, :], mx[:, s, g, :], -float(AD) ** -0.5, None, ALU.mult).then_inc(v_set, 1)
                        if s == 1:
                            inverse(0, g)
                for g in range(4):
                    inverse(1, g)
                for s in range(2):
                    for z in range(0, 8, 2):
                        ps = full(("PT", s, z), i)
                        ve.tensor_copy(PT[s][:, 5 * z:5 * z + 5, :], ps[0:QT, 0:5 * QT].rearrange("p (z n) -> p z n", z=5)).then_inc(emptied_v, 1)
                for s in range(2):
                    for m in range(3):
                        ps = full(("yu", s, m), i)
                        for j in range(2):
                            it = ve.tensor_copy(yT[m][:, bass.ds((2 * i + s) * N + j * QT, QT - j)], ps[0:112, j * QT + j:2 * QT if j else QT])
                        it.then_inc(emptied_v, 1)
            residual("cp", h2)
            layernorm(7, h2, xn)
            ve.wait_ge(xn_ready, 5 * NT)
            st(ve.tensor_copy(xs[:, 0, :, :], xn[:, :, :]))
            own()
            st(ve.tensor_tensor(h1[:, :, :], xn[:, :, :], xs[:, 0, :, :], ALU.subtract))
            own()
            st(ve.tensor_copy(xs[:, 1, :, :], h1[:, :, :]))
            own()
            st(ve.tensor_tensor(h1[:, :, :], h1[:, :, :], xs[:, 1, :, :], ALU.subtract))
            own()
            ve.tensor_copy(xs[:, 2, :, :], h1[:, :, :]).then_inc(xs_r, 1)
            ps = full("mr")
            ve.tensor_copy(pv[:, :, :], ps[0:TT, 0:48].rearrange("p (t n) -> p t n", t=NT)).then_inc(emptied_v, 1)
            ve.wait_ge(*ring.done("mr"))
            top_two(pv[:, :, :])
            ve.tensor_scalar(selb[:, :, :], sel[:, :, :], 1.5, None, ALU.is_lt).then_inc(sel_r, 1)
            st(ve.tensor_scalar(sel[:, :, :], sel[:, :, :], 1.5, None, ALU.is_lt))
            st(ve.tensor_reduce(red[:, :], pv[:, :, :], X, ALU.max))
            own()
            ve.tensor_tensor(pv[:, :, :], pv[:, :, :], bc(red[:, :], [TT, NT, 8]), ALU.subtract).then_inc(mlg, 1)
            ve.wait_ge(mexp, 1)
            st(ve.tensor_tensor(pv[:, :, :], pv[:, :, :], sel[:, :, :], ALU.mult))
            own()
            st(ve.tensor_reduce(gsum[:, :], pv[:, :, :], X, ALU.add))
            own()
            st(ve.reciprocal(gsum[:, :], gsum[:, :]))
            own()
            st(ve.tensor_tensor(cw[:, :, 0:8], pv[:, :, :], bc(gsum[:, :], [TT, NT, 8]), ALU.mult))
            st(ve.memset(key[:, :, 8:10], 1000.0))
            ps = full("cs")
            ve.scalar_tensor_tensor(key[:, :, 0:8], sel[:, :, :], -1000.0, ps[0:TT, 0:48].rearrange("p (t n) -> p t n", t=NT),
                                    ALU.mult, ALU.add).then_inc(emptied_v, 1)
            ve.wait_ge(*ring.done("cs"))
            st(ve.tensor_scalar(key[:, :, 0:8], key[:, :, 0:8], 1000.0, None, ALU.add))
            own()

            def one_hot(s, e):
                for t in range(NT):
                    it = ve.tensor_scalar(oh[:, s, t, :], iota[:, :], key[:, t, bass.ds(e, 1)], None, ALU.is_equal)
                it.then_inc(oh_r, 1)
            for s in range(2):
                one_hot(s, s)
            ve.wait_ge(hb, 2 * NT)
            with ve.Fori(0, ME // 2) as i:
                for s in range(2):
                    ps = full(("d", s), i)
                    for k in range(2):
                        it = ve.tensor_scalar(xe[:, s, k, :], ps[0:DH, k * CAP:(k + 1) * CAP], flnw[:, 1, k:k + 1], None, ALU.mult)
                    it.then_inc(emptied_v, 1)
                for s in range(2):
                    ve.wait_ge(*ring.full(("T", s, 1), i))
                    one_hot(s, 2 * i + 2 + s)
                for s in range(2):
                    ps = full(("pj", s), i)
                    ve.tensor_copy(eo[:, s, :, :], ps[0:CT, 0:2 * D].rearrange("p (c d) -> p c d", c=2)).then_inc(emptied_v, 1)
                for s in range(2):
                    ve.wait_ge(*ring.done(("cb", 1 - s, 4), i, back=1 - s))
                    for z, tiles in enumerate(CB):
                        ps = full(("cb", s, z), i)
                        for q, t in enumerate(tiles):
                            it = ve.scalar_tensor_tensor(h[:, t, :], ps[0:TT, q * D:(q + 1) * D], cw[:, t, bass.ds(2 * i + s, 1)],
                                                         h[:, t, :], ALU.mult, ALU.add)
                        it.then_inc(emptied_v, 1)
            ve.wait_ge(*ring.done(("cb", 1, 4), ME // 2 - 1))
            ve.memset(red[:, :], 0.0).then_inc(hh, 2)

        @block.gpsimd
        def _(po):
            po.wait_ge(*loaded("b0"))
            po.wait_ge(*ring.full(("ln0", 2)))
            for t in range(NT):
                po.tensor_tensor(xn[:, t, :], xn[:, t, :], outb[:, :], ALU.add).then_inc(xob, 1)
            for t in range(NT):
                po.wait_ge(*ring.done(("rs", t)))
                po.tensor_tensor(h[:, t, :], h[:, t, :], h2[:, t, :], ALU.add).then_inc(hb, 1)
            with po.Fori(0, FE // 2) as i:
                for s in range(2):
                    for c in range(2):
                        po.wait_ge(f_wh, 6 * i + 3 * s + (1, 3)[c])
                        it = po.tensor_tensor(wB[:, c, :], rawf[:, c, :], wA[:, c, :].bitcast(F32), ALU.subtract)
                    it.then_inc(f_split, 1)
            po.wait_ge(*ring.done(("vv", 1, 3)))
            for l in range(4):
                it = po.tensor_tensor(prod[1][:, l * 768:(l + 1) * 768].rearrange("p (m n) -> p m n", m=4),
                                      qkv[1][:, l:l + 1, 0:D].to_broadcast([QT, 4, D]), qkv[1][:, :, D:2 * D], ALU.mult)
            it.then_inc(pq, 1)
            po.wait_ge(pv_in, 1)
            for l in range(4):
                it = po.tensor_tensor(prod[1][:, l * 768:(l + 1) * 768].rearrange("p (m h d) -> p m h d", m=4, h=AH),
                                      lg2[:, 1, l, :, :].unsqueeze(3).to_broadcast([QT, 4, AH, AD]),
                                      qkv[1][:, :, 2 * D:3 * D].rearrange("p m (h d) -> p m h d", h=AH), ALU.mult)
            it.then_inc(pv_out, 1)
            with po.Fori(0, B // 2) as i:
                for s in range(2):
                    for g in range(4):
                        po.wait_ge(rsum, 8 * i + 4 * s + g + 1)
                        po.tensor_tensor(P0[s][:, g, :, :], P0[s][:, g, :, :], psums[:, s, g, 0:3].unsqueeze(2).to_broadcast([QT, 3, QT]), ALU.mult)
                        po.tensor_tensor(P1[s][:, g, :, :], P1[s][:, g, :, :], psums[:, s, g, 3:6].unsqueeze(2).to_broadcast([QT, 3, N]),
                                         ALU.mult).then_inc(exp_r, 1)
            for t in range(NT):
                po.wait_ge(*ring.done(("cp", t)))
                po.tensor_tensor(h[:, t, :], h[:, t, :], h2[:, t, :], ALU.add).then_inc(hb, 1)


def lay_out(x, n):
    import numpy as np
    a = {}

    def put(name, v):
        v = np.ascontiguousarray(v)
        a[name] = v.astype(np.float32) if v.dtype == np.float64 else v

    def rows(w, p):
        return w.reshape(w.shape[0] // p, p, *w.shape[1:]).swapaxes(0, 1)

    for s, key, w, p in ((8, "8", "W0", DH), (16, "16", "W1", 128), (32, "32", "W2", 128)):
        g = IMG // s
        v = x.reshape(B, g, s, g, s, C).transpose(2, 4, 5, 0, 1, 3).reshape(s * s * C, B * g * g)
        put("p" + key, rows(v, p))
        put("w" + key, rows(n["L0_tok_" + w], p))
    put("tokb", np.stack([n[f"L0_tok_b{i}"].reshape(2, DH) for i in range(3)], -1).transpose(1, 0, 2))
    put("ident", np.eye(128, dtype=np.float32))
    put("identb", np.eye(128, dtype=np.float32).astype(mybir.dt.np(BF16)))
    put("bones", np.kron(np.eye(2), np.ones((64, 64))).astype(np.float32))
    put("hones", np.kron(np.eye(2), np.ones((64, 1))).astype(np.float32))
    put("ones", np.ones((128, 1), np.float32))
    put("sgn", np.tile(np.repeat([1.0, -1.0], 32), 2)[:, None].astype(np.float32))
    put("sg4", np.repeat([1.0, 1.0, 1.0, -1.0], 32)[:, None].astype(np.float32))
    l0 = lambda k: n["L0_attn_" + k]
    mr, mi = (l0(k).reshape(4, 2, 64, 32).transpose(1, 3, 0, 2) for k in ("m_real", "m_imag"))
    put("m_re", np.stack([mr, mi], 1).reshape(128, 4, 64))
    put("m_im", np.stack([mi, mr], 1).reshape(128, 4, 64))
    pr, pi, cr, ci = (l0(k).T for k in ("P_real", "P_imag", "C_real", "C_imag"))
    put("pc", np.stack([np.stack([np.concatenate([pr, pi]), np.concatenate([cr, ci])], 1),
                        np.stack([np.concatenate([pi, pr]), np.concatenate([ci, cr])], 1)], 1))
    w = np.stack([l0("W_real"), l0("W_imag")], 1)
    put("wp", rows(w.transpose(2, 0, 1, 3).reshape(D, 512), DH))
    put("pw1", rows(l0("pw1").transpose(2, 0, 1).reshape(D, 128), DH))
    put("pb1", l0("pb1").reshape(128, 1))
    pw2 = np.zeros((8, 16, 8), np.float32)
    for j in range(8):
        pw2[j, :, j] = l0("pw2")[j]
    put("pw2", pw2.reshape(128, 8))
    put("valT", rows(l0("values").transpose(2, 0, 1).reshape(D, 512), DH))
    put("owT", rows(l0("out_w").T, DH))
    put("gwT", rows(l0("gate_w").reshape(8, 8, D).transpose(2, 1, 0).reshape(D, 64), DH).reshape(DH, 2, 4, 16))
    put("pb2", l0("pb2")); put("gateb", l0("gate_b")); put("outb", l0("out_b")); put("beta", l0("beta").reshape(1))
    put("rob", l0("r_out_b")); put("rb2", l0("rb2"))
    put("encT", rows(np.concatenate([l0("enc_r_w"), l0("enc_i_w")]).T, DH))
    wr, wi = l0("r_out_w").T[:32], l0("r_out_w").T[32:]
    put("roW", np.concatenate([wr, wr, wi, wi]))
    il = np.zeros((2, TT), np.float32); il[0, :N - TT] = 1; il[1, N - TT:] = 1
    ir = np.zeros((2, HALF), np.float32); ir[0, N:] = NEG; ir[1, :N] = NEG
    put("imgL", il); put("imgR", ir)
    put("rw1", rows(l0("rw1").T, DH)); put("rb1", l0("rb1").reshape(1, 16)); put("rw2", l0("rw2").T)
    put("ew1", rows(l0("ew1").transpose(2, 0, 1).reshape(D, 576), DH)); put("eb1", l0("eb1").reshape(1, 576))
    put("egb", np.stack([l0("eg").reshape(6, DH), l0("ebt").reshape(6, DH)], -1).transpose(1, 0, 2))
    put("ew2", rows(l0("ew2").transpose(0, 2, 1).reshape(576, D), DH)); put("eb2", l0("eb2").reshape(1, 3, D))
    f = lambda k: n["L0_ffn_" + k]
    put("rwt", rows(f("router_w"), DH)); put("rbias", f("routing_bias"))
    put("tri8", (np.arange(8)[None, :] < np.arange(8)[:, None]).astype(np.float32).reshape(64))
    gu = np.stack([np.concatenate([f("rw_" + k), f("sw_" + k)[None]]) for k in ("gate", "up")], 2)
    gu = gu.reshape(FE, D, 2 * FI)
    put("fgu", np.concatenate([gu, gu], 1).reshape(FE, 3, 128, 2 * FI).swapaxes(1, 2).reshape(FE, 128, 6 * FI))
    dn = np.concatenate([f("rw_down"), f("sw_down")[None]])
    put("fdn", dn.reshape(FE, 3, 128, D).swapaxes(1, 2).reshape(FE, 128, 3 * D))
    l1 = lambda k: n["L1_attn_" + k]
    put("wqkv", rows(l1("in_proj_weight").T, DH)); put("bqkv", l1("in_proj_bias").reshape(1, 3 * D))
    put("ow1", rows(l1("out_w").T, DH)); put("ob1", l1("out_b").reshape(1, D))
    put("lsc", l1("logit_scale").reshape(AH)); put("hsc", l1("head_scale").reshape(AH))
    c = lambda k: n["L1_ffn_" + k]
    put("flnw", np.stack([c("ln1_w").reshape(2, DH), c("ln2_w").reshape(2, DH)], 1).transpose(2, 1, 0))
    w = c("c_attn_w").T
    pad = np.zeros((D, 2, 3, 4, 32), np.float32)
    pad[..., :AD] = w[:, :2 * D].reshape(D, 2, 3, 4, AD)
    put("wq2", rows(pad.reshape(D, 768), DH)); put("wv2", rows(w[:, 2 * D:], DH)); cp = np.zeros((3, 4, 32, D), np.float32)
    cp[:, :, :AD] = c("c_proj_w").T.reshape(3, 4, AD, D)
    put("cpw", cp.reshape(3, 128, D)[:, :112].swapaxes(0, 1))
    q0, q1 = np.arange(QT)[:, None], np.arange(N - QT, N)[:, None]
    m0 = np.where(np.arange(QT)[None] <= q0, 0.0, NEG)
    m1 = np.where(np.arange(N)[None] <= q1, 0.0, NEG)
    put("maskA", np.concatenate([m0, m0, m0, m1], 1).astype(mybir.dt.np(BF16)))
    put("maskB", np.concatenate([m1, m1], 1).astype(mybir.dt.np(BF16)))
    put("wg", rows(c("w_g").T, DH))
    put("tri", (np.arange(TT)[:, None] < np.arange(TT)[None]).astype(mybir.dt.np(BF16)))
    put("tones", np.ones((TT, TT)).astype(mybir.dt.np(BF16)))
    put("iota", np.arange(CAP, dtype=np.float32))
    put("mfc", c("c_fc").reshape(ME, 2, DH, MI).swapaxes(1, 2).reshape(ME, DH, 2 * MI))
    put("mpj", c("c_proj_e").reshape(ME, 6, 128, D).swapaxes(1, 2).reshape(ME, 128, 6 * D))
    return a


def kernel(**inputs):
    import numpy as np
    import concourse.bacc as bacc
    from concourse.bass_utils import run_bass_kernel_spmd as run

    n = {k: np.asarray(v) for k, v in inputs.items()}
    arrays = lay_out(n.pop("x"), n)
    nc = bacc.Bacc("TRN2", target_bir_lowering=False, num_devices=1)
    aps = {k: nc.dram_tensor("in_" + k, v.shape, mybir.dt.from_np(v.dtype), kind="ExternalInput").ap() for k, v in arrays.items()}
    out = nc.dram_tensor("out", (B, N, D), F32, kind="ExternalOutput").ap()
    vit_tower(nc, aps, out)
    r = run(nc, [{"in_" + k: v for k, v in arrays.items()}], core_ids=[0])
    return r.results[0]["out"]
```
